# Optimizing a Trainium2 kernel written in Bass

```python
import numpy as np
import jax
import jax.numpy as jnp

def _softmax(x, axis=-1):
    return jax.nn.softmax(x, axis=axis)

def _gelu(x):
    return jax.nn.gelu(x, approximate=True)

def _silu(x):
    return jax.nn.silu(x)

def _sigmoid(x):
    return jax.nn.sigmoid(x)

def _layernorm(x, axis=-1, eps=1e-05):
    m = jnp.mean(x, axis=axis, keepdims=True)
    v = jnp.var(x, axis=axis, keepdims=True)
    return (x - m) / jnp.sqrt(v + eps)

def _scatter_add(tgt, idx, src, axis=0):
    return tgt.at[idx].add(src)

def _segment_sum(src, seg, n):
    return jax.ops.segment_sum(src, seg, n)
kernel_name = 'mk_gnn_resnorm_d4_gnn_r32_d0252f'

def setup_inputs(seed: int=0):
    np.random.seed(seed)
    _w = jnp.asarray

    def _rec_inputs():
        import jax
        import jax.numpy as jnp
        _gk = jax.random.key(seed)
        x = -0.0005121 + 1.001 * jax.random.normal(jax.random.fold_in(_gk, 1), (3125, 64), jnp.float32)
        src = jax.random.randint(jax.random.fold_in(_gk, 2), (100000,), 0, 3125, jnp.int32)
        dst = jnp.minimum((3125 * jax.random.uniform(jax.random.fold_in(_gk, 3), (100000,)) ** 2.0).astype(jnp.int32), 99999)
        _o = jnp.argsort(dst, stable=True)
        src = src[_o]
        dst = dst[_o]
        edge_type_100 = jax.random.randint(jax.random.fold_in(_gk, 13), (100000,), 0, 100, jnp.int32)
        return (x, src, dst, edge_type_100)
    x, src, dst, edge_type_100 = _rec_inputs()

    def _L0_gnn_setup():
        import jax, jax.numpy as jnp
        import numpy as np
        BN_EPS = 1e-05

        def _gcn_conv(x, W, b, src, dst, norm, n):
            h = x @ W
            msg = h[src] * norm[:, None]
            out = jax.ops.segment_sum(msg, dst, num_segments=n)
            return out + b

        def _bn_eval(y, g, be, rm, rv):
            return (y - rm) * jax.lax.rsqrt(rv + BN_EPS) * g + be
        key = jax.random.key(seed)
        ks = jax.random.split(key, 4)
        N, E, Fin, Dh, Fout = (50000, 25000, 64, 64, 64)
        x = jax.random.normal(ks[0], (N, Fin), dtype=jnp.float32)
        W1 = jax.random.normal(ks[1], (Fin, Dh), dtype=jnp.float32) / np.sqrt(Fin)
        W2 = jax.random.normal(ks[2], (Dh, Fout), dtype=jnp.float32) / np.sqrt(Dh)
        edge_index = jax.random.randint(ks[3], (2, E), 0, N, dtype=jnp.int64)
        return {'x': x, 'W1': W1, 'b1': jnp.zeros((Dh,), jnp.float32), 'g1': jnp.ones((Dh,), jnp.float32), 'be1': jnp.zeros((Dh,), jnp.float32), 'rm1': jnp.zeros((Dh,), jnp.float32), 'rv1': jnp.ones((Dh,), jnp.float32), 'W2': W2, 'b2': jnp.zeros((Fout,), jnp.float32), 'g2': jnp.ones((Fout,), jnp.float32), 'be2': jnp.zeros((Fout,), jnp.float32), 'rm2': jnp.zeros((Fout,), jnp.float32), 'rv2': jnp.ones((Fout,), jnp.float32), 'edge_index': edge_index}
    _L0_gnn_all = _L0_gnn_setup()
    _L0_gnn_in = {k: v for k, v in _L0_gnn_all.items() if k in ('W1', 'b1', 'g1', 'be1', 'rm1', 'rv1', 'W2', 'b2', 'g2', 'be2', 'rm2', 'rv2')}
    del _L0_gnn_all

    def _L1_gnn_setup():
        import jax, jax.numpy as jnp
        import numpy as np
        N_NODES = 3125
        N_EDGES = 50000
        D = 64
        H = 128
        key = jax.random.key(seed)
        k1, k2, k3, k4 = jax.random.split(key, 4)
        node_attr = jax.random.normal(k1, (N_NODES, D), dtype=jnp.float32)
        edge_index = jax.random.randint(k2, (2, N_EDGES), 0, N_NODES, dtype=jnp.int64)
        W1 = jax.random.normal(k3, (2 * D, H), dtype=jnp.float32) / np.sqrt(2 * D)
        b1 = jnp.zeros((H,), dtype=jnp.float32)
        W2 = jax.random.normal(k4, (H, D), dtype=jnp.float32) / np.sqrt(H)
        b2 = jnp.zeros((D,), dtype=jnp.float32)
        return {'node_attr': node_attr, 'edge_index': edge_index, 'W1': W1, 'b1': b1, 'W2': W2, 'b2': b2}
    _L1_gnn_all = _L1_gnn_setup()
    _L1_gnn_in = {k: v for k, v in _L1_gnn_all.items() if k in ('W1', 'b1', 'W2', 'b2')}
    del _L1_gnn_all

    def _L2_gnn_setup():
        import jax, jax.numpy as jnp
        import numpy as np
        NUM_ENT = 3125
        NUM_REL = 50
        INIT_DIM = 64
        GCN_DIM = 128
        EMBED_DIM = 64
        E_TOTAL = 100000
        BN_EPS = 1e-05

        def ccorr(a, b):
            d = a.shape[-1]
            fa = jnp.fft.rfft(a, axis=-1)
            fb = jnp.fft.rfft(b, axis=-1)
            return jnp.fft.irfft(jnp.conj(fa) * fb, n=d, axis=-1)

        def compute_norm(row, col, n):
            deg = jax.ops.segment_sum(jnp.ones_like(row, dtype=jnp.float32), row, num_segments=n)
            dinv = jnp.where(deg > 0, deg ** (-0.5), 0.0)
            return dinv[row] * dinv[col]

        def comp_layer(x, edge_index, edge_type, rel, w_in, w_out, w_loop, w_rel, loop_rel, bias, gamma, beta):
            n = x.shape[0]
            ne = edge_index.shape[1] // 2
            rel_full = jnp.concatenate([rel, loop_rel], axis=0)

            def direction(idx, etype, W):
                row, col = (idx[0], idx[1])
                norm = compute_norm(row, col, n)
                m = ccorr(x[col], rel_full[etype]) @ W
                m = m * norm[:, None]
                return jax.ops.segment_sum(m, row, num_segments=n)
            in_res = direction(edge_index[:, :ne], edge_type[:ne], w_in)
            out_res = direction(edge_index[:, ne:], edge_type[ne:], w_out)
            loop_res = ccorr(x, loop_rel) @ w_loop
            out = (in_res + out_res + loop_res) * (1.0 / 3.0) + bias
            mu = out.mean(axis=0)
            var = out.var(axis=0)
            out = (out - mu) / jnp.sqrt(var + BN_EPS) * gamma + beta
            return (jnp.tanh(out), (rel_full @ w_rel)[:-1])
        key = jax.random.key(seed)
        ks = jax.random.split(key, 20)
        f32 = jnp.float32

        def w(k, shape, scale=0.1):
            return jax.random.normal(k, shape, dtype=f32) * scale
        edge_index = jax.random.randint(ks[0], (2, E_TOTAL), 0, NUM_ENT, dtype=jnp.int64 if jax.config.jax_enable_x64 else jnp.int32)
        edge_type = jax.random.randint(ks[1], (E_TOTAL,), 0, 2 * NUM_REL, dtype=edge_index.dtype)
        return {'edge_index': edge_index, 'edge_type': edge_type, 'init_emb': w(ks[2], (NUM_ENT, INIT_DIM), 1.0), 'init_rel': w(ks[3], (2 * NUM_REL, INIT_DIM), 1.0), 'c1_w_in': w(ks[4], (INIT_DIM, GCN_DIM)), 'c1_w_out': w(ks[5], (INIT_DIM, GCN_DIM)), 'c1_w_loop': w(ks[6], (INIT_DIM, GCN_DIM)), 'c1_w_rel': w(ks[7], (INIT_DIM, GCN_DIM)), 'c1_loop_rel': w(ks[8], (1, INIT_DIM)), 'c1_bias': jnp.zeros((GCN_DIM,), f32), 'c1_gamma': jnp.ones((GCN_DIM,), f32), 'c1_beta': jnp.zeros((GCN_DIM,), f32), 'c2_w_in': w(ks[9], (GCN_DIM, EMBED_DIM)), 'c2_w_out': w(ks[10], (GCN_DIM, EMBED_DIM)), 'c2_w_loop': w(ks[11], (GCN_DIM, EMBED_DIM)), 'c2_w_rel': w(ks[12], (GCN_DIM, EMBED_DIM)), 'c2_loop_rel': w(ks[13], (1, GCN_DIM)), 'c2_bias': jnp.zeros((EMBED_DIM,), f32), 'c2_gamma': jnp.ones((EMBED_DIM,), f32), 'c2_beta': jnp.zeros((EMBED_DIM,), f32)}
    _L2_gnn_all = _L2_gnn_setup()
    _L2_gnn_in = {k: v for k, v in _L2_gnn_all.items() if k in ('init_rel', 'c1_w_in', 'c1_w_out', 'c1_w_loop', 'c1_w_rel', 'c1_loop_rel', 'c1_bias', 'c1_gamma', 'c1_beta', 'c2_w_in', 'c2_w_out', 'c2_w_loop', 'c2_w_rel', 'c2_loop_rel', 'c2_bias', 'c2_gamma', 'c2_beta')}
    del _L2_gnn_all

    def _L3_gnn_setup():
        import jax, jax.numpy as jnp
        import numpy as np
        N_NODES = 3125
        N_EDGES = 50000
        D = 64
        BN_EPS = 1e-05
        key = jax.random.key(seed)
        ks = jax.random.split(key, 6)
        feature = jax.random.normal(ks[0], (N_NODES, D), dtype=jnp.float32)
        src = jax.random.randint(ks[1], (N_EDGES,), 0, N_NODES, dtype=jnp.int32)
        dst = jax.random.randint(ks[2], (N_EDGES,), 0, N_NODES, dtype=jnp.int32)
        W = jax.random.normal(ks[3], (D, D), dtype=jnp.float32) / np.sqrt(D)
        b = jax.random.normal(ks[4], (D,), dtype=jnp.float32) * 0.01
        gamma = jnp.ones((D,), dtype=jnp.float32)
        beta = jnp.zeros((D,), dtype=jnp.float32)
        return {'feature': feature, 'W': W, 'b': b, 'gamma': gamma, 'beta': beta, 'src': src, 'dst': dst}
    _L3_gnn_all = _L3_gnn_setup()
    _L3_gnn_in = {k: v for k, v in _L3_gnn_all.items() if k in ('W', 'b', 'gamma', 'beta')}
    del _L3_gnn_all
    return {'x': x, 'src': src, 'dst': dst, 'edge_type_100': edge_type_100, 'L0_gnn_W1': _L0_gnn_in['W1'], 'L0_gnn_b1': _L0_gnn_in['b1'], 'L0_gnn_g1': _L0_gnn_in['g1'], 'L0_gnn_be1': _L0_gnn_in['be1'], 'L0_gnn_rm1': _L0_gnn_in['rm1'], 'L0_gnn_rv1': _L0_gnn_in['rv1'], 'L0_gnn_W2': _L0_gnn_in['W2'], 'L0_gnn_b2': _L0_gnn_in['b2'], 'L0_gnn_g2': _L0_gnn_in['g2'], 'L0_gnn_be2': _L0_gnn_in['be2'], 'L0_gnn_rm2': _L0_gnn_in['rm2'], 'L0_gnn_rv2': _L0_gnn_in['rv2'], 'L1_gnn_W1': _L1_gnn_in['W1'], 'L1_gnn_b1': _L1_gnn_in['b1'], 'L1_gnn_W2': _L1_gnn_in['W2'], 'L1_gnn_b2': _L1_gnn_in['b2'], 'L2_gnn_init_rel': _L2_gnn_in['init_rel'], 'L2_gnn_c1_w_in': _L2_gnn_in['c1_w_in'], 'L2_gnn_c1_w_out': _L2_gnn_in['c1_w_out'], 'L2_gnn_c1_w_loop': _L2_gnn_in['c1_w_loop'], 'L2_gnn_c1_w_rel': _L2_gnn_in['c1_w_rel'], 'L2_gnn_c1_loop_rel': _L2_gnn_in['c1_loop_rel'], 'L2_gnn_c1_bias': _L2_gnn_in['c1_bias'], 'L2_gnn_c1_gamma': _L2_gnn_in['c1_gamma'], 'L2_gnn_c1_beta': _L2_gnn_in['c1_beta'], 'L2_gnn_c2_w_in': _L2_gnn_in['c2_w_in'], 'L2_gnn_c2_w_out': _L2_gnn_in['c2_w_out'], 'L2_gnn_c2_w_loop': _L2_gnn_in['c2_w_loop'], 'L2_gnn_c2_w_rel': _L2_gnn_in['c2_w_rel'], 'L2_gnn_c2_loop_rel': _L2_gnn_in['c2_loop_rel'], 'L2_gnn_c2_bias': _L2_gnn_in['c2_bias'], 'L2_gnn_c2_gamma': _L2_gnn_in['c2_gamma'], 'L2_gnn_c2_beta': _L2_gnn_in['c2_beta'], 'L3_gnn_W': _L3_gnn_in['W'], 'L3_gnn_b': _L3_gnn_in['b'], 'L3_gnn_gamma': _L3_gnn_in['gamma'], 'L3_gnn_beta': _L3_gnn_in['beta']}

def reference(x, src, dst, edge_type_100, L0_gnn_W1, L0_gnn_b1, L0_gnn_g1, L0_gnn_be1, L0_gnn_rm1, L0_gnn_rv1, L0_gnn_W2, L0_gnn_b2, L0_gnn_g2, L0_gnn_be2, L0_gnn_rm2, L0_gnn_rv2, L1_gnn_W1, L1_gnn_b1, L1_gnn_W2, L1_gnn_b2, L2_gnn_init_rel, L2_gnn_c1_w_in, L2_gnn_c1_w_out, L2_gnn_c1_w_loop, L2_gnn_c1_w_rel, L2_gnn_c1_loop_rel, L2_gnn_c1_bias, L2_gnn_c1_gamma, L2_gnn_c1_beta, L2_gnn_c2_w_in, L2_gnn_c2_w_out, L2_gnn_c2_w_loop, L2_gnn_c2_w_rel, L2_gnn_c2_loop_rel, L2_gnn_c2_bias, L2_gnn_c2_gamma, L2_gnn_c2_beta, L3_gnn_W, L3_gnn_b, L3_gnn_gamma, L3_gnn_beta):
    import jax
    import jax.numpy as jnp

    def _L0_gnn_ref(x, W1, b1, g1, be1, rm1, rv1, W2, b2, g2, be2, rm2, rv2, edge_index):
        import jax, jax.numpy as jnp
        import numpy as np
        BN_EPS = 1e-05

        def _gcn_conv(x, W, b, src, dst, norm, n):
            h = x @ W
            msg = h[src] * norm[:, None]
            out = jax.ops.segment_sum(msg, dst, num_segments=n)
            return out + b

        def _bn_eval(y, g, be, rm, rv):
            return (y - rm) * jax.lax.rsqrt(rv + BN_EPS) * g + be
        n = x.shape[0]
        loop = jnp.arange(n, dtype=edge_index.dtype)
        src = jnp.concatenate([edge_index[0], loop])
        dst = jnp.concatenate([edge_index[1], loop])
        deg = jax.ops.segment_sum(jnp.ones_like(dst, dtype=x.dtype), dst, num_segments=n)
        dinv = jnp.where(deg > 0, jax.lax.rsqrt(deg), 0.0)
        norm = dinv[src] * dinv[dst]
        y = _gcn_conv(x, W1, b1, src, dst, norm, n)
        y = jax.nn.relu(_bn_eval(y, g1, be1, rm1, rv1))
        y = _gcn_conv(y, W2, b2, src, dst, norm, n)
        y = _bn_eval(y, g2, be2, rm2, rv2)
        return jax.nn.log_softmax(y, axis=1)

    def _L1_gnn_ref(node_attr, edge_index, W1, b1, W2, b2):
        import jax, jax.numpy as jnp
        import numpy as np
        N_NODES = 3125
        N_EDGES = 50000
        D = 64
        H = 128
        senders, receivers = (edge_index[0], edge_index[1])
        msg = node_attr[senders]
        agg = jax.ops.segment_sum(msg, receivers, num_segments=node_attr.shape[0])
        collected = jnp.concatenate([node_attr, agg], axis=-1)
        h = jax.nn.relu(collected @ W1 + b1)
        out = h @ W2 + b2
        return out

    def _L2_gnn_ref(edge_index, edge_type, init_emb, init_rel, c1_w_in, c1_w_out, c1_w_loop, c1_w_rel, c1_loop_rel, c1_bias, c1_gamma, c1_beta, c2_w_in, c2_w_out, c2_w_loop, c2_w_rel, c2_loop_rel, c2_bias, c2_gamma, c2_beta):
        import jax, jax.numpy as jnp
        import numpy as np
        NUM_ENT = 3125
        NUM_REL = 50
        INIT_DIM = 64
        GCN_DIM = 128
        EMBED_DIM = 64
        E_TOTAL = 100000
        BN_EPS = 1e-05

        def ccorr(a, b):
            d = a.shape[-1]
            fa = jnp.fft.rfft(a, axis=-1)
            fb = jnp.fft.rfft(b, axis=-1)
            return jnp.fft.irfft(jnp.conj(fa) * fb, n=d, axis=-1)

        def compute_norm(row, col, n):
            deg = jax.ops.segment_sum(jnp.ones_like(row, dtype=jnp.float32), row, num_segments=n)
            dinv = jnp.where(deg > 0, deg ** (-0.5), 0.0)
            return dinv[row] * dinv[col]

        def comp_layer(x, edge_index, edge_type, rel, w_in, w_out, w_loop, w_rel, loop_rel, bias, gamma, beta):
            n = x.shape[0]
            ne = edge_index.shape[1] // 2
            rel_full = jnp.concatenate([rel, loop_rel], axis=0)

            def direction(idx, etype, W):
                row, col = (idx[0], idx[1])
                norm = compute_norm(row, col, n)
                m = ccorr(x[col], rel_full[etype]) @ W
                m = m * norm[:, None]
                return jax.ops.segment_sum(m, row, num_segments=n)
            in_res = direction(edge_index[:, :ne], edge_type[:ne], w_in)
            out_res = direction(edge_index[:, ne:], edge_type[ne:], w_out)
            loop_res = ccorr(x, loop_rel) @ w_loop
            out = (in_res + out_res + loop_res) * (1.0 / 3.0) + bias
            mu = out.mean(axis=0)
            var = out.var(axis=0)
            out = (out - mu) / jnp.sqrt(var + BN_EPS) * gamma + beta
            return (jnp.tanh(out), (rel_full @ w_rel)[:-1])
        x, r = comp_layer(init_emb, edge_index, edge_type, init_rel, c1_w_in, c1_w_out, c1_w_loop, c1_w_rel, c1_loop_rel, c1_bias, c1_gamma, c1_beta)
        x, r = comp_layer(x, edge_index, edge_type, r, c2_w_in, c2_w_out, c2_w_loop, c2_w_rel, c2_loop_rel, c2_bias, c2_gamma, c2_beta)
        return x

    def _L3_gnn_ref(feature, W, b, gamma, beta, src, dst):
        import jax, jax.numpy as jnp
        import numpy as np
        N_NODES = 3125
        N_EDGES = 50000
        D = 64
        BN_EPS = 1e-05
        n = feature.shape[0]
        ones_e = jnp.ones(src.shape[0], dtype=feature.dtype)
        deg_out = jnp.maximum(jax.ops.segment_sum(ones_e, src, num_segments=n), 1.0)
        h = feature * (deg_out ** (-0.5))[:, None]
        agg = jax.ops.segment_sum(h[src], dst, num_segments=n)
        deg_in = jnp.maximum(jax.ops.segment_sum(ones_e, dst, num_segments=n), 1.0)
        agg = agg * (deg_in ** (-0.5))[:, None]
        h = agg @ W + b
        mean = jnp.mean(h, axis=0)
        var = jnp.var(h, axis=0)
        h = (h - mean) * jax.lax.rsqrt(var + BN_EPS) * gamma + beta
        h = jax.nn.elu(h)
        return feature + h
    edge_index = jnp.stack([src, dst])
    x = _layernorm(x + _L0_gnn_ref(x, L0_gnn_W1, L0_gnn_b1, L0_gnn_g1, L0_gnn_be1, L0_gnn_rm1, L0_gnn_rv1, L0_gnn_W2, L0_gnn_b2, L0_gnn_g2, L0_gnn_be2, L0_gnn_rm2, L0_gnn_rv2, edge_index), axis=-1)
    x = _layernorm(x + _L1_gnn_ref(x, edge_index, L1_gnn_W1, L1_gnn_b1, L1_gnn_W2, L1_gnn_b2), axis=-1)
    x = _layernorm(x + _L2_gnn_ref(edge_index, edge_type_100, x, L2_gnn_init_rel, L2_gnn_c1_w_in, L2_gnn_c1_w_out, L2_gnn_c1_w_loop, L2_gnn_c1_w_rel, L2_gnn_c1_loop_rel, L2_gnn_c1_bias, L2_gnn_c1_gamma, L2_gnn_c1_beta, L2_gnn_c2_w_in, L2_gnn_c2_w_out, L2_gnn_c2_w_loop, L2_gnn_c2_w_rel, L2_gnn_c2_loop_rel, L2_gnn_c2_bias, L2_gnn_c2_gamma, L2_gnn_c2_beta), axis=-1)
    x = _layernorm(x + _L3_gnn_ref(x, L3_gnn_W, L3_gnn_b, L3_gnn_gamma, L3_gnn_beta, src, dst), axis=-1)
    return x

_drawn_inputs = setup_inputs


def setup_inputs(seed=0):
    import zlib

    import numpy as np

    out = dict(_drawn_inputs(seed))
    spreads = {'L0_gnn_b1': (0.0, 0.1),
     'L0_gnn_g1': (1.0, 0.2),
     'L0_gnn_be1': (0.0, 0.1),
     'L0_gnn_rm1': (0.0, 0.1),
     'L0_gnn_rv1': (1.0, 0.2),
     'L0_gnn_b2': (0.0, 0.1),
     'L0_gnn_g2': (1.0, 0.2),
     'L0_gnn_be2': (0.0, 0.1),
     'L0_gnn_rm2': (0.0, 0.1),
     'L0_gnn_rv2': (1.0, 0.2),
     'L1_gnn_b1': (0.0, 0.358),
     'L1_gnn_b2': (0.0, 0.1),
     'L2_gnn_c1_bias': (0.0, 0.8),
     'L2_gnn_c1_gamma': (1.0, 0.2),
     'L2_gnn_c1_beta': (0.0, 0.1),
     'L2_gnn_c2_bias': (0.0, 0.8),
     'L2_gnn_c2_gamma': (1.0, 0.2),
     'L2_gnn_c2_beta': (0.0, 0.1),
     'L3_gnn_gamma': (1.0, 0.2),
     'L3_gnn_beta': (0.0, 0.279)}
    factors = {'L3_gnn_b': 8.0}
    for name, (base, spread) in spreads.items():
        noise = np.random.default_rng([zlib.crc32(name.encode()), seed]).standard_normal(out[name].shape)
        drawn = base * np.exp(spread * noise) if base else spread * noise
        out[name] = jnp.asarray(drawn.astype(out[name].dtype))
    for name, factor in factors.items():
        out[name] = (out[name] * factor).astype(out[name].dtype)
    return out
```

```python
from contextlib import ExitStack

import numpy as np

import concourse.bass as bass
from concourse import mybir

F32 = mybir.dt.float32
BF16 = mybir.dt.bfloat16
I32 = mybir.dt.int32
I16 = mybir.dt.int16
ALU = mybir.AluOpType
ACT = mybir.ActivationFunctionType
AX = mybir.AxisListType

P = 128
NODES = 3125
BLOCKS = 25
LO = NODES // BLOCKS
D = 64
EDGES = 100000
HALF = EDGES // 2
HP = P // 2
COLS = -(-HALF // HP)
LAST = HALF - (HP - 1) * COLS
BUCKETS = 2 * BLOCKS
TILES = HALF // P + HALF // P + BUCKETS + 2
GROUP = 4
GROUPS = TILES // GROUP
SLOTS = TILES * P
BANK = 512
BANKS = -(-NODES // BANK)
RELS = 100
CH = 104
NCH = TILES // CH
EPS = 1e-5
SCATTER = 23
STEPS = COLS // (2 * SCATTER)
BLOCKS5 = 5
assert TILES % GROUP == 0 and TILES % CH == 0 and STEPS * 2 * SCATTER == COLS
assert HALF // P * 2 + 1 + BUCKETS <= TILES


def dft(d):
    n = np.arange(d)[:, None] * np.arange(d // 2)[None, :] * (2 * np.pi / d)
    re, im = np.cos(n), -np.sin(n)
    im0 = im.copy()
    im[:, 0] = np.cos(np.pi * np.arange(d))
    fwd = np.concatenate([re, im], 1)
    neg = -re
    neg[:, 0] = im[:, 0]
    rel = np.concatenate([re, im0, neg], 1)
    inv = np.concatenate([2 * re, 2 * im], 1) / d
    inv[:, 0] = 1.0 / d
    inv[:, d // 2] = im[:, 0] / d
    return fwd.astype(np.float32), rel.astype(np.float32), inv.astype(np.float32)


def constants():
    c = np.zeros((P, 3 * P + 8 + BLOCKS), np.float32)
    q = np.arange(P)
    c[:, 0:P] = np.eye(P)
    c[:, P:2 * P] = (q[:, None] < q[None, :]) & (q[:, None] // HP == q[None, :] // HP)
    c[:, 2 * P:3 * P] = q[None, :]
    c[:, 3 * P] = q < HP
    c[:, 3 * P + 1] = q >= HP
    c[:, 3 * P + 2] = q
    c[:, 3 * P + 3] = 1
    c[:, 3 * P + 8:] = np.arange(BLOCKS)
    out = {"const_small": c}
    for d in (64, 128):
        fwd, rel, inv = dft(d)
        out[f"const_dft{d}"] = np.concatenate([fwd, rel, inv], 1)
    return out


class Signal:

    def __init__(self, ctx, nc, name):
        self.sem = ctx.enter_context(nc.semaphore(name))
        self.base = 0


class Chain:

    def __init__(self, eng, signal):
        self.eng, self.of, self.n, self.turn = eng, signal, signal.base, 0

    def __call__(self, ins):
        self.n += 1
        ins.then_inc(self.of.sem, 1)
        self.eng.wait_ge(self.of.sem, self.n + self.turn)

    def looped(self, count, per):
        self.turn = 0
        self.n += (count - 1) * per

    def close(self):
        self.of.base = self.n


def gnn_stack(nc, a, out):
    ctx = ExitStack()
    with ctx:
        used = {}

        def sb(name, shape, dt, c=ctx):
            used[name] = used.get(name, 0) + 1
            if used[name] > 1:
                name = f"{name}_{used[name]}"
            return c.enter_context(nc.sbuf_tensor(name, shape, dt))

        def signal(name):
            return Signal(ctx, nc, name)

        psum = ctx.enter_context(nc.psum_tensor("psum", [P, 8 * BANK], F32))
        load = signal("load")
        store = signal("store")
        vec = signal("vec")
        act_step = signal("act_step")
        pe_step = signal("pe_step")
        pool_step = signal("pool_step")
        passed = signal("passed")

        rec_d = nc.dram_tensor("sorted_edges", [SLOTS + P, 4], F32, kind="Internal").ap()
        typ_d = nc.dram_tensor("sorted_types", [TILES + 2 * GROUP, P], BF16, kind="Internal").ap()
        adj_d = nc.dram_tensor("adj_saved", [LO, BLOCKS * NODES], BF16, kind="Internal").ap()
        x_d = nc.dram_tensor("x_saved", [LO, BLOCKS * D], F32, kind="Internal").ap()
        table_d = {d: nc.dram_tensor(f"gather_table{d}", [2 * NODES, d], F32, kind="Internal").ap()
                   for d in (64, 128)}
        loop_d = {d: nc.dram_tensor(f"loop_term{d}", [LO, BLOCKS * d], F32, kind="Internal").ap()
                  for d in (64, 128)}

        cst = sb("cst", [P, 3 * P + 8 + BLOCKS], F32)
        ident, before = cst[:, 0:P], cst[:, P:2 * P]
        iota = cst[:, 2 * P:3 * P]
        in_half = [cst[:, 3 * P + h:3 * P + h + 1] for h in range(2)]
        part = cst[:, 3 * P + 2:3 * P + 3]
        kvals = cst[:, 3 * P + 8:]
        lo_s = sb("lo_s", [P, TILES + GROUP], F32)
        gidx_s = sb("gidx_s", [P, TILES + 2 * GROUP], I32)
        bucket_r = sb("bucket_r", [1, GROUP + TILES], I16)
        deg_half = sb("deg_half", [LO, BUCKETS], F32)
        deg_in = sb("deg_in", [LO, BLOCKS], F32)
        ones_f = sb("ones_f", [P, P], F32)
        one_col = cst[:, 3 * P + 3:3 * P + 4]
        ones_b = sb("ones_b", [P, 1], BF16)
        first_tile_i = sb("first_tile_i", [1, BUCKETS + 2], I32)
        x = sb("x", [LO, BLOCKS, D], F32)
        dinv = sb("dinv", [LO, BLOCKS], F32)
        dinv_half = sb("dinv_half", [LO, BLOCKS, 2], F32)
        rel = sb("rel", [RELS, D], F32)
        rel2 = sb("rel2", [RELS, 2 * D], F32)

        sort = ExitStack()
        with sort:
            src_i = sb("src_i", [P, COLS], I32, sort)
            dst_i = sb("dst_i", [P, COLS], I32, sort)
            typ_i = sb("typ_i", [P, COLS], I32, sort)
            src_f = sb("src_f", [P, COLS], F32, sort)
            key = sb("key", [P, COLS], F32, sort)
            tmp = sb("tmp", [P, COLS], F32, sort)
            run = sb("run", [P, COLS], F32, sort)
            rank = sb("rank", [P, COLS], F32, sort)
            mask = sb("mask", [P, COLS], F32, sort)
            rec = sb("rec", [P, COLS, 4], F32, sort)
            row_i = sb("row_i", [P, COLS], I32, sort)
            cnt = sb("cnt", [P, BLOCKS], F32, sort)
            tot = sb("tot", [P, BLOCKS, 2], F32, sort)
            tot_i = sb("tot_i", [P, BLOCKS, 2], I32, sort)
            nt = sb("nt", [P, BLOCKS, 2], F32, sort)
            incl = sb("incl", [P, BLOCKS, 2], F32, sort)
            base = sb("base", [P, BLOCKS], F32, sort)
            base2 = sb("base2", [P, BLOCKS], F32, sort)
            empty = sb("empty", [P, TILES, 4], F32, sort)
            st_rec = [sb(f"st_rec{h}", [P, SCATTER, 4], F32, sort) for h in range(2)]
            st_row = [sb(f"st_row{h}", [P, SCATTER], I32, sort) for h in range(2)]
            st_made, st_sent = signal("staged"), [signal(f"sent{h}") for h in range(2)]

            with nc.Block() as block:
                @block.vector
                def _(dve):
                    link = Chain(dve, vec)
                    for t, v in ((src_i, -1), (dst_i, 0), (typ_i, 0)):
                        link(nc.vector.memset(t[:], v))
                    link(nc.vector.memset(empty[:, :, 0], -1.0))
                    link(nc.vector.memset(empty[:, :, 1], 0.0))
                    link(nc.vector.memset(empty[:, :, 2], float(P - 1)))
                    link(nc.vector.memset(empty[:, :, 3], 0.0))
                    link(nc.vector.memset(rank[:], 0.0))
                    link(nc.vector.memset(ones_f[:], 1.0))
                    link(nc.vector.memset(ones_b[:], 1.0))
                    link.close()

            with nc.Block() as block:
                @block.sync
                def _(sp):
                    sp.dma_start(cst[:], a["const_small"]).then_inc(load.sem, 16)
                    n = 1
                    for t, name in ((src_i, "src"), (dst_i, "dst"), (typ_i, "edge_type_100")):
                        for h in range(2):
                            at = a[name][h * HALF:(h + 1) * HALF]
                            full = at[0:(HP - 1) * COLS].rearrange("(p c) -> p c", c=COLS)
                            rest = at[(HP - 1) * COLS:HALF].rearrange("(p c) -> p c", p=1)
                            sp.dma_start(t[h * HP:h * HP + HP - 1, :], full).then_inc(load.sem, 16)
                            sp.dma_start(t[h * HP + HP - 1:h * HP + HP, 0:LAST], rest).then_inc(load.sem, 16)
                            n += 2
                    sp.dma_start(rec_d[0:SLOTS, :].rearrange("(p t) w -> p (t w)", p=P),
                                 empty[:].rearrange("p t w -> p (t w)")).then_inc(store.sem, 16)
                    sp.wait_ge(load.sem, load.base + 16 * n)
                    sp.wait_ge(store.sem, store.base + 16)
                    load.base += 16 * n
                    store.base += 16

            with nc.Block() as block:
                @block.vector
                def _(dve):
                    link = Chain(dve, vec)
                    v = nc.vector
                    link(v.tensor_copy(src_f[:], src_i[:]))
                    link(v.tensor_scalar(row_i[:], src_f[:], 1.0 / BLOCKS, 0.02, ALU.mult, ALU.add))
                    link(v.tensor_copy(tmp[:], row_i[:]))
                    link(v.scalar_tensor_tensor(key[:], tmp[:], -float(BLOCKS), src_f[:], ALU.mult, ALU.add))
                    link(v.tensor_scalar(mask[:], key[:], 0.0, None, ALU.is_lt))
                    link(v.tensor_tensor(rec[:, :, 0], tmp[:], mask[:], ALU.subtract))
                    link(v.scalar_tensor_tensor(run[:], mask[:], float(BLOCKS), key[:], ALU.mult, ALU.add))
                    link(v.tensor_scalar(mask[:], src_f[:], 0.0, None, ALU.is_lt))
                    link(v.scalar_tensor_tensor(key[:], mask[:], 100.0, run[:], ALU.mult, ALU.add))
                    link(v.tensor_copy(tmp[:], dst_i[:]))
                    link(v.tensor_scalar(run[:], tmp[:], 1.0, None, ALU.mult))
                    link(v.tensor_scalar(base[:, 0:1], in_half[1], float(NODES), None, ALU.mult))
                    link(v.tensor_scalar(rec[:, :, 1], run[:], base[:, 0:1], None, ALU.add))
                    link(v.tensor_copy(rec[:, :, 2], typ_i[:]))
                    link(v.tensor_scalar(rec[:, :, 3], key[:], 2.0, in_half[1], ALU.mult, ALU.add))
                    with dve.Fori(0, BLOCKS) as k:
                        link.turn = k * 5
                        kv = kvals[:, bass.ds(k, 1)]
                        link(v.tensor_scalar(mask[:], key[:], kv, None, ALU.is_equal))
                        link(v.tensor_tensor_scan(run[:], mask[:], src_f[:], 0.0, ALU.add, ALU.bypass))
                        link(v.tensor_copy(cnt[:, bass.ds(k, 1)], run[:, COLS - 1:COLS]))
                        link(v.tensor_tensor(tmp[:], run[:], mask[:], ALU.mult))
                        link(v.tensor_tensor(rank[:], rank[:], tmp[:], ALU.add))
                    link.looped(BLOCKS, 5)
                    link.close()

            with nc.Block() as block:
                @block.tensor
                def _(pe):
                    nc.tensor.matmul(psum[:, 0:BLOCKS], before, cnt[:], start=True, stop=True)
                    for h in range(2):
                        last = nc.tensor.matmul(psum[:, BANK * (h + 1):BANK * (h + 1) + BLOCKS],
                                                in_half[h].to_broadcast([P, P]), cnt[:],
                                                start=True, stop=True)
                    last.then_inc(pe_step.sem, 1)

                @block.vector
                def _(dve):
                    link = Chain(dve, vec)
                    v = nc.vector
                    dve.wait_ge(pe_step.sem, pe_step.base + 1)
                    pe_step.base += 1
                    for h in range(2):
                        link(v.tensor_scalar(tot[:, :, h], psum[:, BANK * (h + 1):BANK * (h + 1) + BLOCKS],
                                             float(P - 1), None, ALU.add))
                    link(v.tensor_copy(tot_i[:], tot[:]))
                    link(v.tensor_scalar(tot_i[:], tot_i[:], 7, None, ALU.arith_shift_right))
                    link(v.tensor_copy(nt[:], tot_i[:]))
                    link(v.tensor_scalar(nt[:], nt[:], 1.0, None, ALU.max))
                    flat = nt[:].rearrange("p k h -> p (k h)")
                    link(v.tensor_tensor_scan(incl[:].rearrange("p k h -> p (k h)"), flat, flat,
                                              0.0, ALU.add, ALU.bypass))
                    link(v.tensor_tensor(incl[:], incl[:], nt[:], ALU.subtract))
                    link(v.memset(first_tile_i[:], TILES))
                    link(v.tensor_copy(first_tile_i[:, 0:BUCKETS],
                                       incl[0:1].rearrange("p k h -> p (k h)")))
                    link(v.tensor_scalar(base[:], incl[:, :, 0], in_half[0], float(P), ALU.mult, ALU.mult))
                    link(v.tensor_scalar(base2[:], incl[:, :, 1], in_half[1], float(P), ALU.mult, ALU.mult))
                    link(v.tensor_tensor(base[:], base[:], base2[:], ALU.add))
                    link(v.tensor_tensor(base[:], base[:], psum[:, 0:BLOCKS], ALU.add))
                    link(v.tensor_scalar(base[:], base[:], -1.0, None, ALU.add))
                    with dve.Fori(0, BLOCKS) as k:
                        link.turn = k * 2
                        link(v.tensor_scalar(tmp[:], key[:], kvals[:, bass.ds(k, 1)], base[:, bass.ds(k, 1)],
                                             ALU.is_equal, ALU.mult))
                        link(v.tensor_tensor(rank[:], rank[:], tmp[:], ALU.add))
                    link.looped(BLOCKS, 2)
                    link(v.tensor_copy(row_i[:], rank[:]))
                    link(v.tensor_scalar(row_i[:], row_i[:], 7, None, ALU.arith_shift_right))
                    link(v.tensor_copy(tmp[:], row_i[:]))
                    link(v.tensor_copy(row_i[:], rank[:]))
                    link(v.tensor_scalar(row_i[:], row_i[:], P - 1, None, ALU.bitwise_and))
                    link(v.tensor_copy(run[:], row_i[:]))
                    link(v.scalar_tensor_tensor(tmp[:], run[:], float(TILES), tmp[:], ALU.mult, ALU.add))
                    link(v.tensor_scalar(mask[:], src_f[:], 0.0, None, ALU.is_lt))
                    link(v.tensor_tensor_scan(run[:], mask[:], mask[:], 0.0, ALU.add, ALU.bypass))
                    link(v.tensor_scalar(base2[:, 0:1], in_half[1], float(HP), float(SLOTS - 1), ALU.mult, ALU.add))
                    link(v.scalar_tensor_tensor(mask[:], run[:], base2[:, 0:1], mask[:], ALU.add, ALU.mult))
                    link(v.tensor_scalar(run[:], src_f[:], 0.0, None, ALU.is_ge))
                    link(v.tensor_tensor(tmp[:], tmp[:], run[:], ALU.mult))
                    link(v.tensor_tensor(row_i[:], tmp[:], mask[:], ALU.add))
                    link.close()

            with nc.Block() as block:
                @block.vector
                def _(dve):
                    def stage(h, first):
                        at = bass.ds(first + h * SCATTER, SCATTER)
                        nc.vector.tensor_copy(st_row[h][:], row_i[:, at]).then_inc(st_made.sem, 1)
                        nc.vector.tensor_copy(st_rec[h][:], rec[:, at, :]).then_inc(st_made.sem, 1)
                    for h in range(2):
                        stage(h, 0)
                    with dve.Fori(1, STEPS) as k:
                        for h in range(2):
                            dve.wait_ge(st_sent[h].sem, k * (16 * SCATTER))
                            stage(h, k * (2 * SCATTER))

                @block.gpsimd
                def _(pool):
                    with pool.Fori(0, STEPS) as k:
                        for h in range(2):
                            pool.wait_ge(st_made.sem, k * 4 + 2 * h + 2)
                            pool.sem_inc(passed.sem)
                            for c in range(SCATTER):
                                nc.gpsimd.indirect_dma_start(
                                    rec_d, bass.IndirectOffsetOnAxis(ap=st_row[h][:, c:c + 1], axis=0),
                                    st_rec[h][:, c, :], None).then_inc(st_sent[h].sem, 16)
                    for h in range(2):
                        pool.wait_ge(st_sent[h].sem, 16 * SCATTER * STEPS)

        adj_stack = ExitStack()
        adj_t = sb("adj", [LO, BLOCKS * NODES], BF16, adj_stack)
        table = ExitStack()
        dst_s = sb("dst_s", [P, TILES], F32, table)
        with ExitStack() as t1:
            rec_s = sb("rec_s", [P, TILES, 4], F32, t1)
            m1 = sb("m1", [P, TILES], F32, t1)
            typ_t = sb("typ_t", [CH, NCH, P], BF16, t1)
            none_b = sb("none_b", [2 * GROUP, P], BF16, t1)
            with nc.Block() as block:
                @block.sync
                def _(sp):
                    sp.dma_start(rec_s[:].rearrange("p t w -> p (t w)"),
                                 rec_d[0:SLOTS, :].rearrange("(p t) w -> p (t w)", p=P)).then_inc(load.sem, 16)
                    sp.wait_ge(load.sem, load.base + 16)
                    load.base += 16

            with nc.Block() as block:
                @block.vector
                def _(dve):
                    link = Chain(dve, vec)
                    v = nc.vector
                    link(v.memset(none_b[:], float(P - 1)))
                    link(v.memset(lo_s[:], -1.0))
                    link(v.tensor_copy(lo_s[:, 0:TILES], rec_s[:, :, 0]))
                    link(v.memset(gidx_s[:], 0))
                    link(v.tensor_copy(gidx_s[:, 0:TILES], rec_s[:, :, 1]))
                    link(v.memset(bucket_r[:], 0))
                    link(v.tensor_copy(bucket_r[:, GROUP:], rec_s[0:1, :, 3]))
                    link(v.tensor_scalar(m1[:], rec_s[:, :, 1], float(NODES), -float(NODES), ALU.is_ge, ALU.mult))
                    link(v.tensor_tensor(dst_s[:], rec_s[:, :, 1], m1[:], ALU.add))
                    link.close()

            with nc.Block() as block:
                @block.tensor
                def _(pe):
                    for c in range(NCH):
                        nc.tensor.transpose(psum[0:CH, c * BANK:c * BANK + P], rec_s[:, c * CH:(c + 1) * CH, 2],
                                            ident).then_inc(pe_step.sem, 1)

                @block.vector
                def _(dve):
                    for c in range(NCH):
                        dve.wait_ge(pe_step.sem, pe_step.base + c + 1)
                        nc.vector.tensor_copy(typ_t[:, c, :], psum[0:CH, c * BANK:c * BANK + P]).then_inc(vec.sem, 1)

                @block.sync
                def _(sp):
                    sp.wait_ge(vec.sem, vec.base + NCH)
                    sp.dma_start(typ_d[0:TILES, :].rearrange("(c t) p -> t c p", t=CH),
                                 typ_t[:]).then_inc(store.sem, 16)
                    sp.dma_start(typ_d[TILES:TILES + 2 * GROUP, :], none_b[:]).then_inc(store.sem, 16)
                    sp.wait_ge(store.sem, store.base + 32)
            pe_step.base += NCH
            vec.base += NCH
            store.base += 32

        RING = 2
        with table:
            with ExitStack() as t2:
                iota16 = sb("iota16", [P, NODES], I16, t2)
                oh_dst = sb("oh_dst", [P, RING * NODES], BF16, t2)
                oh_src = sb("oh_src", [P, RING * P], BF16, t2)
                zeros = sb("zeros", [P, BANK], BF16, t2)
                tile_made, tile_done, banks_free = signal("tile_made"), signal("tile_done"), signal("banks_free")
                with nc.Block() as block:
                    @block.gpsimd
                    def _(pool):
                        nc.gpsimd.iota(iota16[:], pattern=[[1, NODES]], base=0,
                                       channel_multiplier=0).then_inc(pool_step.sem, 1)
                        pool.wait_ge(pool_step.sem, pool_step.base + 1)

                    @block.vector
                    def _(dve):
                        link = Chain(dve, vec)
                        link(nc.vector.memset(zeros[:], 0.0))
                        link.close()
                pool_step.base += 1

                with nc.Block() as block:
                    @block.vector
                    def _(dve):
                        with dve.Fori(0, TILES // RING) as i:
                            for u in range(RING):
                                dve.wait_ge(tile_done.sem, i * RING + u + 1)
                                nc.vector.tensor_scalar(oh_src[:, u * P:u * P + LO], iota16[:, 0:LO],
                                                        lo_s[:, bass.ds(i * RING + u, 1)], None, ALU.is_equal)
                                nc.vector.tensor_scalar(oh_dst[:, u * NODES:(u + 1) * NODES], iota16[:],
                                                        dst_s[:, bass.ds(i * RING + u, 1)], None,
                                                        ALU.is_equal).then_inc(tile_made.sem, 1)

                    @block.tensor
                    def _(pe):
                        pe.sem_inc(tile_done.sem, RING)
                        nc.tensor.matmul(psum[0:LO, 7 * BANK:8 * BANK], zeros[:, 0:LO], zeros[:],
                                         start=True, stop=False, skip_group_check=True)
                        with pe.Fori(0, BLOCKS) as b:
                            for bank in range(BANKS):
                                pe.wait_ge(banks_free.sem, b * BANKS + bank + 1)
                                nc.tensor.matmul(psum[0:LO, bank * BANK:(bank + 1) * BANK], zeros[:, 0:LO], zeros[:],
                                                 start=True, stop=False, skip_group_check=True)
                            for h in range(2):
                                t0 = pe.value_load(first_tile_i[0:1, bass.ds(b * 2 + h, 1)], min_val=0, max_val=TILES)
                                t1_ = pe.value_load(first_tile_i[0:1, bass.ds(b * 2 + h + 1, 1)], min_val=0, max_val=TILES)
                                with pe.Fori(t0, t1_) as t:
                                    pe.wait_ge(tile_made.sem, t + 1)
                                    lhs = oh_src[:, bass.ds((t % RING) * P, LO)]
                                    for bank in range(BANKS):
                                        w = min(BANK, NODES - bank * BANK)
                                        nc.tensor.matmul(psum[0:LO, bank * BANK:bank * BANK + w], lhs,
                                                         oh_dst[:, bass.ds((t % RING) * NODES + bank * BANK, w)],
                                                         start=False, stop=False, skip_group_check=True)
                                    nc.tensor.matmul(psum[0:LO, bass.ds(b * 2 + (7 * BANK + h), 1)], lhs, ones_b[:],
                                                     start=False, stop=False,
                                                     skip_group_check=True).then_inc(tile_done.sem, 1)

                    @block.scalar
                    def _(act):
                        act.sem_inc(banks_free.sem, BANKS)
                        with act.Fori(0, BLOCKS) as b:
                            t1_ = act.value_load(first_tile_i[0:1, bass.ds(b * 2 + 2, 1)], min_val=0, max_val=TILES)
                            act.wait_ge(tile_done.sem, t1_ + RING)
                            for bank in range(BANKS):
                                w = min(BANK, NODES - bank * BANK)
                                nc.scalar.copy(adj_t[:, bass.ds(b * NODES + bank * BANK, w)],
                                               psum[0:LO, bank * BANK:bank * BANK + w]).then_inc(banks_free.sem, 1)
                        act.wait_ge(banks_free.sem, BANKS * (BLOCKS + 1))
                        nc.scalar.copy(deg_half[:], psum[0:LO, 7 * BANK:7 * BANK + BUCKETS]).then_inc(act_step.sem, 1)
                        act.wait_ge(act_step.sem, act_step.base + 1)

                    @block.sync
                    def _(sp):
                        with sp.Fori(0, BLOCKS) as b:
                            sp.wait_ge(banks_free.sem, b * BANKS + 2 * BANKS)
                            sp.dma_start(adj_d[:, bass.ds(b * NODES, NODES)],
                                         adj_t[:, bass.ds(b * NODES, NODES)]).then_inc(store.sem, 16)
                        sp.wait_ge(store.sem, store.base + 16 * BLOCKS)
                act_step.base += 1
                store.base += 16 * BLOCKS

        adj = adj_t[:].rearrange("p (s l h) -> p s h l", s=BLOCKS, h=BLOCKS)

        agg_done, agg_out = signal("agg_done"), signal("agg_out")
        staged, turned, copied = signal("dense_staged"), signal("turned"), signal("copied")
        projected, evacuated = signal("projected"), signal("evacuated")
        with nc.Block() as block:
            @block.vector
            def _(dve):
                for s in (agg_out, turned, copied, projected, evacuated):
                    dve.sem_inc(s.sem)
                    s.base = 1

        def degrees_in():
            with nc.Block() as block:
                @block.tensor
                def _(pe):
                    with pe.Fori(0, BLOCKS) as d:
                        for s in range(BLOCKS):
                            mm = nc.tensor.matmul(psum[0:LO, bass.ds(d, 1)], adj[:, s, bass.ds(d, 1), :].rearrange("p a l -> p (a l)"),
                                                  ones_b[0:LO, :], start=(s == 0), stop=(s == BLOCKS - 1))
                        mm.then_inc(agg_done.sem, 1)

                @block.vector
                def _(dve):
                    dve.wait_ge(agg_done.sem, agg_done.base + BLOCKS)
                    link = Chain(dve, vec)
                    link(nc.vector.tensor_copy(deg_in[:], psum[0:LO, 0:BLOCKS]))
                    link.close()
            agg_done.base += BLOCKS

        def aggregate(c, h, res):
            parts = sb("agg_parts", [LO, BLOCKS, 3 * D], BF16, c)
            rem = sb("agg_rem", [LO, BLOCKS, D], F32, c)
            with nc.Block() as block:
                @block.vector
                def _(dve):
                    link = Chain(dve, vec)
                    v = nc.vector
                    link(v.tensor_copy(parts[:, :, 0:D], h))
                    link(v.tensor_tensor(rem[:], h, parts[:, :, 0:D], ALU.subtract))
                    link(v.tensor_copy(parts[:, :, D:2 * D], rem[:]))
                    link(v.tensor_tensor(parts[:, :, 2 * D:3 * D], rem[:], parts[:, :, D:2 * D], ALU.subtract))
                    link.close()

            with nc.Block() as block:
                @block.tensor
                def _(pe):
                    with pe.Fori(0, BLOCKS // BLOCKS5) as i:
                        pe.wait_ge(agg_out.sem, i * BLOCKS5 + agg_out.base)
                        for k in range(BLOCKS5):
                            for s in range(BLOCKS):
                                mm = nc.tensor.matmul(psum[0:LO, k * BANK:k * BANK + 3 * D],
                                                      adj[:, s, bass.ds(i * BLOCKS5 + k, 1), :].rearrange("p a l -> p (a l)"),
                                                      parts[:, s, :],
                                                      start=(s == 0), stop=(s == BLOCKS - 1))
                            mm.then_inc(agg_done.sem, 1)

                @block.vector
                def _(dve):
                    with dve.Fori(0, BLOCKS // BLOCKS5) as i:
                        for k in range(BLOCKS5):
                            dve.wait_ge(agg_done.sem, i * BLOCKS5 + k + 1 + agg_done.base)
                            nc.vector.tensor_reduce(
                                res[:, bass.ds(i * BLOCKS5 + k, 1), :].rearrange("p a f -> p (a f)"),
                                psum[0:LO, k * BANK:k * BANK + 3 * D].rearrange("p (c f) -> p f c", c=3),
                                AX.X, ALU.add).then_inc(agg_out.sem, 1)
                    dve.wait_ge(agg_out.sem, agg_out.base + BLOCKS)
            agg_done.base += BLOCKS
            agg_out.base += BLOCKS

        def project(ins, K, ws, res, M):
            C = len(ins)
            with ExitStack() as c:
                stage = sb("stage", [LO, C, BLOCKS5, K], F32, c)
                turn = sb("turn", [K, BLOCKS5, C * LO], F32, c)
                with nc.Block() as block:
                    @block.scalar
                    def _(act):
                        with act.Fori(0, BLOCKS // BLOCKS5) as i:
                            act.wait_ge(turned.sem, i * BLOCKS5 + turned.base)
                            for n in range(C):
                                nc.scalar.copy(stage[:, n, :, :], ins[n][:, bass.ds(i * BLOCKS5, BLOCKS5), :]).then_inc(staged.sem, 1)
                            for k in range(BLOCKS5):
                                act.wait_ge(turned.sem, i * BLOCKS5 + k + 1 + turned.base)
                                act.wait_ge(projected.sem, i * BLOCKS5 + projected.base)
                                nc.scalar.copy(turn[:, k, :], psum[0:K, k * BANK:k * BANK + C * LO]).then_inc(copied.sem, 1)

                    @block.tensor
                    def _(pe):
                        with pe.Fori(0, BLOCKS // BLOCKS5) as i:
                            pe.wait_ge(staged.sem, i * C + C + staged.base)
                            pe.wait_ge(copied.sem, i * BLOCKS5 + copied.base)
                            pe.sem_inc(passed.sem)
                            for k in range(BLOCKS5):
                                for n in range(C):
                                    mm = nc.tensor.transpose(psum[0:K, k * BANK + n * LO:k * BANK + (n + 1) * LO],
                                                             stage[:, n, k, :], ident[0:LO, 0:LO])
                                mm.then_inc(turned.sem, 1)
                            pe.wait_ge(evacuated.sem, i + evacuated.base)
                            for k in range(BLOCKS5):
                                pe.wait_ge(copied.sem, i * BLOCKS5 + k + 1 + copied.base)
                                for n in range(C):
                                    mm = nc.tensor.matmul(psum[0:LO, 5 * BANK + k * P:5 * BANK + k * P + M],
                                                          turn[:, k, n * LO:(n + 1) * LO], ws[n],
                                                          start=(n == 0), stop=(n == C - 1))
                                mm.then_inc(projected.sem, 1)

                    @block.vector
                    def _(dve):
                        with dve.Fori(0, BLOCKS // BLOCKS5) as i:
                            dve.wait_ge(projected.sem, i * BLOCKS5 + BLOCKS5 + projected.base)
                            nc.vector.tensor_copy(
                                res[:, bass.ds(i * BLOCKS5, BLOCKS5), :],
                                psum[0:LO, 5 * BANK:5 * BANK + BLOCKS5 * P].rearrange("p (k m) -> p k m", m=P)[:, :, 0:M],
                            ).then_inc(evacuated.sem, 1)
                        dve.wait_ge(evacuated.sem, evacuated.base + BLOCKS // BLOCKS5)
            turned.base += BLOCKS
            copied.base += BLOCKS
            projected.base += BLOCKS
            staged.base += C * (BLOCKS // BLOCKS5)
            evacuated.base += BLOCKS // BLOCKS5

        def over_nodes(v, m):
            return v.rearrange("p (a m) -> p a m", a=1).to_broadcast([LO, BLOCKS, m])

        def over_features(v, m):
            return v.rearrange("p (b a) -> p b a", a=1).to_broadcast([LO, BLOCKS, m])

        def vector_steps(steps):
            with nc.Block() as block:
                @block.vector
                def _(dve):
                    link = Chain(dve, vec)
                    steps(nc.vector, link)
                    link.close()

        def scalar_step(step):
            with nc.Block() as block:
                @block.scalar
                def _(act):
                    link = Chain(act, act_step)
                    link(step())
                    link.close()

        def load_all(pairs):
            with nc.Block() as block:
                @block.sync
                def _(sp):
                    for dst, src in pairs:
                        sp.dma_start(dst, src).then_inc(load.sem, 16)
                    sp.wait_ge(load.sem, load.base + 16 * len(pairs))
            load.base += 16 * len(pairs)

        def store_all(pairs):
            with nc.Block() as block:
                @block.sync
                def _(sp):
                    for dst, src in pairs:
                        sp.dma_start(dst, src).then_inc(store.sem, 16)
                    sp.wait_ge(store.sem, store.base + 16 * len(pairs))
            store.base += 16 * len(pairs)

        def row(name, n):
            return a[name].rearrange("(a n) -> a n", a=1).to_broadcast([LO, n])

        def inverse_root(c, name, v):
            root = sb(name, list(v.shape), F32, c)
            scalar_step(lambda: nc.scalar.activation(root[:], v, ACT.Sqrt))
            vector_steps(lambda e, link: link(e.reciprocal(v, root[:])))

        def layer_norm(y):
            with ExitStack() as c:
                mean = sb("ln_mean", [LO, BLOCKS], F32, c)
                var = sb("ln_var", [LO, BLOCKS], F32, c)
                sq = sb("ln_sq", [LO, BLOCKS, D], F32, c)

                def center(v, link):
                    link(v.tensor_tensor(x[:], x[:], y, ALU.add))
                    link(v.tensor_reduce(mean[:], x[:], AX.X, ALU.add))
                    link(v.tensor_scalar(mean[:], mean[:], 1.0 / D, None, ALU.mult))
                    link(v.tensor_tensor(x[:], x[:], over_features(mean[:], D), ALU.subtract))
                    link(v.tensor_tensor(sq[:], x[:], x[:], ALU.mult))
                    link(v.tensor_reduce(var[:], sq[:], AX.X, ALU.add))
                    link(v.tensor_scalar(var[:], var[:], 1.0 / D, EPS, ALU.mult, ALU.add))
                vector_steps(center)
                inverse_root(c, "ln_root", var[:])
                vector_steps(lambda v, link: link(v.tensor_tensor(x[:], x[:], over_features(var[:], D), ALU.mult)))

        def batch_norm(y, m, gamma, beta):
            with ExitStack() as c:
                part_sum = sb("bn_part", [LO, m], F32, c)
                stat = sb("bn_stat", [LO, m], F32, c)
                sq = sb("bn_sq", [LO, BLOCKS, m], F32, c)

                def total(src, finish):
                    vector_steps(lambda v, link: link(v.tensor_reduce(part_sum[:], src.rearrange("p b m -> p m b"), AX.X, ALU.add)))
                    with nc.Block() as block:
                        @block.tensor
                        def _(pe):
                            nc.tensor.matmul(psum[0:LO, 0:m], ones_f[0:LO, 0:LO], part_sum[:],
                                             start=True, stop=True).then_inc(pe_step.sem, 1)

                        @block.vector
                        def _(dve):
                            dve.wait_ge(pe_step.sem, pe_step.base + 1)
                            link = Chain(dve, vec)
                            finish(nc.vector, link)
                            link.close()
                    pe_step.base += 1

                def center(v, link):
                    link(v.tensor_scalar(stat[:], psum[0:LO, 0:m], 1.0 / NODES, None, ALU.mult))
                    link(v.tensor_tensor(y, y, over_nodes(stat[:], m), ALU.subtract))
                    link(v.tensor_tensor(sq[:], y, y, ALU.mult))
                total(y, center)
                total(sq[:], lambda v, link: link(v.tensor_scalar(stat[:], psum[0:LO, 0:m], 1.0 / NODES, EPS, ALU.mult, ALU.add)))
                inverse_root(c, "bn_root", stat[:])

                def scale(v, link):
                    link(v.tensor_tensor(stat[:], stat[:], gamma, ALU.mult))
                    link(v.tensor_tensor(y, y, over_nodes(stat[:], m), ALU.mult))
                    link(v.tensor_tensor(y, y, over_nodes(beta, m), ALU.add))
                vector_steps(scale)

        load_all([(x[:].rearrange("p b f -> p (b f)"), a["x"].rearrange("(p b) f -> p (b f)", b=BLOCKS))])
        degrees_in()
        with ExitStack() as c:
            vectors = ["b1", "g1", "be1", "rm1", "rv1", "b2", "g2", "be2", "rm2", "rv2"]
            vs = sb("l0_vectors", [LO, len(vectors), D], F32, c)
            w = sb("l0_w", [D, 2, D], F32, c)
            load_all([(vs[:, i, :], row(f"L0_gnn_{n}", D)) for i, n in enumerate(vectors)]
                     + [(w[:, i, :], a[f"L0_gnn_W{i + 1}"]) for i in range(2)])
            at = {n: vs[:, i, :] for i, n in enumerate(vectors)}
            vector_steps(lambda v, link: (link(v.tensor_scalar(dinv[:], deg_in[:], 1.0, None, ALU.add)),
                                          link(v.tensor_scalar(at["rv1"], at["rv1"], EPS, None, ALU.add)),
                                          link(v.tensor_scalar(at["rv2"], at["rv2"], EPS, None, ALU.add))))
            inverse_root(c, "dinv_root", dinv[:])
            inverse_root(c, "rv1_root", at["rv1"])
            inverse_root(c, "rv2_root", at["rv2"])
            h = sb("l0_h", [LO, BLOCKS, D], F32, c)
            y = sb("l0_y", [LO, BLOCKS, D], F32, c)
            vector_steps(lambda v, link: link(v.tensor_copy(h[:], x[:])))
            for i in (1, 2):
                with ExitStack() as c2:
                    vector_steps(lambda v, link: link(v.tensor_tensor(h[:], h[:], over_features(dinv[:], D), ALU.mult)))
                    aggregate(c2, h[:], y[:])
                    vector_steps(lambda v, link: (link(v.tensor_tensor(y[:], y[:], h[:], ALU.add)),
                                                  link(v.tensor_tensor(y[:], y[:], over_features(dinv[:], D), ALU.mult))))
                project([y[:]], D, [w[:, i - 1, :]], h[:], D)

                def norm(v, link, i=i):
                    link(v.tensor_tensor(at[f"g{i}"], at[f"g{i}"], at[f"rv{i}"], ALU.mult))
                    link(v.tensor_tensor(at[f"b{i}"], at[f"b{i}"], at[f"rm{i}"], ALU.subtract))
                    link(v.tensor_tensor(h[:], h[:], over_nodes(at[f"b{i}"], D), ALU.add))
                    link(v.tensor_tensor(h[:], h[:], over_nodes(at[f"g{i}"], D), ALU.mult))
                    link(v.tensor_tensor(h[:], h[:], over_nodes(at[f"be{i}"], D), ALU.add))
                    if i == 1:
                        link(v.tensor_scalar(h[:], h[:], 0.0, None, ALU.max))
                vector_steps(norm)
            top = sb("l0_top", [LO, BLOCKS], F32, c)
            total = sb("l0_total", [LO, BLOCKS], F32, c)
            vector_steps(lambda v, link: (link(v.tensor_reduce(top[:], h[:], AX.X, ALU.max)),
                                          link(v.tensor_tensor(h[:], h[:], over_features(top[:], D), ALU.subtract))))
            scalar_step(lambda: nc.scalar.activation(y[:], h[:], ACT.Exp))
            vector_steps(lambda v, link: link(v.tensor_reduce(total[:], y[:], AX.X, ALU.add)))
            scalar_step(lambda: nc.scalar.activation(top[:], total[:], ACT.Ln))
            vector_steps(lambda v, link: link(v.tensor_tensor(h[:], h[:], over_features(top[:], D), ALU.subtract)))
            layer_norm(h[:])

        with ExitStack() as c:
            w1 = sb("l1_w1", [D, 2, 2 * D], F32, c)
            w2 = sb("l1_w2", [2 * D, D], F32, c)
            b1 = sb("l1_b1", [LO, 2 * D], F32, c)
            b2 = sb("l1_b2", [LO, D], F32, c)
            load_all([(w1[:], a["L1_gnn_W1"].rearrange("(c k) m -> k c m", c=2)), (w2[:], a["L1_gnn_W2"]),
                      (b1[:], row("L1_gnn_b1", 2 * D)), (b2[:], row("L1_gnn_b2", D))])
            y = sb("l1_y", [LO, BLOCKS, D], F32, c)
            with ExitStack() as c2:
                aggregate(c2, x[:], y[:])
            hid = sb("l1_hid", [LO, BLOCKS, 2 * D], F32, c)
            project([x[:], y[:]], D, [w1[:, 0, :], w1[:, 1, :]], hid[:], 2 * D)
            vector_steps(lambda v, link: (link(v.tensor_tensor(hid[:], hid[:], over_nodes(b1[:], 2 * D), ALU.add)),
                                          link(v.tensor_scalar(hid[:], hid[:], 0.0, None, ALU.max))))
            project([hid[:]], 2 * D, [w2[:]], y[:], D)
            vector_steps(lambda v, link: link(v.tensor_tensor(y[:], y[:], over_nodes(b2[:], D), ALU.add)))
            layer_norm(y[:])
        adj_stack.close()

        with ExitStack() as c:
            some = sb("some", [LO, BLOCKS, 2], F32, c)
            deg3 = deg_half[:].rearrange("p (b h) -> p b h", h=2)
            vector_steps(lambda v, link: (link(v.tensor_scalar(some[:], deg3, 0.0, None, ALU.is_gt)),
                                          link(v.tensor_scalar(dinv_half[:], deg3, 1.0, None, ALU.max))))
            inverse_root(c, "half_root", dinv_half[:])
            vector_steps(lambda v, link: link(v.tensor_tensor(dinv_half[:], dinv_half[:], some[:], ALU.mult)))

        RING = 4
        gathered = [signal(f"gathered{u}") for u in range(RING)]
        typed = [signal(f"typed{u}") for u in range(RING)]
        idx_ready, oh_t_made, oh_s_made = signal("idx_ready"), signal("oh_t_made"), signal("oh_s_made")
        rel_done, mult_done, prod_done = signal("rel_done"), signal("mult_done"), signal("prod_done")
        scat_done, squared, zeroed = signal("scat_done"), signal("squared"), signal("zeroed")
        TURNS = GROUPS // RING

        def edge_pass(d, acc, rel_parts):
            W = 3 * d // 2
            RS = 2 * d
            RB = GROUP * RS
            with ExitStack() as c:
                gi = [sb(f"gi{u}", [P, GROUP], I32, c) for u in range(RING)]
                gx = [sb(f"gx{u}", [P, GROUP, d], F32, c) for u in range(RING)]
                tb = [sb(f"tb{u}", [P, GROUP * P], BF16, c) for u in range(RING)]
                oh_t = [sb(f"oh_t{u}", [P, GROUP * P], BF16, c) for u in range(2)]
                oh_s = [sb(f"oh_s{u}", [P, GROUP, LO], F32, c) for u in range(2)]
                part_prod = sb("part_prod", [P, GROUP, 2, d], F32, c)
                zero_f = sb("zero_f", [P, LO], F32, c)
                sq_s = sb("sq_s", [P, GROUP, LO], F32, c)
                prod = [sb(f"prod{u}", [P, GROUP, d], F32, c) for u in range(2)]
                ps_rel = [psum[:, u * RB:(u + 1) * RB] for u in range(2)]
                ps_out = [psum[0:LO, 2 * RB + u * BANK:2 * RB + u * BANK + GROUP * d] for u in range(2)]
                types = typ_d.rearrange("(a t) p -> a (t p)", a=1)
                acc2 = acc.rearrange("p k f -> p (k f)")
                with nc.Block() as block:
                    @block.gpsimd
                    def _(pool):
                        with pool.Fori(0, TURNS) as i:
                            for u in range(RING):
                                g1 = i * RING + (u + 1)
                                pool.wait_ge(mult_done.sem, g1 + mult_done.base)
                                pool.wait_ge(idx_ready.sem, g1 + idx_ready.base)
                                pool.sem_inc(passed.sem)
                                for k in range(GROUP):
                                    nc.gpsimd.indirect_dma_start(
                                        gx[u][:, k, :], None, table_d[d],
                                        bass.IndirectOffsetOnAxis(ap=gi[u][:, k:k + 1], axis=0),
                                    ).then_inc(gathered[u].sem, 16)

                    @block.scalar
                    def _(act):
                        def indices(u, at):
                            nc.scalar.copy(gi[u][:], gidx_s[:, bass.ds(at, GROUP)]).then_inc(idx_ready.sem, 1)

                        def src_one_hot(at, u, n):
                            for k in range(GROUP):
                                if k == 0:
                                    act.wait_ge(scat_done.sem, n + scat_done.base)
                                    act.wait_ge(oh_s_made.sem, n + oh_s_made.base)
                                sq = nc.scalar.activation(sq_s[:, k, :], iota[:, 0:LO], ACT.Square,
                                                          bias=lo_s[:, bass.ds(at + k, 1)], scale=-1.0)
                            sq.then_inc(squared.sem, 1)
                            act.wait_ge(squared.sem, n + squared.base)
                            nc.scalar.activation(oh_s[u % 2][:], sq_s[:], ACT.Relu, bias=one_col,
                                                 scale=-2.0).then_inc(oh_s_made.sem, 1)
                        act.sem_inc(oh_s_made.sem)
                        act.sem_inc(scat_done.sem)
                        for u in range(RING):
                            indices(u, u * GROUP)

                        def ahead(u, turn):
                            w = (u + 2) % RING
                            act.wait_ge(gathered[w].sem, (turn + u // 2) * (16 * GROUP) + gathered[w].base)
                            indices(w, turn * (RING * GROUP) + (u + 2) * GROUP)

                        for u in range(RING):
                            if u >= 2:
                                ahead(u, 0)
                            src_one_hot(u * GROUP, u, u + 1)
                        with act.Fori(1, TURNS) as i:
                            for u in range(RING):
                                ahead(u, i)
                                src_one_hot(i * (RING * GROUP) + u * GROUP, u, i * RING + (u + 1))

                    @block.sync
                    def _(sp):
                        def types_of(at, u, n):
                            sp.wait_ge(oh_t_made.sem, n)
                            sp.dma_start(tb[u][:], types[:, bass.ds(at, GROUP * P)].to_broadcast([P, GROUP * P])).then_inc(typed[u].sem, 16)
                        with sp.Fori(0, TURNS) as i:
                            for u in range(RING):
                                types_of(i * (RING * GROUP * P) + u * GROUP * P, u, i * RING + (u + 1) + oh_t_made.base)
                        for u in range(2):
                            types_of((GROUPS + u) * GROUP * P, u, GROUPS + u + 1 + oh_t_made.base)

                    @block.vector
                    def _(dve):
                        link = Chain(dve, vec)
                        v = nc.vector
                        dve.sem_inc(mult_done.sem, RING)
                        dve.sem_inc(prod_done.sem)
                        dve.sem_inc(oh_t_made.sem, RING)

                        def type_one_hot(u, n):
                            dve.wait_ge(typed[u].sem, n * 16 + 16 + typed[u].base)
                            v.tensor_scalar(oh_t[u % 2][:], tb[u][:], part, None, ALU.is_equal).then_inc(oh_t_made.sem, 1)

                        def add(bucket, u, k):
                            to = acc2[:, bass.ds(bucket * d, d)]
                            link(v.tensor_tensor(to, to, ps_out[u % 2][:, k * d:(k + 1) * d], ALU.add))

                        link(v.memset(acc, 0.0))
                        v.memset(zero_f[:], 0.0).then_inc(zeroed.sem, 1)
                        type_one_hot(0, 0)
                        type_one_hot(1, 0)
                        regs = [[dve.alloc_register(f"bucket{d}_{u}_{k}") for k in range(GROUP)] for u in range(RING)]

                        def load_buckets(u, first):
                            dve.load(regs[u], bucket_r[0:1, bass.ds(first, GROUP)])
                            return [dve.snap(r, min_val=0, max_val=BUCKETS - 1) for r in regs[u]]

                        with dve.Fori(0, TURNS) as i:
                            link.turn = i * (RING * GROUP)
                            for u in range(RING):
                                g1 = i * RING + (u + 1)
                                dve.wait_ge(rel_done.sem, g1 + rel_done.base)

                                type_one_hot((u + 2) % RING, i + (u + 2) // RING)
                                dve.wait_ge(gathered[u].sem, i * (16 * GROUP) + 16 * GROUP + gathered[u].base)
                                dve.wait_ge(prod_done.sem, g1 + prod_done.base)
                                rel = ps_rel[u % 2].rearrange("p (g w) -> p g w", w=RS)
                                for s in range(2):
                                    mul = v.tensor_tensor(
                                        part_prod[:, :, s, :].rearrange("p g (a f) -> p g a f", a=2),
                                        gx[u][:, :, s * d // 2:(s + 1) * d // 2].rearrange("p g (a f) -> p g a f", a=1).to_broadcast([P, GROUP, 2, d // 2]),
                                        rel[:, :, s * d // 2:s * d // 2 + d].rearrange("p g (a f) -> p g a f", a=2),
                                        ALU.mult)
                                mul.then_inc(mult_done.sem, 1)
                                buckets = load_buckets(u, i * (RING * GROUP) + u * GROUP)

                                def add_last(k):
                                    add(buckets[k], u + 1, k)

                                dve.wait_ge(scat_done.sem, g1 + 1 + scat_done.base)
                                add_last(0)
                                dve.wait_ge(mult_done.sem, g1 + RING + mult_done.base)
                                v.tensor_tensor(prod[u % 2][:], part_prod[:, :, 0, :], part_prod[:, :, 1, :],
                                                ALU.add).then_inc(prod_done.sem, 1)
                                add_last(1)
                                add_last(2)
                                add_last(3)
                        link.turn = 0
                        link.n += (TURNS - 1) * RING * GROUP
                        buckets = load_buckets(0, TURNS * RING * GROUP)
                        dve.wait_ge(scat_done.sem, GROUPS + 2 + scat_done.base)
                        for k in range(GROUP):
                            add(buckets[k], RING - 1, k)
                        link.close()

                    @block.tensor
                    def _(pe):
                        def relations(u, n, free):
                            pe.wait_ge(oh_t_made.sem, n + RING + oh_t_made.base)
                            pe.wait_ge(mult_done.sem, free)
                            for k in range(GROUP):
                                for s in range(3):
                                    mm = nc.tensor.matmul(ps_rel[u % 2][:, k * RS:k * RS + W], oh_t[u % 2][:, k * P:(k + 1) * P],
                                                          rel_parts[:, s, :], start=(s == 0), stop=(s == 2))
                            mm.then_inc(rel_done.sem, 1)

                        for u in range(2):
                            relations(u, u + 1, RING + mult_done.base)
                        pe.wait_ge(zeroed.sem, 1 + zeroed.base)
                        for k in range(GROUP):
                            mm = nc.tensor.matmul(ps_out[1][:, k * d:(k + 1) * d], zero_f[:], zero_f[:, 0:1].to_broadcast([P, d]),
                                                  start=True, stop=True)
                        mm.then_inc(scat_done.sem, 1)
                        with pe.Fori(0, TURNS) as i:
                            for u in range(RING):
                                g1 = i * RING + (u + 1)
                                pe.wait_ge(oh_s_made.sem, g1 + 1 + oh_s_made.base)
                                pe.wait_ge(prod_done.sem, g1 + 1 + prod_done.base)
                                for k in range(GROUP):
                                    mm = nc.tensor.matmul(ps_out[u % 2][:, k * d:(k + 1) * d], oh_s[u % 2][:, k, :],
                                                          prod[u % 2][:, k, :], start=True, stop=True)
                                mm.then_inc(scat_done.sem, 1)
                                relations(u % 2, g1 + 2, g1 + RING + mult_done.base)
            for s, n in ((mult_done, GROUPS + RING), (oh_t_made, GROUPS + 2 + RING), (oh_s_made, GROUPS + 1), (squared, GROUPS), (zeroed, 1),
                         (idx_ready, GROUPS + 2), (rel_done, GROUPS + 2), (prod_done, GROUPS + 1), (scat_done, GROUPS + 2),
                         (typed[0], 16), (typed[1], 16)):
                s.base += n
            for u in range(RING):
                gathered[u].base += 16 * GROUP * TURNS
                typed[u].base += 16 * TURNS

        def small_products(jobs):
            with nc.Block() as block:
                @block.tensor
                def _(pe):
                    for j, (to, lhs, rhs, turned_) in enumerate(jobs):
                        k, m = to.shape
                        where = psum[0:k, j * BANK:j * BANK + m]
                        mm = nc.tensor.transpose(where, lhs, rhs) if turned_ else \
                            nc.tensor.matmul(where, lhs, rhs, start=True, stop=True)
                        mm.then_inc(pe_step.sem, 1)

                @block.vector
                def _(dve):
                    link = Chain(dve, vec)
                    for j, (to, *_) in enumerate(jobs):
                        k, m = to.shape
                        dve.wait_ge(pe_step.sem, pe_step.base + j + 1)
                        link(nc.vector.tensor_copy(to, psum[0:k, j * BANK:j * BANK + m]))
                    link.close()
            pe_step.base += len(jobs)

        load_all([(rel[:], a["L2_gnn_init_rel"])])

        def comp_layer(c, n, d, m, feats, rel_in, res, rel_next):
            W = 3 * d // 2
            pre = f"L2_gnn_c{n}_"
            wp = sb(f"wp{n}", [d, 3, m], F32, c)
            rel_parts = sb(f"rel_parts{n}", [P, 3, W], BF16, c)
            with ExitStack() as c2:
                dftc = sb(f"dft{n}", [d, 2 * d + W], F32, c2)
                win = sb(f"w{n}", [d, 3, m], F32, c2)
                wrel = sb(f"wrel{n}", [d, m], F32, c2)
                loop_col = sb(f"loop_col{n}", [d, 1], F32, c2)
                rel_t = sb(f"rel_t{n}", [d, RELS], F32, c2)
                inv_t = sb(f"inv_t{n}", [d, d], F32, c2)
                rel_f = sb(f"rel_f{n}", [P, W], F32, c2)
                loop_f = sb(f"loop_f{n}", [LO, W], F32, c2)
                load_all([(dftc[:], a[f"const_dft{d}"]), (wrel[:], a[pre + "w_rel"]),
                          (loop_col[:], a[pre + "loop_rel"].rearrange("a (k b) -> (a k) b", b=1))]
                         + [(win[:, i, :], a[pre + w]) for i, w in enumerate(("w_in", "w_out", "w_loop"))])
                fwd, relm, inv = dftc[:, 0:d], dftc[:, d:d + W], dftc[:, d + W:2 * d + W]
                vector_steps(lambda v, link: (link(v.memset(rel_f[:], 0.0)), link(v.memset(rel_parts[:], 0.0))))
                small_products([(rel_t[:], rel_in, ident[0:RELS, 0:RELS], True),
                                (inv_t[:], inv, ident[0:d, 0:d], True),
                                (loop_f[:], loop_col[:].to_broadcast([d, LO]), relm, False)])
                jobs = [(rel_f[0:RELS, :], rel_t[:], relm, False)]
                jobs += [(wp[:, i, :], inv, win[:, i, :], False) for i in range(3)]
                if rel_next is not None:
                    jobs += [(rel_next, rel_t[:], wrel[:], False)]
                small_products(jobs)

                rem = sb(f"rel_rem{n}", [P, W], F32, c2)

                def split(v, link):
                    link(v.tensor_copy(rel_parts[:, 0, :], rel_f[:]))
                    link(v.tensor_tensor(rem[:], rel_f[:], rel_parts[:, 0, :], ALU.subtract))
                    link(v.tensor_copy(rel_parts[:, 1, :], rem[:]))
                    link(v.tensor_tensor(rel_parts[:, 2, :], rem[:], rel_parts[:, 1, :], ALU.subtract))
                vector_steps(split)
                xf = sb(f"xf{n}", [LO, BLOCKS, d], F32, c2)
                project([feats], d, [fwd], xf[:], d)
                with ExitStack() as c3:
                    sc = sb(f"scaled{n}", [LO, BLOCKS, d], F32, c3)
                    for hf in range(2):
                        vector_steps(lambda v, link: link(v.tensor_tensor(sc[:], xf[:], over_features(dinv_half[:, :, hf], d), ALU.mult)))
                        store_all([(table_d[d][hf * NODES:(hf + 1) * NODES, :].rearrange("(p b) f -> p (b f)", b=BLOCKS),
                                    sc[:].rearrange("p b f -> p (b f)"))])
                    def loop_term(v, link):
                        half = d // 2
                        for o in range(2):
                            to = keep[:, :, o * half:(o + 1) * half]
                            for s, t in ((0, to), (1, tmp2[:])):
                                link(v.tensor_tensor(t, xf[:, :, s * half:(s + 1) * half],
                                                     over_nodes(loop_f[:, (s + o) * half:(s + o + 1) * half], half), ALU.mult))
                            link(v.tensor_tensor(to, to, tmp2[:], ALU.add))
                    tmp2 = sb(f"loop_tmp{n}", [LO, BLOCKS, d // 2], F32, c3)
                    keep = sb(f"loop_keep{n}", [LO, BLOCKS, d], F32, c3)
                    vector_steps(loop_term)
                    store_all([(loop_d[d], keep[:].rearrange("p b f -> p (b f)"))])
            acc = sb(f"acc{n}", [LO, BUCKETS, d], F32, c)
            edge_pass(d, acc[:], rel_parts)
            acc3 = acc[:].rearrange("p (b h) f -> p b h f", h=2)
            with ExitStack() as c2:
                lt = sb(f"lt{n}", [LO, BLOCKS, d], F32, c2)
                load_all([(lt[:].rearrange("p b f -> p (b f)"), loop_d[d])])
                vector_steps(lambda v, link: [link(v.tensor_tensor(acc3[:, :, hf, :], acc3[:, :, hf, :],
                                                                   over_features(dinv_half[:, :, hf], d), ALU.mult)) for hf in range(2)])
                project([acc3[:, :, 0, :], acc3[:, :, 1, :], lt[:]], d, [wp[:, i, :] for i in range(3)], res, m)

        def finish_comp(n, m, y):
            pre = f"L2_gnn_c{n}_"
            with ExitStack() as c:
                vb = sb(f"comp_v{n}", [LO, 3, m], F32, c)
                load_all([(vb[:, i, :], row(pre + w, m)) for i, w in enumerate(("bias", "gamma", "beta"))])
                vector_steps(lambda v, link: (link(v.tensor_scalar(y, y, 1.0 / 3.0, None, ALU.mult)),
                                              link(v.tensor_tensor(y, y, over_nodes(vb[:, 0, :], m), ALU.add))))
                batch_norm(y, m, vb[:, 1, :], vb[:, 2, :])
                scalar_step(lambda: nc.scalar.activation(y, y, ACT.Tanh))

        with ExitStack() as c:
            y1 = sb("comp_y1", [LO, BLOCKS, 2 * D], F32, c)
            y2 = sb("comp_y2", [LO, BLOCKS, D], F32, c)
            with ExitStack() as c2:
                comp_layer(c2, 1, D, 2 * D, x[:], rel[:], y1[:], rel2[:])
            finish_comp(1, 2 * D, y1[:])
            with ExitStack() as c2:
                comp_layer(c2, 2, 2 * D, D, y1[:], rel2[:], y2[:], None)
            finish_comp(2, D, y2[:])
            layer_norm(y2[:])

        with ExitStack() as c:
            adj_t = sb("adj_again", [LO, BLOCKS * NODES], BF16, c)
            adj = adj_t[:].rearrange("p (s l h) -> p s h l", s=BLOCKS, h=BLOCKS)
            load_all([(adj_t[:], adj_d)])
            w = sb("l3_w", [D, D], F32, c)
            vb = sb("l3_v", [LO, 3, D], F32, c)
            load_all([(w[:], a["L3_gnn_W"])] + [(vb[:, i, :], row(f"L3_gnn_{n}", D)) for i, n in enumerate(("b", "gamma", "beta"))])
            sc_out = sb("l3_out", [LO, BLOCKS], F32, c)
            sc_in = sb("l3_in", [LO, BLOCKS], F32, c)
            deg3 = deg_half[:].rearrange("p (b h) -> p b h", h=2)
            vector_steps(lambda v, link: (link(v.tensor_reduce(sc_out[:], deg3, AX.X, ALU.add)),
                                          link(v.tensor_scalar(sc_out[:], sc_out[:], 1.0, None, ALU.max)),
                                          link(v.tensor_scalar(sc_in[:], deg_in[:], 1.0, None, ALU.max))))
            inverse_root(c, "l3_root_out", sc_out[:])
            inverse_root(c, "l3_root_in", sc_in[:])
            h = sb("l3_h", [LO, BLOCKS, D], F32, c)
            y = sb("l3_y", [LO, BLOCKS, D], F32, c)
            vector_steps(lambda v, link: link(v.tensor_tensor(h[:], x[:], over_features(sc_out[:], D), ALU.mult)))
            with ExitStack() as c2:
                aggregate(c2, h[:], y[:])
            vector_steps(lambda v, link: link(v.tensor_tensor(y[:], y[:], over_features(sc_in[:], D), ALU.mult)))
            project([y[:]], D, [w[:]], h[:], D)
            vector_steps(lambda v, link: link(v.tensor_tensor(h[:], h[:], over_nodes(vb[:, 0, :], D), ALU.add)))
            batch_norm(h[:], D, vb[:, 1, :], vb[:, 2, :])
            vector_steps(lambda v, link: link(v.tensor_scalar(y[:], h[:], 0.0, None, ALU.min)))
            scalar_step(lambda: nc.scalar.activation(y[:], y[:], ACT.Exp))
            vector_steps(lambda v, link: (link(v.tensor_scalar(h[:], h[:], 0.0, -1.0, ALU.max, ALU.add)),
                                          link(v.tensor_tensor(h[:], h[:], y[:], ALU.add)),
                                          link(v.tensor_tensor(h[:], h[:], x[:], ALU.add))))
            layer_norm(h[:])
        store_all([(out.rearrange("(p b) f -> p (b f)", b=BLOCKS), x[:].rearrange("p b f -> p (b f)"))])


_OUTS = [((NODES, D), "float32")]


def kernel(**inputs):
    import concourse.bacc as _bacc
    from concourse.bass_utils import run_bass_kernel_spmd as _run

    nc = _bacc.Bacc("TRN2", target_bir_lowering=False, num_devices=1)
    arrays, aps = {}, {}
    for name, value in {**inputs, **constants()}.items():
        v = np.ascontiguousarray(value)
        arrays[f"in_{name}"] = v
        aps[name] = nc.dram_tensor(f"in_{name}", v.shape, mybir.dt.from_np(v.dtype), kind="ExternalInput").ap()
    out = nc.dram_tensor("out_0", (NODES, D), F32, kind="ExternalOutput").ap()
    gnn_stack(nc, aps, out)
    r = _run(nc, [arrays], core_ids=[0])
    return r.results[0]["out_0"]
```

```python
from contextlib import ExitStack

import numpy as np

import concourse.bass as bass
from concourse import mybir

F32 = mybir.dt.float32
BF16 = mybir.dt.bfloat16
I32 = mybir.dt.int32
I16 = mybir.dt.int16
U16 = mybir.dt.uint16
ALU = mybir.AluOpType
ACT = mybir.ActivationFunctionType
AX = mybir.AxisListType

P = 128
NODES = 3125
BLOCKS = 25
LO = NODES // BLOCKS
D = 64
EDGES = 100000
HALF = EDGES // 2
HP = P // 2
COLS = -(-HALF // HP)
LAST = HALF - (HP - 1) * COLS
BUCKETS = 2 * BLOCKS
TILES = HALF // P + HALF // P + BUCKETS + 2
GROUP = 4
GROUPS = TILES // GROUP
SLOTS = TILES * P
BANK = 512
BANKS = -(-NODES // BANK)
RELS = 100
CH = 104
NCH = TILES // CH
EPS = 1e-5
QUAD = 4
VR = 3
SHIFT = 8
SCATTER = 23
STEPS = COLS // (2 * SCATTER)
BLOCKS5 = 5
assert TILES % GROUP == 0 and TILES % CH == 0 and STEPS * 2 * SCATTER == COLS
assert HALF // P * 2 + 1 + BUCKETS <= TILES


def dft(d):
    n = np.arange(d)[:, None] * np.arange(d // 2)[None, :] * (2 * np.pi / d)
    re, im = np.cos(n), -np.sin(n)
    im0 = im.copy()
    im[:, 0] = np.cos(np.pi * np.arange(d))
    fwd = np.concatenate([re, im], 1)
    neg = -re
    neg[:, 0] = im[:, 0]
    rel = np.concatenate([re, im0, neg], 1)
    inv = np.concatenate([2 * re, 2 * im], 1) / d
    inv[:, 0] = 1.0 / d
    inv[:, d // 2] = im[:, 0] / d
    return fwd.astype(np.float32), rel.astype(np.float32), inv.astype(np.float32)


def constants():
    c = np.zeros((P, 3 * P + 8 + BLOCKS), np.float32)
    q = np.arange(P)
    c[:, 0:P] = np.eye(P)
    c[:, P:2 * P] = (q[:, None] < q[None, :]) & (q[:, None] // HP == q[None, :] // HP)
    c[:, 2 * P:3 * P] = q[None, :]
    c[:, 3 * P] = q < HP
    c[:, 3 * P + 1] = q >= HP
    c[:, 3 * P + 2] = q
    c[:, 3 * P + 3] = 1
    c[:, 3 * P + 8:] = np.arange(BLOCKS)
    out = {"const_small": c}
    for d in (64, 128):
        fwd, rel, inv = dft(d)
        out[f"const_dft{d}"] = np.concatenate([fwd, rel, inv], 1)
    return out


class Signal:

    def __init__(self, ctx, nc, name):
        self.sem = ctx.enter_context(nc.semaphore(name))
        self.base = 0


class Chain:

    def __init__(self, eng, signal):
        self.eng, self.of, self.n, self.turn = eng, signal, signal.base, 0

    def __call__(self, ins):
        self.n += 1
        ins.then_inc(self.of.sem, 1)
        self.eng.wait_ge(self.of.sem, self.n + self.turn)

    def looped(self, count, per):
        self.turn = 0
        self.n += (count - 1) * per

    def close(self):
        self.of.base = self.n


def gnn_stack(nc, a, out):
    ctx = ExitStack()
    with ctx:
        used = {}

        def sb(name, shape, dt, c=ctx):
            used[name] = used.get(name, 0) + 1
            if used[name] > 1:
                name = f"{name}_{used[name]}"
            return c.enter_context(nc.sbuf_tensor(name, shape, dt))

        def signal(name):
            return Signal(ctx, nc, name)

        psum = ctx.enter_context(nc.psum_tensor("psum", [P, 8 * BANK], F32))
        load = signal("load")
        store = signal("store")
        vec = signal("vec")
        act_step = signal("act_step")
        pe_step = signal("pe_step")
        pool_step = signal("pool_step")
        passed = signal("passed")

        rec_d = nc.dram_tensor("sorted_edges", [SLOTS + P, 4], F32, kind="Internal").ap()
        typ_d = nc.dram_tensor("sorted_types", [TILES + 2 * GROUP, P], BF16, kind="Internal").ap()
        adj_d = nc.dram_tensor("adj_saved", [LO, BLOCKS * NODES], BF16, kind="Internal").ap()
        left_d = nc.dram_tensor("adj_left", [LO, BLOCKS * NODES], BF16, kind="Internal").ap()
        quads_d = nc.dram_tensor("fours", [1, (TILES + QUAD) * 4], U16, kind="Internal").ap()
        bank_d = nc.dram_tensor("tile_banks", [2, TILES], F32, kind="Internal").ap()
        x_d = nc.dram_tensor("x_saved", [LO, BLOCKS * D], F32, kind="Internal").ap()
        table_d = {d: nc.dram_tensor(f"gather_table{d}", [2 * NODES, d], F32, kind="Internal").ap()
                   for d in (64, 128)}
        loop_d = {d: nc.dram_tensor(f"loop_term{d}", [LO, BLOCKS * d], F32, kind="Internal").ap()
                  for d in (64, 128)}

        cst = sb("cst", [P, 3 * P + 8 + BLOCKS], F32)
        ident, before = cst[:, 0:P], cst[:, P:2 * P]
        iota = cst[:, 2 * P:3 * P]
        in_half = [cst[:, 3 * P + h:3 * P + h + 1] for h in range(2)]
        part = cst[:, 3 * P + 2:3 * P + 3]
        kvals = cst[:, 3 * P + 8:]
        lo_s = sb("lo_s", [P, TILES + GROUP], F32)
        gidx_s = sb("gidx_s", [P, TILES + 2 * GROUP], I32)
        bucket_r = sb("bucket_r", [1, GROUP + TILES], I16)
        deg_half = sb("deg_half", [LO, BUCKETS], F32)
        deg_in = sb("deg_in", [LO, BLOCKS], F32)
        ones_f = sb("ones_f", [P, P], F32)
        one_col = cst[:, 3 * P + 3:3 * P + 4]
        ones_b = sb("ones_b", [P, 1], BF16)
        first_tile_i = sb("first_tile_i", [1, BUCKETS + 2], I32)
        first_tile_f = sb("first_tile_f", [P, BLOCKS], F32)
        extra_i = sb("extra_i", [1, 1], I32)
        start_col = sb("start_col", [P, 1], F32)
        x_room = sb("x", [P, max(BLOCKS * D, 2 * (TILES + QUAD))], F32)
        x = x_room[0:LO, 0:BLOCKS * D].rearrange("p (s d) -> p s d", s=BLOCKS)
        dinv = sb("dinv", [LO, BLOCKS], F32)
        dinv_half = sb("dinv_half", [LO, BLOCKS, 2], F32)
        rel = sb("rel", [RELS, D], F32)
        rel2 = sb("rel2", [RELS, 2 * D], F32)

        sort = ExitStack()
        with sort:
            src_i = sb("src_i", [P, COLS], I32, sort)
            dst_i = sb("dst_i", [P, COLS], I32, sort)
            typ_i = sb("typ_i", [P, COLS], I32, sort)
            src_f = sb("src_f", [P, COLS], F32, sort)
            key = sb("key", [P, COLS], F32, sort)
            tmp = sb("tmp", [P, COLS], F32, sort)
            run = sb("run", [P, COLS], F32, sort)
            rank = sb("rank", [P, COLS], F32, sort)
            mask = sb("mask", [P, COLS], F32, sort)
            rec = sb("rec", [P, COLS, 4], F32, sort)
            row_i = sb("row_i", [P, COLS], I32, sort)
            cnt = sb("cnt", [P, BLOCKS], F32, sort)
            tot = sb("tot", [P, BLOCKS, 2], F32, sort)
            tot_i = sb("tot_i", [P, BLOCKS, 2], I32, sort)
            nt = sb("nt", [P, BLOCKS, 2], F32, sort)
            incl = sb("incl", [P, BLOCKS, 2], F32, sort)
            base = sb("base", [P, BLOCKS], F32, sort)
            base2 = sb("base2", [P, BLOCKS], F32, sort)
            empty = sb("empty", [P, TILES, 4], F32, sort)
            dst_lo = sb("dst_lo", [P, COLS], F32, sort)
            dst_block = sb("dst_block", [P, COLS], F32, sort)
            zero_b = sb("zero_b", [P, P], BF16, sort)
            oh_slo = [sb(f"oh_slo{h}", [P, SCATTER, LO], BF16, sort) for h in range(2)]
            oh_sbk = [sb(f"oh_sbk{h}", [P, SCATTER, BUCKETS], BF16, sort) for h in range(2)]
            oh_dlo = [sb(f"oh_dlo{h}", [P, SCATTER, LO], BF16, sort) for h in range(2)]
            oh_dbk = [sb(f"oh_dbk{h}", [P, SCATTER, BLOCKS], BF16, sort) for h in range(2)]
            deg_made, deg_used = signal("deg_made"), signal("deg_used")
            st_rec = [sb(f"st_rec{h}", [P, SCATTER, 4], F32, sort) for h in range(2)]
            st_row = [sb(f"st_row{h}", [P, SCATTER], I32, sort) for h in range(2)]
            st_made, st_sent = signal("staged"), [signal(f"sent{h}") for h in range(2)]

            with nc.Block() as block:
                @block.vector
                def _(dve):
                    link = Chain(dve, vec)
                    for t, v in ((src_i, -1), (dst_i, -1), (typ_i, 0)):
                        link(nc.vector.memset(t[:], v))
                    link(nc.vector.memset(empty[:, :, 0], -1.0))
                    link(nc.vector.memset(empty[:, :, 1], 0.0))
                    link(nc.vector.memset(empty[:, :, 2], float(P - 1)))
                    link(nc.vector.memset(empty[:, :, 3], 0.0))
                    link(nc.vector.memset(rank[:], 0.0))
                    link(nc.vector.memset(zero_b[:], 0.0))
                    link(nc.vector.memset(ones_f[:], 1.0))
                    link(nc.vector.memset(ones_b[:], 1.0))
                    link.close()

            with nc.Block() as block:
                @block.sync
                def _(sp):
                    sp.dma_start(cst[:], a["const_small"]).then_inc(load.sem, 16)
                    n = 1
                    for t, name in ((src_i, "src"), (dst_i, "dst"), (typ_i, "edge_type_100")):
                        for h in range(2):
                            at = a[name][h * HALF:(h + 1) * HALF]
                            full = at[0:(HP - 1) * COLS].rearrange("(p c) -> p c", c=COLS)
                            rest = at[(HP - 1) * COLS:HALF].rearrange("(p c) -> p c", p=1)
                            sp.dma_start(t[h * HP:h * HP + HP - 1, :], full).then_inc(load.sem, 16)
                            sp.dma_start(t[h * HP + HP - 1:h * HP + HP, 0:LAST], rest).then_inc(load.sem, 16)
                            n += 2
                    sp.dma_start(rec_d[0:SLOTS, :].rearrange("(p t) w -> p (t w)", p=P),
                                 empty[:].rearrange("p t w -> p (t w)")).then_inc(store.sem, 16)
                    sp.wait_ge(load.sem, load.base + 16 * n)
                    sp.wait_ge(store.sem, store.base + 16)
                    load.base += 16 * n
                    store.base += 16

            with nc.Block() as block:
                @block.vector
                def _(dve):
                    link = Chain(dve, vec)
                    v = nc.vector
                    def divide(n, lo, block):
                        link(v.tensor_scalar(row_i[:], n, 1.0 / BLOCKS, 0.02, ALU.mult, ALU.add))
                        link(v.tensor_copy(tmp[:], row_i[:]))
                        link(v.scalar_tensor_tensor(key[:], tmp[:], -float(BLOCKS), n, ALU.mult, ALU.add))
                        link(v.tensor_scalar(mask[:], key[:], 0.0, None, ALU.is_lt))
                        link(v.tensor_tensor(lo, tmp[:], mask[:], ALU.subtract))
                        link(v.scalar_tensor_tensor(block, mask[:], float(BLOCKS), key[:], ALU.mult, ALU.add))
                    link(v.tensor_copy(src_f[:], dst_i[:]))
                    divide(src_f[:], dst_lo[:], dst_block[:])
                    link(v.tensor_copy(src_f[:], src_i[:]))
                    divide(src_f[:], rec[:, :, 0], run[:])
                    link(v.tensor_scalar(mask[:], src_f[:], 0.0, None, ALU.is_lt))
                    link(v.scalar_tensor_tensor(key[:], mask[:], 100.0, run[:], ALU.mult, ALU.add))
                    link(v.tensor_copy(tmp[:], dst_i[:]))
                    link(v.tensor_scalar(run[:], tmp[:], 1.0, None, ALU.mult))
                    link(v.tensor_scalar(base[:, 0:1], in_half[1], float(NODES), None, ALU.mult))
                    link(v.tensor_scalar(rec[:, :, 1], run[:], base[:, 0:1], None, ALU.add))
                    link(v.tensor_copy(rec[:, :, 2], typ_i[:]))
                    link(v.tensor_scalar(rec[:, :, 3], key[:], 2.0, in_half[1], ALU.mult, ALU.add))
                    with dve.Fori(0, BLOCKS) as k:
                        link.turn = k * 5
                        kv = kvals[:, bass.ds(k, 1)]
                        link(v.tensor_scalar(mask[:], key[:], kv, None, ALU.is_equal))
                        link(v.tensor_tensor_scan(run[:], mask[:], src_f[:], 0.0, ALU.add, ALU.bypass))
                        link(v.tensor_copy(cnt[:, bass.ds(k, 1)], run[:, COLS - 1:COLS]))
                        link(v.tensor_tensor(tmp[:], run[:], mask[:], ALU.mult))
                        link(v.tensor_tensor(rank[:], rank[:], tmp[:], ALU.add))
                    link.looped(BLOCKS, 5)
                    link.close()

            with nc.Block() as block:
                @block.tensor
                def _(pe):
                    nc.tensor.matmul(psum[:, 0:BLOCKS], before, cnt[:], start=True, stop=True)
                    for h in range(2):
                        last = nc.tensor.matmul(psum[:, BANK * (h + 1):BANK * (h + 1) + BLOCKS],
                                                in_half[h].to_broadcast([P, P]), cnt[:],
                                                start=True, stop=True)
                    last.then_inc(pe_step.sem, 1)

                @block.vector
                def _(dve):
                    link = Chain(dve, vec)
                    v = nc.vector
                    dve.wait_ge(pe_step.sem, pe_step.base + 1)
                    pe_step.base += 1
                    for h in range(2):
                        link(v.tensor_scalar(tot[:, :, h], psum[:, BANK * (h + 1):BANK * (h + 1) + BLOCKS],
                                             float(P - 1), None, ALU.add))
                    link(v.tensor_copy(tot_i[:], tot[:]))
                    link(v.tensor_scalar(tot_i[:], tot_i[:], 7, None, ALU.arith_shift_right))
                    link(v.tensor_copy(nt[:], tot_i[:]))
                    link(v.tensor_scalar(nt[:], nt[:], 1.0, None, ALU.max))
                    flat = nt[:].rearrange("p k h -> p (k h)")
                    link(v.tensor_tensor_scan(incl[:].rearrange("p k h -> p (k h)"), flat, flat,
                                              0.0, ALU.add, ALU.bypass))
                    link(v.tensor_tensor(incl[:], incl[:], nt[:], ALU.subtract))
                    link(v.tensor_copy(first_tile_f[:], incl[:, :, 0]))
                    link(v.memset(first_tile_i[:], TILES))
                    link(v.tensor_copy(first_tile_i[:, 0:BUCKETS],
                                       incl[0:1].rearrange("p k h -> p (k h)")))
                    link(v.tensor_scalar(base[:], incl[:, :, 0], in_half[0], float(P), ALU.mult, ALU.mult))
                    link(v.tensor_scalar(base2[:], incl[:, :, 1], in_half[1], float(P), ALU.mult, ALU.mult))
                    link(v.tensor_tensor(base[:], base[:], base2[:], ALU.add))
                    link(v.tensor_tensor(base[:], base[:], psum[:, 0:BLOCKS], ALU.add))
                    link(v.tensor_scalar(base[:], base[:], -1.0, None, ALU.add))
                    with dve.Fori(0, BLOCKS) as k:
                        link.turn = k * 2
                        link(v.tensor_scalar(tmp[:], key[:], kvals[:, bass.ds(k, 1)], base[:, bass.ds(k, 1)],
                                             ALU.is_equal, ALU.mult))
                        link(v.tensor_tensor(rank[:], rank[:], tmp[:], ALU.add))
                    link.looped(BLOCKS, 2)
                    link(v.tensor_copy(row_i[:], rank[:]))
                    link(v.tensor_scalar(row_i[:], row_i[:], 7, None, ALU.arith_shift_right))
                    link(v.tensor_copy(tmp[:], row_i[:]))
                    link(v.tensor_copy(row_i[:], rank[:]))
                    link(v.tensor_scalar(row_i[:], row_i[:], P - 1, None, ALU.bitwise_and))
                    link(v.tensor_copy(run[:], row_i[:]))
                    link(v.scalar_tensor_tensor(tmp[:], run[:], float(TILES), tmp[:], ALU.mult, ALU.add))
                    link(v.tensor_scalar(mask[:], src_f[:], 0.0, None, ALU.is_lt))
                    link(v.tensor_tensor_scan(run[:], mask[:], mask[:], 0.0, ALU.add, ALU.bypass))
                    link(v.tensor_scalar(base2[:, 0:1], in_half[1], float(HP), float(SLOTS - 1), ALU.mult, ALU.add))
                    link(v.scalar_tensor_tensor(mask[:], run[:], base2[:, 0:1], mask[:], ALU.add, ALU.mult))
                    link(v.tensor_scalar(run[:], src_f[:], 0.0, None, ALU.is_ge))
                    link(v.tensor_tensor(tmp[:], tmp[:], run[:], ALU.mult))
                    link(v.tensor_tensor(row_i[:], tmp[:], mask[:], ALU.add))
                    link.close()

            with nc.Block() as block:
                @block.vector
                def _(dve):
                    def stage(h, first):
                        at = bass.ds(first + h * SCATTER, SCATTER)
                        nc.vector.tensor_copy(st_row[h][:], row_i[:, at]).then_inc(st_made.sem, 1)
                        nc.vector.tensor_copy(st_rec[h][:], rec[:, at, :]).then_inc(st_made.sem, 1)

                    def one_hots(h, first, n):
                        dve.wait_ge(deg_used.sem, n)
                        at = bass.ds(first + h * SCATTER, SCATTER)
                        for to, of, size in ((oh_slo, rec[:, at, 0:1], LO), (oh_sbk, rec[:, at, 3:4], BUCKETS),
                                             (oh_dlo, dst_lo[:, at].rearrange("p (g a) -> p g a", a=1), LO),
                                             (oh_dbk, dst_block[:, at].rearrange("p (g a) -> p g a", a=1), BLOCKS)):
                            ins = nc.vector.tensor_tensor(
                                to[h][:], iota[:, 0:size].rearrange("p (a l) -> p a l", a=1).to_broadcast([P, SCATTER, size]),
                                of.to_broadcast([P, SCATTER, size]), ALU.is_equal)
                        ins.then_inc(deg_made.sem, 1)
                    dve.sem_inc(deg_used.sem, 2)
                    for h in range(2):
                        stage(h, 0)
                    for h in range(2):
                        one_hots(h, 0, h + 1)
                    with dve.Fori(1, STEPS) as k:
                        for h in range(2):
                            dve.wait_ge(st_sent[h].sem, k * (16 * SCATTER))
                            stage(h, k * (2 * SCATTER))
                            one_hots(h, k * (2 * SCATTER), k * 2 + (h + 1))
                    dve.wait_ge(deg_used.sem, 2 * STEPS + 2)
                    nc.vector.tensor_copy(deg_half[:], psum[0:LO, 0:BUCKETS]).then_inc(deg_made.sem, 1)
                    nc.vector.tensor_copy(deg_in[:], psum[0:LO, BANK:BANK + BLOCKS]).then_inc(deg_made.sem, 1)
                    dve.wait_ge(deg_made.sem, 2 * STEPS + 2)

                @block.tensor
                def _(pe):
                    for bank, size in ((0, BUCKETS), (1, BLOCKS)):
                        nc.tensor.matmul(psum[0:LO, bank * BANK:bank * BANK + size], zero_b[:, 0:LO], zero_b[:, 0:size],
                                         start=True, stop=False, skip_group_check=True)
                    with pe.Fori(0, STEPS) as k:
                        for h in range(2):
                            pe.wait_ge(deg_made.sem, k * 2 + (h + 1))
                            for c in range(SCATTER):
                                nc.tensor.matmul(psum[0:LO, 0:BUCKETS], oh_slo[h][:, c, :], oh_sbk[h][:, c, :],
                                                 start=False, stop=False, skip_group_check=True)
                                mm = nc.tensor.matmul(psum[0:LO, BANK:BANK + BLOCKS], oh_dlo[h][:, c, :], oh_dbk[h][:, c, :],
                                                      start=False, stop=False, skip_group_check=True)
                            mm.then_inc(deg_used.sem, 1)

                @block.gpsimd
                def _(pool):
                    with pool.Fori(0, STEPS) as k:
                        for h in range(2):
                            pool.wait_ge(st_made.sem, k * 4 + 2 * h + 2)
                            pool.sem_inc(passed.sem)
                            for c in range(SCATTER):
                                nc.gpsimd.indirect_dma_start(
                                    rec_d, bass.IndirectOffsetOnAxis(ap=st_row[h][:, c:c + 1], axis=0),
                                    st_rec[h][:, c, :], None).then_inc(st_sent[h].sem, 16)
                    for h in range(2):
                        pool.wait_ge(st_sent[h].sem, 16 * SCATTER * STEPS)

        adj_stack = ExitStack()
        ROW = TILES + QUAD
        dst_s = x_room[:, 0:ROW]
        key_s = x_room[:, ROW:2 * ROW]
        with ExitStack() as t1:
            rec_s = sb("rec_s", [P, TILES, 4], F32, t1)
            m1 = sb("m1", [P, TILES], F32, t1)
            m2 = sb("m2", [P, TILES], F32, t1)
            typ_t = sb("typ_t", [CH, NCH, P], BF16, t1)
            none_b = sb("none_b", [2 * GROUP, P], BF16, t1)
            out_deg = sb("out_deg", [LO, BLOCKS], F32, t1)
            most = sb("most", [LO, 1], F32, t1)
            extra = sb("extra", [1, 1], F32, t1)
            lohi = sb("lohi", [CH, 2, NCH], F32, t1)
            lohi_i = sb("lohi_i", [CH, 2, NCH], I32, t1)
            with nc.Block() as block:
                @block.sync
                def _(sp):
                    sp.dma_start(rec_s[:].rearrange("p t w -> p (t w)"),
                                 rec_d[0:SLOTS, :].rearrange("(p t) w -> p (t w)", p=P)).then_inc(load.sem, 16)
                    sp.wait_ge(load.sem, load.base + 16)
                    load.base += 16

            with nc.Block() as block:
                @block.vector
                def _(dve):
                    link = Chain(dve, vec)
                    v = nc.vector
                    link(v.memset(none_b[:], float(P - 1)))
                    link(v.memset(lo_s[:], -1.0))
                    link(v.tensor_copy(lo_s[:, 0:TILES], rec_s[:, :, 0]))
                    link(v.memset(gidx_s[:], 0))
                    link(v.tensor_copy(gidx_s[:, 0:TILES], rec_s[:, :, 1]))
                    link(v.memset(bucket_r[:], 0))
                    link(v.tensor_copy(bucket_r[:, GROUP:], rec_s[0:1, :, 3]))
                    link(v.tensor_scalar(m1[:], rec_s[:, :, 1], float(NODES), None, ALU.is_ge))
                    link(v.memset(dst_s[:], -1.0))
                    link(v.scalar_tensor_tensor(dst_s[:, 0:TILES], m1[:], -float(NODES), rec_s[:, :, 1], ALU.mult, ALU.add))
                    link(v.tensor_tensor(m1[:], rec_s[:, :, 3], m1[:], ALU.subtract))
                    link(v.memset(key_s[:], -1.0))
                    link(v.scalar_tensor_tensor(key_s[:, 0:TILES], m1[:], LO / 2.0, lo_s[:, 0:TILES], ALU.mult, ALU.add))
                    link(v.tensor_scalar(m1[:], lo_s[:, 0:TILES], 0.0, None, ALU.is_lt))
                    link(v.scalar_tensor_tensor(m2[:], m1[:], -9999.0, dst_s[:, 0:TILES], ALU.mult, ALU.add))
                    link(v.scalar_tensor_tensor(m1[:], m1[:], 9999.0, dst_s[:, 0:TILES], ALU.mult, ALU.add))
                    link(v.tensor_reduce(out_deg[:], deg_half[:].rearrange("p (b h) -> p b h", h=2), AX.X, ALU.add))
                    link(v.tensor_reduce(most[:], out_deg[:], AX.X, ALU.max))
                    link(v.tensor_tensor(first_tile_f[:], first_tile_f[:], ident[:, 0:BLOCKS], ALU.mult))
                    link(v.tensor_reduce(start_col[:], first_tile_f[:], AX.X, ALU.add))
                    link.close()

            with nc.Block() as block:
                @block.tensor
                def _(pe):
                    nc.tensor.matmul(psum[0:1, 6 * BANK:6 * BANK + LO], most[:], ident[0:LO, 0:LO],
                                     start=True, stop=True).then_inc(pe_step.sem, 1)
                    for c in range(NCH):
                        if c > 1:
                            pe.wait_ge(vec.sem, vec.base + 3 * (c - 1))
                        for i, of in enumerate((rec_s[:, c * CH:(c + 1) * CH, 2], m1[:, c * CH:(c + 1) * CH],
                                                m2[:, c * CH:(c + 1) * CH])):
                            nc.tensor.transpose(psum[0:CH, (3 * (c % 2) + i) * BANK:(3 * (c % 2) + i) * BANK + P], of,
                                                ident).then_inc(pe_step.sem, 1)

                @block.vector
                def _(dve):
                    v = nc.vector
                    for c in range(NCH):
                        at = [psum[0:CH, (3 * (c % 2) + i) * BANK:(3 * (c % 2) + i) * BANK + P] for i in range(3)]
                        dve.wait_ge(pe_step.sem, pe_step.base + 3 * c + 4)
                        v.tensor_copy(typ_t[:, c, :], at[0]).then_inc(vec.sem, 1)
                        v.tensor_reduce(lohi[:, 0, c:c + 1], at[1], AX.X, ALU.min).then_inc(vec.sem, 1)
                        v.tensor_reduce(lohi[:, 1, c:c + 1], at[2], AX.X, ALU.max).then_inc(vec.sem, 1)
                    vec.base += 3 * NCH
                    dve.wait_ge(vec.sem, vec.base)
                    link = Chain(dve, vec)
                    link(v.tensor_reduce(extra[:], psum[0:1, 6 * BANK:6 * BANK + LO], AX.X, ALU.max))
                    link(v.tensor_scalar(extra[:], extra[:], 256.0, None, ALU.is_gt))
                    link(v.tensor_copy(extra_i[:], extra[:]))
                    link(v.tensor_scalar(lohi[:, 1, :], lohi[:, 1, :], 0.0, None, ALU.max))
                    link(v.tensor_tensor(lohi[:, 0, :], lohi[:, 0, :], lohi[:, 1, :], ALU.min))
                    link(v.tensor_copy(lohi_i[:], lohi[:]))
                    link(v.tensor_scalar(lohi_i[:], lohi_i[:], 9, None, ALU.arith_shift_right))
                    link(v.tensor_copy(lohi[:], lohi_i[:]))
                    link.close()

                @block.sync
                def _(sp):
                    sp.wait_ge(vec.sem, vec.base)
                    sp.dma_start(typ_d[0:TILES, :].rearrange("(c t) p -> t c p", t=CH),
                                 typ_t[:]).then_inc(store.sem, 16)
                    sp.dma_start(typ_d[TILES:TILES + 2 * GROUP, :], none_b[:]).then_inc(store.sem, 16)
                    for i in range(2):
                        sp.dma_start(bank_d[i, :].rearrange("(c t) -> t c", t=CH),
                                     lohi[:, i, :], allow_slow_non_contiguous=True).then_inc(store.sem, 16)
                    sp.wait_ge(store.sem, store.base + 64)
                    store.base += 64
            pe_step.base += 3 * NCH + 1

        with ExitStack() as t1:
            def row_of(name, dt=F32):
                return sb(name, [1, ROW], dt, t1)
            quads = sb("quads", [1, ROW, 4], U16, t1)
            tiles_i = sb("tiles_i", [P, TILES], I32, t1)
            starts = sb("starts", [P, TILES], F32, t1)
            first, last, same, nth, nth_i, blocked, lead, q_first, q_end, t_a = (
                row_of(n, I32 if n == "nth_i" else F32) for n in
                ("first", "last", "same", "nth", "nth_i", "blocked", "lead", "q_first", "q_end", "t_a"))
            with nc.Block() as block:
                @block.gpsimd
                def _(pool):
                    nc.gpsimd.iota(tiles_i[:], pattern=[[1, TILES]], base=0,
                                   channel_multiplier=0).then_inc(pool_step.sem, 1)

                @block.sync
                def _(sp):
                    sp.wait_ge(vec.sem, vec.base + 2)
                    for i, to in enumerate((first, last)):
                        sp.dma_start(to[:, 0:TILES], bank_d[i:i + 1, :]).then_inc(load.sem, 16)

                @block.tensor
                def _(pe):
                    pe.wait_ge(vec.sem, vec.base + 4)
                    for i, (a0, a1) in enumerate(((0, BANK), (BANK, TILES))):
                        nc.tensor.matmul(psum[0:1, a0:a1], ones_f[0:BLOCKS, 0:1], starts[0:BLOCKS, a0:a1],
                                         start=True, stop=True).then_inc(pe_step.sem, 1)

                @block.vector
                def _(dve):
                    link = Chain(dve, vec)
                    v = nc.vector
                    link(v.memset(first[:], 99.0))
                    link(v.memset(last[:], -99.0))
                    link(v.memset(same[:], 0.0))
                    dve.wait_ge(pool_step.sem, pool_step.base + 1)
                    link(v.tensor_scalar(starts[:], tiles_i[:], start_col[:], None, ALU.is_equal))
                    dve.wait_ge(pe_step.sem, pe_step.base + 2)
                    link(v.tensor_scalar(same[:, 0:TILES], psum[0:1, 0:TILES], -1.0, 1.0, ALU.mult, ALU.add))
                    link(v.tensor_tensor_scan(nth[:], same[:], same[:], 0.0, ALU.mult, ALU.add))
                    link(v.tensor_copy(nth_i[:], nth[:]))
                    link(v.tensor_scalar(nth_i[:], nth_i[:], QUAD - 1, None, ALU.bitwise_and))
                    link(v.tensor_scalar(lead[:], nth_i[:], 0.0, None, ALU.is_equal))
                    link(v.memset(lead[:, TILES:], 0.0))
                    dve.wait_ge(load.sem, load.base + 32)
                    link(v.tensor_copy(q_first[:], first[:]))
                    link(v.tensor_copy(q_end[:], last[:]))
                    for k in range(1, QUAD):
                        n = ROW - k
                        link(v.tensor_scalar(blocked[:, 0:n], nth[:, k:], float(k), 99.0, ALU.is_lt, ALU.mult))
                        link(v.tensor_tensor(t_a[:, 0:n], first[:, k:], blocked[:, 0:n], ALU.add))
                        link(v.tensor_tensor(q_first[:, 0:n], q_first[:, 0:n], t_a[:, 0:n], ALU.min))
                        link(v.tensor_tensor(t_a[:, 0:n], last[:, k:], blocked[:, 0:n], ALU.subtract))
                        link(v.tensor_tensor(q_end[:, 0:n], q_end[:, 0:n], t_a[:, 0:n], ALU.max))
                    link(v.tensor_scalar(q_first[:], q_first[:], float(BANKS - 1), None, ALU.min))
                    link(v.tensor_scalar(q_end[:], q_end[:], 0.0, 1.0, ALU.max, ALU.add))
                    link(v.tensor_copy(quads[:, :, 0], q_first[:]))
                    link(v.tensor_copy(quads[:, :, 1], q_end[:]))
                    link(v.tensor_tensor(t_a[:], q_end[:], q_first[:], ALU.subtract))
                    link(v.tensor_tensor(t_a[:], t_a[:], lead[:], ALU.mult))
                    link(v.tensor_tensor_scan(nth[:], t_a[:], t_a[:], 0.0, ALU.add, ALU.bypass))
                    link(v.tensor_tensor(nth[:], nth[:], t_a[:], ALU.subtract))
                    link(v.tensor_tensor(nth[:], nth[:], q_first[:], ALU.subtract))
                    link(v.tensor_scalar(quads[:, :, 2], nth[:], float(SHIFT), None, ALU.add))
                    link(v.tensor_tensor_scan(nth[:], lead[:], lead[:], 0.0, ALU.add, ALU.bypass))
                    link(v.tensor_tensor(quads[:, :, 3], nth[:], lead[:], ALU.subtract))
                    link.close()
            pool_step.base += 1
            load.base += 32
            pe_step.base += 2

            with nc.Block() as block:
                @block.sync
                def _(sp):
                    sp.dma_start(quads_d, quads[:].rearrange("p t w -> p (t w)")).then_inc(store.sem, 16)
                    sp.wait_ge(store.sem, store.base + 16)
            store.base += 16

        adj_t = sb("adj", [LO, BLOCKS * NODES], BF16, adj_stack)
        with ExitStack() as t2:
            quads = sb("quads", [1, ROW, 4], U16, t2)
            iota16 = sb("iota16", [P, BANKS * BANK], I16, t2)
            oh_dst = sb("oh_dst", [P, VR * QUAD * BANK], BF16, t2)
            oh_src = sb("oh_src", [P, VR * QUAD, LO], BF16, t2)
            sq_src = sb("sq_src", [P, QUAD, LO], BF16, t2)
            left = sb("left", [LO, NODES], BF16, t2)
            zeros = sb("zeros", [P, LO], BF16, t2)
            with nc.Block() as block:
                @block.gpsimd
                def _(pool):
                    nc.gpsimd.iota(iota16[:], pattern=[[1, BANKS * BANK]], base=0,
                                   channel_multiplier=0).then_inc(pool_step.sem, 1)
                    pool.wait_ge(pool_step.sem, pool_step.base + 1)

                @block.vector
                def _(dve):
                    link = Chain(dve, vec)
                    link(nc.vector.memset(zeros[:], 0.0))
                    link.close()

                @block.sync
                def _(sp):
                    sp.dma_start(quads[:].rearrange("p t w -> p (t w)"), quads_d).then_inc(load.sem, 16)
                    sp.wait_ge(load.sem, load.base + 16)
            pool_step.base += 1
            load.base += 16

            def block_tiles(eng, b):
                return [eng.value_load(first_tile_i[0:1, bass.ds(b * 2 + e, 1)], min_val=0, max_val=TILES)
                        for e in (0, 2)]

            def four(eng, regs, t):
                eng.load(regs, quads[0:1, bass.ds(t, 1), :].rearrange("p a w -> p (a w)"))
                return [eng.snap(r, min_val=lo, max_val=hi) for r, lo, hi in
                        zip(regs, (0, 1, 0, 0), (BANKS - 1, BANKS, BANKS * TILES, TILES))]

            def build(left_over):
                tag = "left" if left_over else "count"
                src_made, dst_made, dst_used = signal(f"{tag}_src_made"), signal(f"{tag}_dst_made"), signal(f"{tag}_dst_used")
                src_squared = signal(f"{tag}_src_squared")
                banks_free, kept = signal(f"{tag}_banks_free"), signal(f"{tag}_kept")

                def if_wanted(eng, part):
                    if not left_over:
                        part(eng)
                    else:
                        with eng.If(eng.value_load(extra_i[0:1, 0:1], min_val=0, max_val=1) != 0):
                            part(eng)
                        eng.sem_inc(passed.sem)

                def dve_part(dve):
                    regs = [dve.alloc_register(f"{tag}_four_v{i}") for i in range(4)]
                    with dve.Fori(0, BLOCKS) as b:
                        t0, t1_ = block_tiles(dve, b)
                        with dve.Fori(t0, t1_, QUAD) as t:
                            first_bank, end_bank, visits, _ = four(dve, regs, t)
                            with dve.Fori(first_bank, end_bank) as bank:
                                v = dve.snap(visits + bank, min_val=0, max_val=BANKS * TILES)
                                dve.wait_ge(dst_used.sem, v + 1)
                                for k in range(QUAD):
                                    ins = nc.vector.tensor_scalar(
                                        oh_dst[:, bass.ds((v % VR) * (QUAD * BANK) + k * BANK, BANK)],
                                        iota16[:, bass.ds(bank * BANK, BANK)], dst_s[:, bass.ds(t + k, 1)],
                                        None, ALU.is_equal)
                                ins.then_inc(dst_made.sem, 1)
                        if left_over:
                            first_bank, _, visits, _ = four(dve, regs, t1_)
                            dve.wait_ge(dst_used.sem, visits + first_bank + VR)
                            dve.wait_ge(kept.sem, b * 16 + 16)
                            dve.sem_inc(passed.sem)
                            for bank in range(BANKS):
                                w = min(BANK, NODES - bank * BANK)
                                nc.vector.tensor_tensor(
                                    left[:, bank * BANK:bank * BANK + w], psum[0:LO, bank * BANK:bank * BANK + w],
                                    adj_t[:, bass.ds(b * NODES + bank * BANK, w)], ALU.subtract).then_inc(banks_free.sem, 1)

                def pe_part(pe):
                    regs = [pe.alloc_register(f"{tag}_four_p{i}") for i in range(4)]
                    pe.sem_inc(dst_made.sem, SHIFT)
                    pe.sem_inc(dst_used.sem, SHIFT + VR)
                    with pe.Fori(0, BLOCKS) as b:
                        t0, t1_ = block_tiles(pe, b)
                        for bank in range(BANKS):
                            pe.wait_ge(banks_free.sem, b * BANKS + bank + 1)
                            nc.tensor.matmul(psum[0:LO, bank * BANK:(bank + 1) * BANK], zeros[:], zeros[:, 0:1].to_broadcast([P, BANK]),
                                             start=True, stop=False, skip_group_check=True)
                        with pe.Fori(t0, t1_, QUAD) as t:
                            first_bank, end_bank, visits, number = four(pe, regs, t)
                            pe.wait_ge(src_made.sem, number + 2)
                            pe.sem_inc(passed.sem)
                            with pe.Fori(first_bank, end_bank) as bank:
                                v = pe.snap(visits + bank, min_val=0, max_val=BANKS * TILES)
                                pe.wait_ge(dst_made.sem, v + 1)
                                for k in range(QUAD):
                                    mm = nc.tensor.matmul(
                                        psum[0:LO, bass.ds(bank * BANK, BANK)],
                                        oh_src[:, bass.ds((number % VR) * QUAD + k, 1), :].rearrange("p a l -> p (a l)"),
                                        oh_dst[:, bass.ds((v % VR) * (QUAD * BANK) + k * BANK, BANK)],
                                        start=False, stop=False, skip_group_check=True)
                                mm.then_inc(dst_used.sem, 1)

                def act_part(act):
                    act.sem_inc(banks_free.sem, BANKS)
                    act.sem_inc(kept.sem, 16)
                    act.sem_inc(src_made.sem)
                    regs = [[act.alloc_register(f"{tag}_four_a{n}_{i}") for i in range(4)] for n in range(3)]

                    def src_one_hots(regs, t, b):
                        first_bank, _, visits, number = four(act, regs, t)
                        act.wait_ge(dst_used.sem, visits + first_bank + 1)
                        act.wait_ge(src_made.sem, number + 1)
                        for k in range(QUAD):
                            sq = nc.scalar.activation(sq_src[:, k, :], iota16[:, bass.ds(b * LO, LO)], ACT.Square,
                                                      bias=key_s[:, bass.ds(t + k, 1)], scale=-1.0)
                        sq.then_inc(src_squared.sem, 1)
                        act.wait_ge(src_squared.sem, number + 1)
                        nc.scalar.activation(oh_src[:, bass.ds((number % VR) * QUAD, QUAD), :], sq_src[:], ACT.Relu,
                                             bias=one_col, scale=-2.0).then_inc(src_made.sem, 1)
                        return visits + first_bank
                    src_one_hots(regs[0], 0, 0)
                    with act.Fori(0, BLOCKS) as b:
                        t0, t1_ = block_tiles(act, b)
                        with act.If(t0 + QUAD < t1_):
                            with act.Fori(t0 + QUAD, t1_, QUAD) as t:
                                src_one_hots(regs[1], t, b)
                        act.sem_inc(passed.sem)
                        visits = src_one_hots(regs[2], t1_, b + 1)
                        if not left_over:
                            act.wait_ge(dst_used.sem, visits + VR)
                            for bank in range(BANKS):
                                w = min(BANK, NODES - bank * BANK)
                                nc.scalar.copy(adj_t[:, bass.ds(b * NODES + bank * BANK, w)],
                                               psum[0:LO, bank * BANK:bank * BANK + w]).then_inc(banks_free.sem, 1)
                    if not left_over:
                        act.wait_ge(banks_free.sem, BANKS * (BLOCKS + 1))

                def sp_part(sp):
                    with sp.Fori(0, BLOCKS) as b:
                        sp.wait_ge(banks_free.sem, b * BANKS + 2 * BANKS)
                        sp.dma_start((left_d if left_over else adj_d)[:, bass.ds(b * NODES, NODES)],
                                     left[:] if left_over else adj_t[:, bass.ds(b * NODES, NODES)]).then_inc(kept.sem, 16)
                        if left_over:
                            sp.wait_ge(kept.sem, b * 16 + 32)
                            sp.sem_inc(passed.sem)
                    if not left_over:
                        sp.wait_ge(kept.sem, 16 * BLOCKS + 16)

                with nc.Block() as block:
                    @block.scalar
                    def _(act):
                        if_wanted(act, act_part)

                    @block.vector
                    def _(dve):
                        if_wanted(dve, dve_part)

                    @block.tensor
                    def _(pe):
                        if_wanted(pe, pe_part)

                    @block.sync
                    def _(sp):
                        if_wanted(sp, sp_part)

            build(False)
            build(True)

        adj = adj_t[:].rearrange("p (s l h) -> p s h l", s=BLOCKS, h=BLOCKS)

        left_in, left_made, left_summed, left_added = (signal(n) for n in ("left_in", "left_made", "left_summed", "left_added"))
        agg_done, agg_out = signal("agg_done"), signal("agg_out")
        staged, turned, copied = signal("dense_staged"), signal("turned"), signal("copied")
        projected, evacuated = signal("projected"), signal("evacuated")
        with nc.Block() as block:
            @block.vector
            def _(dve):
                for s in (agg_out, turned, copied, projected, evacuated, left_added):
                    dve.sem_inc(s.sem)
                    s.base = 1

        def aggregate(c, h, res):
            parts = sb("agg_parts", [LO, BLOCKS, 3 * D], BF16, c)
            left = sb("agg_left", [LO, 2 * BLOCKS * D], BF16, c)
            rem = left[:].bitcast(F32).rearrange("p (s f) -> p s f", s=BLOCKS)
            left_sum = sb("agg_left_sum", [LO, D], F32, c)
            with nc.Block() as block:
                @block.vector
                def _(dve):
                    link = Chain(dve, vec)
                    v = nc.vector
                    link(v.tensor_copy(parts[:, :, 0:D], h))
                    link(v.tensor_tensor(rem, h, parts[:, :, 0:D], ALU.subtract))
                    link(v.tensor_copy(parts[:, :, D:2 * D], rem))
                    link(v.tensor_tensor(parts[:, :, 2 * D:3 * D], rem, parts[:, :, D:2 * D], ALU.subtract))
                    link.close()

            with nc.Block() as block:
                @block.tensor
                def _(pe):
                    with pe.Fori(0, BLOCKS // BLOCKS5) as i:
                        pe.wait_ge(agg_out.sem, i * BLOCKS5 + agg_out.base)
                        for k in range(BLOCKS5):
                            for s in range(BLOCKS):
                                mm = nc.tensor.matmul(psum[0:LO, k * BANK:k * BANK + 3 * D],
                                                      adj[:, s, bass.ds(i * BLOCKS5 + k, 1), :].rearrange("p a l -> p (a l)"),
                                                      parts[:, s, :],
                                                      start=(s == 0), stop=(s == BLOCKS - 1))
                            mm.then_inc(agg_done.sem, 1)

                @block.vector
                def _(dve):
                    with dve.Fori(0, BLOCKS // BLOCKS5) as i:
                        for k in range(BLOCKS5):
                            dve.wait_ge(agg_done.sem, i * BLOCKS5 + k + 1 + agg_done.base)
                            nc.vector.tensor_reduce(
                                res[:, bass.ds(i * BLOCKS5 + k, 1), :].rearrange("p a f -> p (a f)"),
                                psum[0:LO, k * BANK:k * BANK + 3 * D].rearrange("p (c f) -> p f c", c=3),
                                AX.X, ALU.add).then_inc(agg_out.sem, 1)
                    dve.wait_ge(agg_out.sem, agg_out.base + BLOCKS)
            agg_done.base += BLOCKS
            agg_out.base += BLOCKS

            with nc.Block() as block:
                @block.sync
                def _(sp):
                    with sp.If(sp.value_load(extra_i[0:1, 0:1], min_val=0, max_val=1) != 0):
                        with sp.Fori(0, BLOCKS) as s:
                            sp.wait_ge(left_added.sem, s * BLOCKS + left_added.base)
                            sp.sem_inc(passed.sem)
                            sp.dma_start(left[:, 0:NODES], left_d[:, bass.ds(s * NODES, NODES)]).then_inc(left_in.sem, 16)
                    sp.sem_inc(passed.sem)


                @block.tensor
                def _(pe):
                    with pe.If(pe.value_load(extra_i[0:1, 0:1], min_val=0, max_val=1) != 0):
                        with pe.Fori(0, BLOCKS) as s:
                            pe.wait_ge(left_in.sem, s * 16 + 16 + left_in.base)
                            pe.sem_inc(passed.sem)
                            with pe.Fori(0, BLOCKS) as i:
                                pe.wait_ge(left_added.sem, s * BLOCKS + i + left_added.base)
                                nc.tensor.matmul(psum[0:LO, 0:3 * D],
                                                 left[:, 0:NODES].rearrange("p (l h) -> p h l", h=BLOCKS)[:, bass.ds(i, 1), :].rearrange("p a l -> p (a l)"),
                                                 parts[:, bass.ds(s, 1), :].rearrange("p a f -> p (a f)"),
                                                 start=True, stop=True).then_inc(left_made.sem, 1)
                    pe.sem_inc(passed.sem)


                @block.vector
                def _(dve):
                    with dve.If(dve.value_load(extra_i[0:1, 0:1], min_val=0, max_val=1) != 0):
                        with dve.Fori(0, BLOCKS) as s:
                            with dve.Fori(0, BLOCKS) as i:
                                dve.wait_ge(left_made.sem, s * BLOCKS + i + 1 + left_made.base)
                                nc.vector.tensor_reduce(left_sum[:], psum[0:LO, 0:3 * D].rearrange("p (c f) -> p f c", c=3),
                                                        AX.X, ALU.add).then_inc(left_summed.sem, 1)
                                dve.wait_ge(left_summed.sem, s * BLOCKS + i + 1 + left_summed.base)
                                at = res[:, bass.ds(i, 1), :].rearrange("p a f -> p (a f)")
                                nc.vector.tensor_tensor(at, at, left_sum[:], ALU.add).then_inc(left_added.sem, 1)
                                dve.wait_ge(left_added.sem, s * BLOCKS + i + 1 + left_added.base)
                    dve.sem_inc(passed.sem)
            left_in.base += 16 * BLOCKS
            for s in (left_added, left_made, left_summed):
                s.base += BLOCKS * BLOCKS

        def project(ins, K, ws, res, M):
            C = len(ins)
            with ExitStack() as c:
                stage = sb("stage", [LO, C, BLOCKS5, K], F32, c)
                turn = sb("turn", [K, BLOCKS5, C * LO], F32, c)
                with nc.Block() as block:
                    @block.scalar
                    def _(act):
                        with act.Fori(0, BLOCKS // BLOCKS5) as i:
                            act.wait_ge(turned.sem, i * BLOCKS5 + turned.base)
                            for n in range(C):
                                nc.scalar.copy(stage[:, n, :, :], ins[n][:, bass.ds(i * BLOCKS5, BLOCKS5), :]).then_inc(staged.sem, 1)
                            for k in range(BLOCKS5):
                                act.wait_ge(turned.sem, i * BLOCKS5 + k + 1 + turned.base)
                                act.wait_ge(projected.sem, i * BLOCKS5 + projected.base)
                                nc.scalar.copy(turn[:, k, :], psum[0:K, k * BANK:k * BANK + C * LO]).then_inc(copied.sem, 1)

                    @block.tensor
                    def _(pe):
                        with pe.Fori(0, BLOCKS // BLOCKS5) as i:
                            pe.wait_ge(staged.sem, i * C + C + staged.base)
                            pe.wait_ge(copied.sem, i * BLOCKS5 + copied.base)
                            pe.sem_inc(passed.sem)
                            for k in range(BLOCKS5):
                                for n in range(C):
                                    mm = nc.tensor.transpose(psum[0:K, k * BANK + n * LO:k * BANK + (n + 1) * LO],
                                                             stage[:, n, k, :], ident[0:LO, 0:LO])
                                mm.then_inc(turned.sem, 1)
                            pe.wait_ge(evacuated.sem, i + evacuated.base)
                            for k in range(BLOCKS5):
                                pe.wait_ge(copied.sem, i * BLOCKS5 + k + 1 + copied.base)
                                for n in range(C):
                                    mm = nc.tensor.matmul(psum[0:LO, 5 * BANK + k * P:5 * BANK + k * P + M],
                                                          turn[:, k, n * LO:(n + 1) * LO], ws[n],
                                                          start=(n == 0), stop=(n == C - 1))
                                mm.then_inc(projected.sem, 1)

                    @block.vector
                    def _(dve):
                        with dve.Fori(0, BLOCKS // BLOCKS5) as i:
                            dve.wait_ge(projected.sem, i * BLOCKS5 + BLOCKS5 + projected.base)
                            nc.vector.tensor_copy(
                                res[:, bass.ds(i * BLOCKS5, BLOCKS5), :],
                                psum[0:LO, 5 * BANK:5 * BANK + BLOCKS5 * P].rearrange("p (k m) -> p k m", m=P)[:, :, 0:M],
                            ).then_inc(evacuated.sem, 1)
                        dve.wait_ge(evacuated.sem, evacuated.base + BLOCKS // BLOCKS5)
            turned.base += BLOCKS
            copied.base += BLOCKS
            projected.base += BLOCKS
            staged.base += C * (BLOCKS // BLOCKS5)
            evacuated.base += BLOCKS // BLOCKS5

        def over_nodes(v, m):
            return v.rearrange("p (a m) -> p a m", a=1).to_broadcast([LO, BLOCKS, m])

        def over_features(v, m):
            return v.rearrange("p (b a) -> p b a", a=1).to_broadcast([LO, BLOCKS, m])

        def vector_steps(steps):
            with nc.Block() as block:
                @block.vector
                def _(dve):
                    link = Chain(dve, vec)
                    steps(nc.vector, link)
                    link.close()

        def scalar_step(step):
            with nc.Block() as block:
                @block.scalar
                def _(act):
                    link = Chain(act, act_step)
                    link(step())
                    link.close()

        def load_all(pairs):
            with nc.Block() as block:
                @block.sync
                def _(sp):
                    for dst, src in pairs:
                        sp.dma_start(dst, src).then_inc(load.sem, 16)
                    sp.wait_ge(load.sem, load.base + 16 * len(pairs))
            load.base += 16 * len(pairs)

        def store_all(pairs):
            with nc.Block() as block:
                @block.sync
                def _(sp):
                    for dst, src in pairs:
                        sp.dma_start(dst, src).then_inc(store.sem, 16)
                    sp.wait_ge(store.sem, store.base + 16 * len(pairs))
            store.base += 16 * len(pairs)

        def row(name, n):
            return a[name].rearrange("(a n) -> a n", a=1).to_broadcast([LO, n])

        def inverse_root(c, name, v):
            root = sb(name, list(v.shape), F32, c)
            scalar_step(lambda: nc.scalar.activation(root[:], v, ACT.Sqrt))
            vector_steps(lambda e, link: link(e.reciprocal(v, root[:])))

        def layer_norm(y):
            with ExitStack() as c:
                mean = sb("ln_mean", [LO, BLOCKS], F32, c)
                var = sb("ln_var", [LO, BLOCKS], F32, c)
                sq = sb("ln_sq", [LO, BLOCKS, D], F32, c)

                def center(v, link):
                    link(v.tensor_tensor(x[:], x[:], y, ALU.add))
                    link(v.tensor_reduce(mean[:], x[:], AX.X, ALU.add))
                    link(v.tensor_scalar(mean[:], mean[:], 1.0 / D, None, ALU.mult))
                    link(v.tensor_tensor(x[:], x[:], over_features(mean[:], D), ALU.subtract))
                    link(v.tensor_tensor(sq[:], x[:], x[:], ALU.mult))
                    link(v.tensor_reduce(var[:], sq[:], AX.X, ALU.add))
                    link(v.tensor_scalar(var[:], var[:], 1.0 / D, EPS, ALU.mult, ALU.add))
                vector_steps(center)
                inverse_root(c, "ln_root", var[:])
                vector_steps(lambda v, link: link(v.tensor_tensor(x[:], x[:], over_features(var[:], D), ALU.mult)))

        def batch_norm(y, m, gamma, beta):
            with ExitStack() as c:
                part_sum = sb("bn_part", [LO, m], F32, c)
                stat = sb("bn_stat", [LO, m], F32, c)
                sq = sb("bn_sq", [LO, BLOCKS, m], F32, c)

                def total(src, finish):
                    vector_steps(lambda v, link: link(v.tensor_reduce(part_sum[:], src.rearrange("p b m -> p m b"), AX.X, ALU.add)))
                    with nc.Block() as block:
                        @block.tensor
                        def _(pe):
                            nc.tensor.matmul(psum[0:LO, 0:m], ones_f[0:LO, 0:LO], part_sum[:],
                                             start=True, stop=True).then_inc(pe_step.sem, 1)

                        @block.vector
                        def _(dve):
                            dve.wait_ge(pe_step.sem, pe_step.base + 1)
                            link = Chain(dve, vec)
                            finish(nc.vector, link)
                            link.close()
                    pe_step.base += 1

                def center(v, link):
                    link(v.tensor_scalar(stat[:], psum[0:LO, 0:m], 1.0 / NODES, None, ALU.mult))
                    link(v.tensor_tensor(y, y, over_nodes(stat[:], m), ALU.subtract))
                    link(v.tensor_tensor(sq[:], y, y, ALU.mult))
                total(y, center)
                total(sq[:], lambda v, link: link(v.tensor_scalar(stat[:], psum[0:LO, 0:m], 1.0 / NODES, EPS, ALU.mult, ALU.add)))
                inverse_root(c, "bn_root", stat[:])

                def scale(v, link):
                    link(v.tensor_tensor(stat[:], stat[:], gamma, ALU.mult))
                    link(v.tensor_tensor(y, y, over_nodes(stat[:], m), ALU.mult))
                    link(v.tensor_tensor(y, y, over_nodes(beta, m), ALU.add))
                vector_steps(scale)

        load_all([(x[:].rearrange("p b f -> p (b f)"), a["x"].rearrange("(p b) f -> p (b f)", b=BLOCKS))])
        with ExitStack() as c:
            vectors = ["b1", "g1", "be1", "rm1", "rv1", "b2", "g2", "be2", "rm2", "rv2"]
            vs = sb("l0_vectors", [LO, len(vectors), D], F32, c)
            w = sb("l0_w", [D, 2, D], F32, c)
            load_all([(vs[:, i, :], row(f"L0_gnn_{n}", D)) for i, n in enumerate(vectors)]
                     + [(w[:, i, :], a[f"L0_gnn_W{i + 1}"]) for i in range(2)])
            at = {n: vs[:, i, :] for i, n in enumerate(vectors)}
            vector_steps(lambda v, link: (link(v.tensor_scalar(dinv[:], deg_in[:], 1.0, None, ALU.add)),
                                          link(v.tensor_scalar(at["rv1"], at["rv1"], EPS, None, ALU.add)),
                                          link(v.tensor_scalar(at["rv2"], at["rv2"], EPS, None, ALU.add))))
            inverse_root(c, "dinv_root", dinv[:])
            inverse_root(c, "rv1_root", at["rv1"])
            inverse_root(c, "rv2_root", at["rv2"])
            h = sb("l0_h", [LO, BLOCKS, D], F32, c)
            y = sb("l0_y", [LO, BLOCKS, D], F32, c)
            vector_steps(lambda v, link: link(v.tensor_copy(h[:], x[:])))
            for i in (1, 2):
                with ExitStack() as c2:
                    vector_steps(lambda v, link: link(v.tensor_tensor(h[:], h[:], over_features(dinv[:], D), ALU.mult)))
                    aggregate(c2, h[:], y[:])
                    vector_steps(lambda v, link: (link(v.tensor_tensor(y[:], y[:], h[:], ALU.add)),
                                                  link(v.tensor_tensor(y[:], y[:], over_features(dinv[:], D), ALU.mult))))
                project([y[:]], D, [w[:, i - 1, :]], h[:], D)

                def norm(v, link, i=i):
                    link(v.tensor_tensor(at[f"g{i}"], at[f"g{i}"], at[f"rv{i}"], ALU.mult))
                    link(v.tensor_tensor(at[f"b{i}"], at[f"b{i}"], at[f"rm{i}"], ALU.subtract))
                    link(v.tensor_tensor(h[:], h[:], over_nodes(at[f"b{i}"], D), ALU.add))
                    link(v.tensor_tensor(h[:], h[:], over_nodes(at[f"g{i}"], D), ALU.mult))
                    link(v.tensor_tensor(h[:], h[:], over_nodes(at[f"be{i}"], D), ALU.add))
                    if i == 1:
                        link(v.tensor_scalar(h[:], h[:], 0.0, None, ALU.max))
                vector_steps(norm)
            top = sb("l0_top", [LO, BLOCKS], F32, c)
            total = sb("l0_total", [LO, BLOCKS], F32, c)
            vector_steps(lambda v, link: (link(v.tensor_reduce(top[:], h[:], AX.X, ALU.max)),
                                          link(v.tensor_tensor(h[:], h[:], over_features(top[:], D), ALU.subtract))))
            scalar_step(lambda: nc.scalar.activation(y[:], h[:], ACT.Exp))
            vector_steps(lambda v, link: link(v.tensor_reduce(total[:], y[:], AX.X, ALU.add)))
            scalar_step(lambda: nc.scalar.activation(top[:], total[:], ACT.Ln))
            vector_steps(lambda v, link: link(v.tensor_tensor(h[:], h[:], over_features(top[:], D), ALU.subtract)))
            layer_norm(h[:])

        with ExitStack() as c:
            w1 = sb("l1_w1", [D, 2, 2 * D], F32, c)
            w2 = sb("l1_w2", [2 * D, D], F32, c)
            b1 = sb("l1_b1", [LO, 2 * D], F32, c)
            b2 = sb("l1_b2", [LO, D], F32, c)
            load_all([(w1[:], a["L1_gnn_W1"].rearrange("(c k) m -> k c m", c=2)), (w2[:], a["L1_gnn_W2"]),
                      (b1[:], row("L1_gnn_b1", 2 * D)), (b2[:], row("L1_gnn_b2", D))])
            y = sb("l1_y", [LO, BLOCKS, D], F32, c)
            with ExitStack() as c2:
                aggregate(c2, x[:], y[:])
            hid = sb("l1_hid", [LO, BLOCKS, 2 * D], F32, c)
            project([x[:], y[:]], D, [w1[:, 0, :], w1[:, 1, :]], hid[:], 2 * D)
            vector_steps(lambda v, link: (link(v.tensor_tensor(hid[:], hid[:], over_nodes(b1[:], 2 * D), ALU.add)),
                                          link(v.tensor_scalar(hid[:], hid[:], 0.0, None, ALU.max))))
            project([hid[:]], 2 * D, [w2[:]], y[:], D)
            vector_steps(lambda v, link: link(v.tensor_tensor(y[:], y[:], over_nodes(b2[:], D), ALU.add)))
            layer_norm(y[:])
        adj_stack.close()

        with ExitStack() as c:
            some = sb("some", [LO, BLOCKS, 2], F32, c)
            deg3 = deg_half[:].rearrange("p (b h) -> p b h", h=2)
            vector_steps(lambda v, link: (link(v.tensor_scalar(some[:], deg3, 0.0, None, ALU.is_gt)),
                                          link(v.tensor_scalar(dinv_half[:], deg3, 1.0, None, ALU.max))))
            inverse_root(c, "half_root", dinv_half[:])
            vector_steps(lambda v, link: link(v.tensor_tensor(dinv_half[:], dinv_half[:], some[:], ALU.mult)))

        RING = 4
        gathered = [signal(f"gathered{u}") for u in range(RING)]
        typed = [signal(f"typed{u}") for u in range(RING)]
        idx_ready, oh_t_made, oh_s_made = signal("idx_ready"), signal("oh_t_made"), signal("oh_s_made")
        rel_done, mult_done, prod_done = signal("rel_done"), signal("mult_done"), signal("prod_done")
        scat_done, squared, zeroed = signal("scat_done"), signal("squared"), signal("zeroed")
        TURNS = GROUPS // RING

        def edge_pass(d, acc, rel_parts):
            W = 3 * d // 2
            RS = 2 * d
            RB = GROUP * RS
            with ExitStack() as c:
                gi = [sb(f"gi{u}", [P, GROUP], I32, c) for u in range(RING)]
                gx = [sb(f"gx{u}", [P, GROUP, d], F32, c) for u in range(RING)]
                tb = [sb(f"tb{u}", [P, GROUP * P], BF16, c) for u in range(RING)]
                oh_t = [sb(f"oh_t{u}", [P, GROUP * P], BF16, c) for u in range(2)]
                oh_s = [sb(f"oh_s{u}", [P, GROUP, LO], F32, c) for u in range(2)]
                part_prod = sb("part_prod", [P, GROUP, 2, d], F32, c)
                zero_f = sb("zero_f", [P, LO], F32, c)
                sq_s = sb("sq_s", [P, GROUP, LO], F32, c)
                prod = [sb(f"prod{u}", [P, GROUP, d], F32, c) for u in range(2)]
                ps_rel = [psum[:, u * RB:(u + 1) * RB] for u in range(2)]
                ps_out = [psum[0:LO, 2 * RB + u * BANK:2 * RB + u * BANK + GROUP * d] for u in range(2)]
                types = typ_d.rearrange("(a t) p -> a (t p)", a=1)
                acc2 = acc.rearrange("p k f -> p (k f)")
                with nc.Block() as block:
                    @block.gpsimd
                    def _(pool):
                        with pool.Fori(0, TURNS) as i:
                            for u in range(RING):
                                g1 = i * RING + (u + 1)
                                pool.wait_ge(mult_done.sem, g1 + mult_done.base)
                                pool.wait_ge(idx_ready.sem, g1 + idx_ready.base)
                                pool.sem_inc(passed.sem)
                                for k in range(GROUP):
                                    nc.gpsimd.indirect_dma_start(
                                        gx[u][:, k, :], None, table_d[d],
                                        bass.IndirectOffsetOnAxis(ap=gi[u][:, k:k + 1], axis=0),
                                    ).then_inc(gathered[u].sem, 16)

                    @block.scalar
                    def _(act):
                        def indices(u, at):
                            nc.scalar.copy(gi[u][:], gidx_s[:, bass.ds(at, GROUP)]).then_inc(idx_ready.sem, 1)

                        def src_one_hot(at, u, n):
                            for k in range(GROUP):
                                if k == 0:
                                    act.wait_ge(scat_done.sem, n + scat_done.base)
                                    act.wait_ge(oh_s_made.sem, n + oh_s_made.base)
                                sq = nc.scalar.activation(sq_s[:, k, :], iota[:, 0:LO], ACT.Square,
                                                          bias=lo_s[:, bass.ds(at + k, 1)], scale=-1.0)
                            sq.then_inc(squared.sem, 1)
                            act.wait_ge(squared.sem, n + squared.base)
                            nc.scalar.activation(oh_s[u % 2][:], sq_s[:], ACT.Relu, bias=one_col,
                                                 scale=-2.0).then_inc(oh_s_made.sem, 1)
                        act.sem_inc(oh_s_made.sem)
                        act.sem_inc(scat_done.sem)
                        for u in range(RING):
                            indices(u, u * GROUP)

                        def ahead(u, turn):
                            w = (u + 2) % RING
                            act.wait_ge(gathered[w].sem, (turn + u // 2) * (16 * GROUP) + gathered[w].base)
                            indices(w, turn * (RING * GROUP) + (u + 2) * GROUP)

                        for u in range(RING):
                            if u >= 2:
                                ahead(u, 0)
                            src_one_hot(u * GROUP, u, u + 1)
                        with act.Fori(1, TURNS) as i:
                            for u in range(RING):
                                ahead(u, i)
                                src_one_hot(i * (RING * GROUP) + u * GROUP, u, i * RING + (u + 1))

                    @block.sync
                    def _(sp):
                        def types_of(at, u, n):
                            sp.wait_ge(oh_t_made.sem, n)
                            sp.dma_start(tb[u][:], types[:, bass.ds(at, GROUP * P)].to_broadcast([P, GROUP * P])).then_inc(typed[u].sem, 16)
                        with sp.Fori(0, TURNS) as i:
                            for u in range(RING):
                                types_of(i * (RING * GROUP * P) + u * GROUP * P, u, i * RING + (u + 1) + oh_t_made.base)
                        for u in range(2):
                            types_of((GROUPS + u) * GROUP * P, u, GROUPS + u + 1 + oh_t_made.base)

                    @block.vector
                    def _(dve):
                        link = Chain(dve, vec)
                        v = nc.vector
                        dve.sem_inc(mult_done.sem, RING)
                        dve.sem_inc(prod_done.sem)
                        dve.sem_inc(oh_t_made.sem, RING)

                        def type_one_hot(u, n):
                            dve.wait_ge(typed[u].sem, n * 16 + 16 + typed[u].base)
                            v.tensor_scalar(oh_t[u % 2][:], tb[u][:], part, None, ALU.is_equal).then_inc(oh_t_made.sem, 1)

                        def add(bucket, u, k):
                            to = acc2[:, bass.ds(bucket * d, d)]
                            link(v.tensor_tensor(to, to, ps_out[u % 2][:, k * d:(k + 1) * d], ALU.add))

                        link(v.memset(acc, 0.0))
                        v.memset(zero_f[:], 0.0).then_inc(zeroed.sem, 1)
                        type_one_hot(0, 0)
                        type_one_hot(1, 0)
                        regs = [[dve.alloc_register(f"bucket{d}_{u}_{k}") for k in range(GROUP)] for u in range(RING)]

                        def load_buckets(u, first):
                            dve.load(regs[u], bucket_r[0:1, bass.ds(first, GROUP)])
                            return [dve.snap(r, min_val=0, max_val=BUCKETS - 1) for r in regs[u]]

                        with dve.Fori(0, TURNS) as i:
                            link.turn = i * (RING * GROUP)
                            for u in range(RING):
                                g1 = i * RING + (u + 1)
                                dve.wait_ge(rel_done.sem, g1 + rel_done.base)

                                type_one_hot((u + 2) % RING, i + (u + 2) // RING)
                                dve.wait_ge(gathered[u].sem, i * (16 * GROUP) + 16 * GROUP + gathered[u].base)
                                dve.wait_ge(prod_done.sem, g1 + prod_done.base)
                                rel = ps_rel[u % 2].rearrange("p (g w) -> p g w", w=RS)
                                for s in range(2):
                                    mul = v.tensor_tensor(
                                        part_prod[:, :, s, :].rearrange("p g (a f) -> p g a f", a=2),
                                        gx[u][:, :, s * d // 2:(s + 1) * d // 2].rearrange("p g (a f) -> p g a f", a=1).to_broadcast([P, GROUP, 2, d // 2]),
                                        rel[:, :, s * d // 2:s * d // 2 + d].rearrange("p g (a f) -> p g a f", a=2),
                                        ALU.mult)
                                mul.then_inc(mult_done.sem, 1)
                                buckets = load_buckets(u, i * (RING * GROUP) + u * GROUP)

                                def add_last(k):
                                    add(buckets[k], u + 1, k)

                                dve.wait_ge(scat_done.sem, g1 + 1 + scat_done.base)
                                add_last(0)
                                dve.wait_ge(mult_done.sem, g1 + RING + mult_done.base)
                                v.tensor_tensor(prod[u % 2][:], part_prod[:, :, 0, :], part_prod[:, :, 1, :],
                                                ALU.add).then_inc(prod_done.sem, 1)
                                add_last(1)
                                add_last(2)
                                add_last(3)
                        link.turn = 0
                        link.n += (TURNS - 1) * RING * GROUP
                        buckets = load_buckets(0, TURNS * RING * GROUP)
                        dve.wait_ge(scat_done.sem, GROUPS + 2 + scat_done.base)
                        for k in range(GROUP):
                            add(buckets[k], RING - 1, k)
                        link.close()

                    @block.tensor
                    def _(pe):
                        def relations(u, n, free):
                            pe.wait_ge(oh_t_made.sem, n + RING + oh_t_made.base)
                            pe.wait_ge(mult_done.sem, free)
                            for k in range(GROUP):
                                for s in range(3):
                                    mm = nc.tensor.matmul(ps_rel[u % 2][:, k * RS:k * RS + W], oh_t[u % 2][:, k * P:(k + 1) * P],
                                                          rel_parts[:, s, :], start=(s == 0), stop=(s == 2))
                            mm.then_inc(rel_done.sem, 1)

                        for u in range(2):
                            relations(u, u + 1, RING + mult_done.base)
                        pe.wait_ge(zeroed.sem, 1 + zeroed.base)
                        for k in range(GROUP):
                            mm = nc.tensor.matmul(ps_out[1][:, k * d:(k + 1) * d], zero_f[:], zero_f[:, 0:1].to_broadcast([P, d]),
                                                  start=True, stop=True)
                        mm.then_inc(scat_done.sem, 1)
                        with pe.Fori(0, TURNS) as i:
                            for u in range(RING):
                                g1 = i * RING + (u + 1)
                                pe.wait_ge(oh_s_made.sem, g1 + 1 + oh_s_made.base)
                                pe.wait_ge(prod_done.sem, g1 + 1 + prod_done.base)
                                for k in range(GROUP):
                                    mm = nc.tensor.matmul(ps_out[u % 2][:, k * d:(k + 1) * d], oh_s[u % 2][:, k, :],
                                                          prod[u % 2][:, k, :], start=True, stop=True)
                                mm.then_inc(scat_done.sem, 1)
                                relations(u % 2, g1 + 2, g1 + RING + mult_done.base)
            for s, n in ((mult_done, GROUPS + RING), (oh_t_made, GROUPS + 2 + RING), (oh_s_made, GROUPS + 1), (squared, GROUPS), (zeroed, 1),
                         (idx_ready, GROUPS + 2), (rel_done, GROUPS + 2), (prod_done, GROUPS + 1), (scat_done, GROUPS + 2),
                         (typed[0], 16), (typed[1], 16)):
                s.base += n
            for u in range(RING):
                gathered[u].base += 16 * GROUP * TURNS
                typed[u].base += 16 * TURNS

        def small_products(jobs):
            with nc.Block() as block:
                @block.tensor
                def _(pe):
                    for j, (to, lhs, rhs, turned_) in enumerate(jobs):
                        k, m = to.shape
                        where = psum[0:k, j * BANK:j * BANK + m]
                        mm = nc.tensor.transpose(where, lhs, rhs) if turned_ else \
                            nc.tensor.matmul(where, lhs, rhs, start=True, stop=True)
                        mm.then_inc(pe_step.sem, 1)

                @block.vector
                def _(dve):
                    link = Chain(dve, vec)
                    for j, (to, *_) in enumerate(jobs):
                        k, m = to.shape
                        dve.wait_ge(pe_step.sem, pe_step.base + j + 1)
                        link(nc.vector.tensor_copy(to, psum[0:k, j * BANK:j * BANK + m]))
                    link.close()
            pe_step.base += len(jobs)

        load_all([(rel[:], a["L2_gnn_init_rel"])])

        def comp_layer(c, n, d, m, feats, rel_in, res, rel_next):
            W = 3 * d // 2
            pre = f"L2_gnn_c{n}_"
            wp = sb(f"wp{n}", [d, 3, m], F32, c)
            rel_parts = sb(f"rel_parts{n}", [P, 3, W], BF16, c)
            with ExitStack() as c2:
                dftc = sb(f"dft{n}", [d, 2 * d + W], F32, c2)
                win = sb(f"w{n}", [d, 3, m], F32, c2)
                wrel = sb(f"wrel{n}", [d, m], F32, c2)
                loop_col = sb(f"loop_col{n}", [d, 1], F32, c2)
                rel_t = sb(f"rel_t{n}", [d, RELS], F32, c2)
                inv_t = sb(f"inv_t{n}", [d, d], F32, c2)
                rel_f = sb(f"rel_f{n}", [P, W], F32, c2)
                loop_f = sb(f"loop_f{n}", [LO, W], F32, c2)
                load_all([(dftc[:], a[f"const_dft{d}"]), (wrel[:], a[pre + "w_rel"]),
                          (loop_col[:], a[pre + "loop_rel"].rearrange("a (k b) -> (a k) b", b=1))]
                         + [(win[:, i, :], a[pre + w]) for i, w in enumerate(("w_in", "w_out", "w_loop"))])
                fwd, relm, inv = dftc[:, 0:d], dftc[:, d:d + W], dftc[:, d + W:2 * d + W]
                vector_steps(lambda v, link: (link(v.memset(rel_f[:], 0.0)), link(v.memset(rel_parts[:], 0.0))))
                small_products([(rel_t[:], rel_in, ident[0:RELS, 0:RELS], True),
                                (inv_t[:], inv, ident[0:d, 0:d], True),
                                (loop_f[:], loop_col[:].to_broadcast([d, LO]), relm, False)])
                jobs = [(rel_f[0:RELS, :], rel_t[:], relm, False)]
                jobs += [(wp[:, i, :], inv, win[:, i, :], False) for i in range(3)]
                if rel_next is not None:
                    jobs += [(rel_next, rel_t[:], wrel[:], False)]
                small_products(jobs)

                rem = sb(f"rel_rem{n}", [P, W], F32, c2)

                def split(v, link):
                    link(v.tensor_copy(rel_parts[:, 0, :], rel_f[:]))
                    link(v.tensor_tensor(rem[:], rel_f[:], rel_parts[:, 0, :], ALU.subtract))
                    link(v.tensor_copy(rel_parts[:, 1, :], rem[:]))
                    link(v.tensor_tensor(rel_parts[:, 2, :], rem[:], rel_parts[:, 1, :], ALU.subtract))
                vector_steps(split)
                xf = sb(f"xf{n}", [LO, BLOCKS, d], F32, c2)
                project([feats], d, [fwd], xf[:], d)
                with ExitStack() as c3:
                    sc = sb(f"scaled{n}", [LO, BLOCKS, d], F32, c3)
                    for hf in range(2):
                        vector_steps(lambda v, link: link(v.tensor_tensor(sc[:], xf[:], over_features(dinv_half[:, :, hf], d), ALU.mult)))
                        store_all([(table_d[d][hf * NODES:(hf + 1) * NODES, :].rearrange("(p b) f -> p (b f)", b=BLOCKS),
                                    sc[:].rearrange("p b f -> p (b f)"))])
                    def loop_term(v, link):
                        half = d // 2
                        for o in range(2):
                            to = keep[:, :, o * half:(o + 1) * half]
                            for s, t in ((0, to), (1, tmp2[:])):
                                link(v.tensor_tensor(t, xf[:, :, s * half:(s + 1) * half],
                                                     over_nodes(loop_f[:, (s + o) * half:(s + o + 1) * half], half), ALU.mult))
                            link(v.tensor_tensor(to, to, tmp2[:], ALU.add))
                    tmp2 = sb(f"loop_tmp{n}", [LO, BLOCKS, d // 2], F32, c3)
                    keep = sb(f"loop_keep{n}", [LO, BLOCKS, d], F32, c3)
                    vector_steps(loop_term)
                    store_all([(loop_d[d], keep[:].rearrange("p b f -> p (b f)"))])
            acc = sb(f"acc{n}", [LO, BUCKETS, d], F32, c)
            edge_pass(d, acc[:], rel_parts)
            acc3 = acc[:].rearrange("p (b h) f -> p b h f", h=2)
            with ExitStack() as c2:
                lt = sb(f"lt{n}", [LO, BLOCKS, d], F32, c2)
                load_all([(lt[:].rearrange("p b f -> p (b f)"), loop_d[d])])
                vector_steps(lambda v, link: [link(v.tensor_tensor(acc3[:, :, hf, :], acc3[:, :, hf, :],
                                                                   over_features(dinv_half[:, :, hf], d), ALU.mult)) for hf in range(2)])
                project([acc3[:, :, 0, :], acc3[:, :, 1, :], lt[:]], d, [wp[:, i, :] for i in range(3)], res, m)

        def finish_comp(n, m, y):
            pre = f"L2_gnn_c{n}_"
            with ExitStack() as c:
                vb = sb(f"comp_v{n}", [LO, 3, m], F32, c)
                load_all([(vb[:, i, :], row(pre + w, m)) for i, w in enumerate(("bias", "gamma", "beta"))])
                vector_steps(lambda v, link: (link(v.tensor_scalar(y, y, 1.0 / 3.0, None, ALU.mult)),
                                              link(v.tensor_tensor(y, y, over_nodes(vb[:, 0, :], m), ALU.add))))
                batch_norm(y, m, vb[:, 1, :], vb[:, 2, :])
                scalar_step(lambda: nc.scalar.activation(y, y, ACT.Tanh))

        with ExitStack() as c:
            y1 = sb("comp_y1", [LO, BLOCKS, 2 * D], F32, c)
            y2 = sb("comp_y2", [LO, BLOCKS, D], F32, c)
            with ExitStack() as c2:
                comp_layer(c2, 1, D, 2 * D, x[:], rel[:], y1[:], rel2[:])
            finish_comp(1, 2 * D, y1[:])
            with ExitStack() as c2:
                comp_layer(c2, 2, 2 * D, D, y1[:], rel2[:], y2[:], None)
            finish_comp(2, D, y2[:])
            layer_norm(y2[:])

        with ExitStack() as c:
            adj_t = sb("adj_again", [LO, BLOCKS * NODES], BF16, c)
            adj = adj_t[:].rearrange("p (s l h) -> p s h l", s=BLOCKS, h=BLOCKS)
            load_all([(adj_t[:], adj_d)])
            w = sb("l3_w", [D, D], F32, c)
            vb = sb("l3_v", [LO, 3, D], F32, c)
            load_all([(w[:], a["L3_gnn_W"])] + [(vb[:, i, :], row(f"L3_gnn_{n}", D)) for i, n in enumerate(("b", "gamma", "beta"))])
            sc_out = sb("l3_out", [LO, BLOCKS], F32, c)
            sc_in = sb("l3_in", [LO, BLOCKS], F32, c)
            deg3 = deg_half[:].rearrange("p (b h) -> p b h", h=2)
            vector_steps(lambda v, link: (link(v.tensor_reduce(sc_out[:], deg3, AX.X, ALU.add)),
                                          link(v.tensor_scalar(sc_out[:], sc_out[:], 1.0, None, ALU.max)),
                                          link(v.tensor_scalar(sc_in[:], deg_in[:], 1.0, None, ALU.max))))
            inverse_root(c, "l3_root_out", sc_out[:])
            inverse_root(c, "l3_root_in", sc_in[:])
            h = sb("l3_h", [LO, BLOCKS, D], F32, c)
            y = sb("l3_y", [LO, BLOCKS, D], F32, c)
            vector_steps(lambda v, link: link(v.tensor_tensor(h[:], x[:], over_features(sc_out[:], D), ALU.mult)))
            with ExitStack() as c2:
                aggregate(c2, h[:], y[:])
            vector_steps(lambda v, link: link(v.tensor_tensor(y[:], y[:], over_features(sc_in[:], D), ALU.mult)))
            project([y[:]], D, [w[:]], h[:], D)
            vector_steps(lambda v, link: link(v.tensor_tensor(h[:], h[:], over_nodes(vb[:, 0, :], D), ALU.add)))
            batch_norm(h[:], D, vb[:, 1, :], vb[:, 2, :])
            vector_steps(lambda v, link: link(v.tensor_scalar(y[:], h[:], 0.0, None, ALU.min)))
            scalar_step(lambda: nc.scalar.activation(y[:], y[:], ACT.Exp))
            vector_steps(lambda v, link: (link(v.tensor_scalar(h[:], h[:], 0.0, -1.0, ALU.max, ALU.add)),
                                          link(v.tensor_tensor(h[:], h[:], y[:], ALU.add)),
                                          link(v.tensor_tensor(h[:], h[:], x[:], ALU.add))))
            layer_norm(h[:])
        store_all([(out.rearrange("(p b) f -> p (b f)", b=BLOCKS), x[:].rearrange("p b f -> p (b f)"))])


_OUTS = [((NODES, D), "float32")]


def kernel(**inputs):
    import concourse.bacc as _bacc
    from concourse.bass_utils import run_bass_kernel_spmd as _run

    nc = _bacc.Bacc("TRN2", target_bir_lowering=False, num_devices=1)
    arrays, aps = {}, {}
    for name, value in {**inputs, **constants()}.items():
        v = np.ascontiguousarray(value)
        arrays[f"in_{name}"] = v
        aps[name] = nc.dram_tensor(f"in_{name}", v.shape, mybir.dt.from_np(v.dtype), kind="ExternalInput").ap()
    out = nc.dram_tensor("out_0", (NODES, D), F32, kind="ExternalOutput").ap()
    gnn_stack(nc, aps, out)
    r = _run(nc, [arrays], core_ids=[0])
    return r.results[0]["out_0"]
```

```python
from contextlib import ExitStack

import numpy as np

import concourse.bass as bass
from concourse import mybir

F32 = mybir.dt.float32
BF16 = mybir.dt.bfloat16
I32 = mybir.dt.int32
I16 = mybir.dt.int16
U16 = mybir.dt.uint16
ALU = mybir.AluOpType
ACT = mybir.ActivationFunctionType
AX = mybir.AxisListType

P = 128
NODES = 3125
BLOCKS = 25
LO = NODES // BLOCKS
D = 64
EDGES = 100000
HALF = EDGES // 2
HC = 392
COLS = 2 * HC
LAST = HALF - (P - 1) * HC
UNUSED = P * HC - HALF
BUCKETS = 2 * BLOCKS
HT = 416
TILES = 2 * HT
GROUP = 4
GROUPS = TILES // GROUP
SLOTS = HT * P
BANK = 512
BANKS = -(-NODES // BANK)
RELS = 100
CH = 104
NCH = HT // CH
EPS = 1e-5
QUAD = 4
VR = 3
SR = 4
SHIFT = 8
SCATTER = 28
STEPS = HC // (2 * SCATTER)
BLOCKS5 = 5
ROW = HT + QUAD
assert HT % GROUP == 0 and HT % CH == 0 and STEPS * 2 * SCATTER == HC
assert HALF // P + BLOCKS <= HT and 0 < LAST <= HC


def dft(d):
    n = np.arange(d)[:, None] * np.arange(d // 2)[None, :] * (2 * np.pi / d)
    re, im = np.cos(n), -np.sin(n)
    im0 = im.copy()
    im[:, 0] = np.cos(np.pi * np.arange(d))
    fwd = np.concatenate([re, im], 1)
    neg = -re
    neg[:, 0] = im[:, 0]
    rel = np.concatenate([re, im0, neg], 1)
    inv = np.concatenate([2 * re, 2 * im], 1) / d
    inv[:, 0] = 1.0 / d
    inv[:, d // 2] = im[:, 0] / d
    return fwd.astype(np.float32), rel.astype(np.float32), inv.astype(np.float32)


def constants():
    c = np.zeros((P, 3 * P + 8 + BLOCKS), np.float32)
    q = np.arange(P)
    c[:, 0:P] = np.eye(P)
    c[:, P:2 * P] = q[:, None] < q[None, :]
    c[:, 2 * P:3 * P] = q[None, :]
    c[:, 3 * P + 2] = q
    c[:, 3 * P + 3] = 1
    c[:, 3 * P + 8:] = np.arange(BLOCKS)
    out = {"const_small": c}
    for d in (64, 128):
        fwd, rel, inv = dft(d)
        out[f"const_dft{d}"] = np.concatenate([fwd, rel, inv], 1)
    return out


class Signal:

    def __init__(self, ctx, nc, name):
        self.sem = ctx.enter_context(nc.semaphore(name))
        self.base = 0


class Chain:

    def __init__(self, eng, signal):
        self.eng, self.of, self.n, self.turn = eng, signal, signal.base, 0

    def __call__(self, ins):
        self.n += 1
        ins.then_inc(self.of.sem, 1)
        self.eng.wait_ge(self.of.sem, self.n + self.turn)

    def looped(self, count, per):
        self.turn = 0
        self.n += (count - 1) * per

    def close(self):
        self.of.base = self.n


def gnn_stack(nc, a, out):
    ctx = ExitStack()
    with ctx:
        used = {}

        def sb(name, shape, dt, c=ctx):
            used[name] = used.get(name, 0) + 1
            if used[name] > 1:
                name = f"{name}_{used[name]}"
            return c.enter_context(nc.sbuf_tensor(name, shape, dt))

        def signal(name):
            return Signal(ctx, nc, name)

        psum = ctx.enter_context(nc.psum_tensor("psum", [P, 8 * BANK], F32))
        load = signal("load")
        store = signal("store")
        vec = signal("vec")
        act_step = signal("act_step")
        pe_step = signal("pe_step")
        pool_step = signal("pool_step")
        passed = signal("passed")

        rec_d = [nc.dram_tensor(f"sorted_edges{h}", [SLOTS + 2 * UNUSED, 4], F32, kind="Internal").ap() for h in range(2)]
        out_rec_d = nc.dram_tensor("out_edges", [P, HC * 4], F32, kind="Internal").ap()
        out_row_d = nc.dram_tensor("out_rows", [P, HC], I32, kind="Internal").ap()
        typ_d = nc.dram_tensor("sorted_types", [TILES + 2 * GROUP, P], BF16, kind="Internal").ap()
        adj_d = nc.dram_tensor("adj_saved", [LO, BLOCKS * NODES], BF16, kind="Internal").ap()
        left_d = nc.dram_tensor("adj_left", [LO, BLOCKS * NODES], BF16, kind="Internal").ap()
        quads_d = nc.dram_tensor("fours", [2, ROW * 4], U16, kind="Internal").ap()
        bank_d = nc.dram_tensor("tile_banks", [2, TILES], F32, kind="Internal").ap()
        table_d = {d: nc.dram_tensor(f"gather_table{d}", [2 * NODES, d], F32, kind="Internal").ap()
                   for d in (64, 128)}
        loop_d = {d: nc.dram_tensor(f"loop_term{d}", [LO, BLOCKS * d], F32, kind="Internal").ap()
                  for d in (64, 128)}

        cst = sb("cst", [P, 3 * P + 8 + BLOCKS], F32)
        ident, before = cst[:, 0:P], cst[:, P:2 * P]
        iota = cst[:, 2 * P:3 * P]
        part = cst[:, 3 * P + 2:3 * P + 3]
        kvals = cst[:, 3 * P + 8:]
        lo_s = sb("lo_s", [P, TILES + GROUP], F32)
        gidx_s = sb("gidx_s", [P, TILES + 2 * GROUP], I32)
        bucket_r = sb("bucket_r", [1, GROUP + TILES], I16)
        deg_half = sb("deg_half", [LO, BUCKETS], F32)
        deg_in = sb("deg_in", [LO, BLOCKS], F32)
        ones_f = sb("ones_f", [P, P], F32)
        one_col = cst[:, 3 * P + 3:3 * P + 4]
        first_tile_i = sb("first_tile_i", [1, 2 * (BLOCKS + 1)], I32)
        first_tile_f = sb("first_tile_f", [P, 2, BLOCKS], F32)
        st_rec = [sb(f"st_rec{h}", [P, SCATTER, 4], F32) for h in range(2)]
        st_row = [sb(f"st_row{h}", [P, SCATTER], I32) for h in range(2)]
        extra_i = sb("extra_i", [1, 1], I32)
        start_col = sb("start_col", [P, 2], F32)
        x_room = sb("x", [P, max(BLOCKS * D, 2 * (TILES + QUAD))], F32)
        x = x_room[0:LO, 0:BLOCKS * D].rearrange("p (s d) -> p s d", s=BLOCKS)
        dinv = sb("dinv", [LO, BLOCKS], F32)
        dinv_half = sb("dinv_half", [LO, BLOCKS, 2], F32)
        rel = sb("rel", [RELS, D], F32)
        rel2 = sb("rel2", [RELS, 2 * D], F32)

        sort = ExitStack()
        with sort:
            src_i = sb("src_i", [P, COLS], I32, sort)
            dst_i = sb("dst_i", [P, COLS], I32, sort)
            typ_i = sb("typ_i", [P, COLS], I32, sort)
            src_f = sb("src_f", [P, COLS], F32, sort)
            key = sb("key", [P, COLS], F32, sort)
            tmp = sb("tmp", [P, COLS], F32, sort)
            run = sb("run", [P, COLS], F32, sort)
            rank = sb("rank", [P, COLS], F32, sort)
            mask = sb("mask", [P, COLS], F32, sort)
            block_rank = sb("block_rank", [P, 2, COLS], F32, sort)
            ranked, rank_added = signal("ranked"), signal("rank_added")
            rec = sb("rec", [P, COLS, 4], F32, sort)
            row_i = sb("row_i", [P, COLS], I32, sort)
            cnt = sb("cnt", [P, 2, BLOCKS], F32, sort)
            tot_i = sb("tot_i", [P, 2, BLOCKS], I32, sort)
            nt = sb("nt", [P, 2, BLOCKS], F32, sort)
            base = sb("base", [P, 2, BLOCKS], F32, sort)
            empty = sb("empty", [P, HT, 4], F32, sort)
            dst_lo = sb("dst_lo", [P, COLS], F32, sort)
            dst_block = sb("dst_block", [P, COLS], F32, sort)
            zero_b = sb("zero_b", [P, P], BF16, sort)
            oh_slo = [sb(f"oh_slo{h}", [P, SCATTER, LO], BF16, sort) for h in range(2)]
            oh_sbk = [sb(f"oh_sbk{h}", [P, SCATTER, BUCKETS], BF16, sort) for h in range(2)]
            oh_dlo = [sb(f"oh_dlo{h}", [P, SCATTER, LO], BF16, sort) for h in range(2)]
            oh_dbk = [sb(f"oh_dbk{h}", [P, SCATTER, BLOCKS], BF16, sort) for h in range(2)]
            deg_made, deg_used = signal("deg_made"), signal("deg_used")
            st_made, st_sent = signal("staged"), [signal(f"sent{h}") for h in range(2)]

            with nc.Block() as block:
                @block.vector
                def _(dve):
                    link = Chain(dve, vec)
                    for t, v in ((src_i, -1), (dst_i, -1), (typ_i, 0)):
                        link(nc.vector.memset(t[:], v))
                    link(nc.vector.memset(empty[:, :, 0], -1.0))
                    link(nc.vector.memset(empty[:, :, 1], 0.0))
                    link(nc.vector.memset(empty[:, :, 2], float(P - 1)))
                    link(nc.vector.memset(empty[:, :, 3], 0.0))
                    link(nc.vector.memset(rank[:], 0.0))
                    link(nc.vector.memset(zero_b[:], 0.0))
                    link(nc.vector.memset(ones_f[:], 1.0))
                    link.close()

            with nc.Block() as block:
                @block.sync
                def _(sp):
                    sp.dma_start(cst[:], a["const_small"]).then_inc(load.sem, 16)
                    n = 1
                    for t, name in ((src_i, "src"), (dst_i, "dst"), (typ_i, "edge_type_100")):
                        for h in range(2):
                            at = a[name][h * HALF:(h + 1) * HALF]
                            full = at[0:(P - 1) * HC].rearrange("(p c) -> p c", c=HC)
                            rest = at[(P - 1) * HC:HALF].rearrange("(p c) -> p c", p=1)
                            sp.dma_start(t[0:P - 1, h * HC:(h + 1) * HC], full).then_inc(load.sem, 16)
                            sp.dma_start(t[P - 1:P, h * HC:h * HC + LAST], rest).then_inc(load.sem, 16)
                            n += 2
                    for h in range(2):
                        sp.dma_start(rec_d[h][0:SLOTS, :].rearrange("(p t) w -> p (t w)", p=P),
                                     empty[:].rearrange("p t w -> p (t w)")).then_inc(store.sem, 16)
                    sp.wait_ge(load.sem, load.base + 16 * n)
                    sp.wait_ge(store.sem, store.base + 32)
                    load.base += 16 * n
                    store.base += 32

            with nc.Block() as block:
                @block.vector
                def _(dve):
                    link = Chain(dve, vec)
                    v = nc.vector
                    def divide(n, lo, block):
                        link(v.tensor_scalar(row_i[:], n, 1.0 / BLOCKS, 0.02, ALU.mult, ALU.add))
                        link(v.tensor_copy(tmp[:], row_i[:]))
                        link(v.scalar_tensor_tensor(key[:], tmp[:], -float(BLOCKS), n, ALU.mult, ALU.add))
                        link(v.tensor_scalar(mask[:], key[:], 0.0, None, ALU.is_lt))
                        link(v.tensor_tensor(lo, tmp[:], mask[:], ALU.subtract))
                        link(v.scalar_tensor_tensor(block, mask[:], float(BLOCKS), key[:], ALU.mult, ALU.add))
                    link(v.tensor_copy(src_f[:], dst_i[:]))
                    divide(src_f[:], dst_lo[:], dst_block[:])
                    link(v.tensor_copy(src_f[:], src_i[:]))
                    divide(src_f[:], rec[:, :, 0], run[:])
                    link(v.tensor_scalar(mask[:], src_f[:], 0.0, None, ALU.is_lt))
                    link(v.scalar_tensor_tensor(key[:], mask[:], 100.0, run[:], ALU.mult, ALU.add))
                    for h in range(2):
                        at = slice(h * HC, (h + 1) * HC)
                        link(v.tensor_scalar(rec[:, at, 1], dst_i[:, at], float(h * NODES), None, ALU.add))
                        link(v.tensor_scalar(rec[:, at, 3], key[:, at], float(h * BLOCKS), None, ALU.add))
                    link(v.tensor_copy(rec[:, :, 2], typ_i[:]))
                    dve.sem_inc(rank_added.sem, 2)
                    with dve.Fori(0, BLOCKS) as k:
                        link.turn = k * 3
                        link(v.tensor_scalar(mask[:], key[:], kvals[:, bass.ds(k, 1)], None, ALU.is_equal))
                        link(v.tensor_tensor_scan(run[:], mask[:], src_f[:], 0.0, ALU.add, ALU.bypass))
                        dve.wait_ge(rank_added.sem, k + 1)
                        v.tensor_tensor(block_rank[:, bass.ds(k % 2, 1), :].rearrange("p a c -> p (a c)"),
                                        run[:], mask[:], ALU.mult).then_inc(ranked.sem, 1)
                        link(v.tensor_copy(cnt[:, :, bass.ds(k, 1)].rearrange("p h a -> p (h a)"),
                                           run[:].rearrange("p (h c) -> p h c", h=2)[:, :, HC - 1]))
                        dve.wait_ge(ranked.sem, k + 1)
                    link.looped(BLOCKS, 3)
                    link(v.tensor_copy(base[:, 1, :], cnt[:, 0, :]))
                    link(v.memset(base[:, 0, :], 0.0))
                    link(v.tensor_tensor(cnt[:, 1, :], cnt[:, 1, :], cnt[:, 0, :], ALU.subtract))
                    link.close()

                @block.gpsimd
                def _(pool):
                    with pool.Fori(0, BLOCKS) as k:
                        pool.wait_ge(ranked.sem, k + 1)
                        pool.sem_inc(passed.sem)
                        nc.gpsimd.tensor_tensor(rank[:], rank[:], block_rank[:, bass.ds(k % 2, 1), :].rearrange("p a c -> p (a c)"),
                                                ALU.add).then_inc(rank_added.sem, 1)
                        pool.wait_ge(rank_added.sem, k + 3)

            with nc.Block() as block:
                @block.tensor
                def _(pe):
                    counts = cnt[:].rearrange("p h k -> p (h k)")
                    nc.tensor.matmul(psum[:, 0:BUCKETS], before, counts, start=True, stop=True)
                    nc.tensor.matmul(psum[:, BANK:BANK + BUCKETS], ones_f[:], counts,
                                     start=True, stop=True).then_inc(pe_step.sem, 1)

                @block.vector
                def _(dve):
                    link = Chain(dve, vec)
                    v = nc.vector
                    dve.wait_ge(pe_step.sem, pe_step.base + 1)
                    pe_step.base += 1
                    flat = [t[:].rearrange("p h k -> p (h k)") for t in (nt, tot_i, first_tile_f, base)]
                    link(v.tensor_scalar(flat[0], psum[:, BANK:BANK + BUCKETS], float(P - 1), None, ALU.add))
                    link(v.tensor_copy(flat[1], flat[0]))
                    link(v.tensor_scalar(flat[1], flat[1], 7, None, ALU.arith_shift_right))
                    link(v.tensor_copy(flat[0], flat[1]))
                    link(v.tensor_scalar(flat[0], flat[0], 1.0, None, ALU.max))
                    for h in range(2):
                        link(v.tensor_tensor_scan(first_tile_f[:, h, :], nt[:, h, :], nt[:, h, :], 0.0, ALU.add, ALU.bypass))
                    link(v.tensor_tensor(flat[2], flat[2], flat[0], ALU.subtract))
                    link(v.memset(first_tile_i[:], HT))
                    for h in range(2):
                        link(v.tensor_copy(first_tile_i[:, h * (BLOCKS + 1):h * (BLOCKS + 1) + BLOCKS], first_tile_f[0:1, h, :]))
                    link(v.tensor_tensor(flat[3], psum[:, 0:BUCKETS], flat[3], ALU.subtract))
                    link(v.scalar_tensor_tensor(flat[3], flat[2], float(P), flat[3], ALU.mult, ALU.add))
                    link(v.tensor_scalar(flat[3], flat[3], -1.0, None, ALU.add))
                    with dve.Fori(0, BLOCKS) as k:
                        dve.wait_ge(rank_added.sem, k + (BLOCKS + 1))
                        for h in range(2):
                            v.tensor_scalar(block_rank[:, bass.ds(k % 2, 1), h * HC:(h + 1) * HC].rearrange("p a c -> p (a c)"),
                                            key[:, h * HC:(h + 1) * HC], kvals[:, bass.ds(k, 1)],
                                            base[:, h, bass.ds(k, 1)], ALU.is_equal, ALU.mult).then_inc(ranked.sem, 1)
                    dve.wait_ge(rank_added.sem, 2 * BLOCKS + 2)
                    link(v.tensor_copy(row_i[:], rank[:]))
                    link(v.tensor_scalar(row_i[:], row_i[:], 7, None, ALU.arith_shift_right))
                    link(v.tensor_copy(tmp[:], row_i[:]))
                    link(v.tensor_copy(row_i[:], rank[:]))
                    link(v.tensor_scalar(row_i[:], row_i[:], P - 1, None, ALU.bitwise_and))
                    link(v.tensor_copy(run[:], row_i[:]))
                    link(v.scalar_tensor_tensor(tmp[:], run[:], float(HT), tmp[:], ALU.mult, ALU.add))
                    link(v.tensor_scalar(mask[:], src_f[:], 0.0, None, ALU.is_lt))
                    link(v.tensor_tensor_scan(run[:], mask[:], mask[:], 0.0, ALU.add, ALU.bypass))
                    link(v.scalar_tensor_tensor(mask[:], run[:], float(SLOTS - 1), mask[:], ALU.add, ALU.mult))
                    link(v.tensor_scalar(run[:], src_f[:], 0.0, None, ALU.is_ge))
                    link(v.tensor_tensor(tmp[:], tmp[:], run[:], ALU.mult))
                    link(v.tensor_tensor(row_i[:], tmp[:], mask[:], ALU.add))
                    link.close()

                @block.gpsimd
                def _(pool):
                    with pool.Fori(0, BLOCKS) as k:
                        pool.wait_ge(ranked.sem, k * 2 + (BLOCKS + 2))
                        pool.sem_inc(passed.sem)
                        nc.gpsimd.tensor_tensor(rank[:], rank[:], block_rank[:, bass.ds(k % 2, 1), :].rearrange("p a c -> p (a c)"),
                                                ALU.add).then_inc(rank_added.sem, 1)
                        pool.wait_ge(rank_added.sem, k + (BLOCKS + 3))

            with nc.Block() as block:
                @block.vector
                def _(dve):
                    def stage(h, first):
                        at = bass.ds(first + h * SCATTER, SCATTER)
                        nc.vector.tensor_copy(st_row[h][:], row_i[:, at]).then_inc(st_made.sem, 1)
                        nc.vector.tensor_copy(st_rec[h][:], rec[:, at, :]).then_inc(st_made.sem, 1)

                    def one_hots(h, first, n):
                        dve.wait_ge(deg_used.sem, n)
                        at = bass.ds(first, SCATTER)
                        for to, of, size in ((oh_slo, rec[:, at, 0:1], LO), (oh_sbk, rec[:, at, 3:4], BUCKETS),
                                             (oh_dlo, dst_lo[:, at].rearrange("p (g a) -> p g a", a=1), LO),
                                             (oh_dbk, dst_block[:, at].rearrange("p (g a) -> p g a", a=1), BLOCKS)):
                            ins = nc.vector.tensor_tensor(
                                to[h][:], iota[:, 0:size].rearrange("p (a l) -> p a l", a=1).to_broadcast([P, SCATTER, size]),
                                of.to_broadcast([P, SCATTER, size]), ALU.is_equal)
                        ins.then_inc(deg_made.sem, 1)
                    dve.sem_inc(deg_used.sem, 2)
                    for h in range(2):
                        stage(h, 0)
                    for c in range(4):
                        one_hots(c % 2, c * SCATTER, c + 1)
                    with dve.Fori(1, STEPS) as k:
                        for h in range(2):
                            dve.wait_ge(st_sent[h].sem, k * (16 * SCATTER))
                            stage(h, k * (2 * SCATTER))
                            for c in (2 * h, 2 * h + 1):
                                one_hots(c % 2, k * (4 * SCATTER) + c * SCATTER, k * 4 + (c + 1))
                    dve.wait_ge(deg_used.sem, 4 * STEPS + 2)
                    nc.vector.tensor_copy(deg_half[:], psum[0:LO, 0:BUCKETS]).then_inc(deg_made.sem, 1)
                    nc.vector.tensor_copy(deg_in[:], psum[0:LO, BANK:BANK + BLOCKS]).then_inc(deg_made.sem, 1)
                    dve.wait_ge(deg_made.sem, 4 * STEPS + 2)

                @block.tensor
                def _(pe):
                    for bank, size in ((0, BUCKETS), (1, BLOCKS)):
                        nc.tensor.matmul(psum[0:LO, bank * BANK:bank * BANK + size], zero_b[:, 0:LO], zero_b[:, 0:size],
                                         start=True, stop=False, skip_group_check=True)
                    with pe.Fori(0, STEPS) as k:
                        for j in range(4):
                            h = j % 2
                            pe.wait_ge(deg_made.sem, k * 4 + (j + 1))
                            for c in range(SCATTER):
                                nc.tensor.matmul(psum[0:LO, 0:BUCKETS], oh_slo[h][:, c, :], oh_sbk[h][:, c, :],
                                                 start=False, stop=False, skip_group_check=True)
                                mm = nc.tensor.matmul(psum[0:LO, BANK:BANK + BLOCKS], oh_dlo[h][:, c, :], oh_dbk[h][:, c, :],
                                                      start=False, stop=False, skip_group_check=True)
                            mm.then_inc(deg_used.sem, 1)

                @block.gpsimd
                def _(pool):
                    with pool.Fori(0, STEPS) as k:
                        for h in range(2):
                            pool.wait_ge(st_made.sem, k * 4 + 2 * h + 2)
                            pool.sem_inc(passed.sem)
                            for c in range(SCATTER):
                                nc.gpsimd.indirect_dma_start(
                                    rec_d[0], bass.IndirectOffsetOnAxis(ap=st_row[h][:, c:c + 1], axis=0),
                                    st_rec[h][:, c, :], None).then_inc(st_sent[h].sem, 16)
                    for h in range(2):
                        pool.wait_ge(st_sent[h].sem, 16 * SCATTER * STEPS)

                @block.sync
                def _(sp):
                    sp.dma_start(out_rec_d, rec[:, HC:COLS, :].rearrange("p c w -> p (c w)")).then_inc(store.sem, 16)
                    sp.dma_start(out_row_d, row_i[:, HC:COLS]).then_inc(store.sem, 16)
                    sp.wait_ge(store.sem, store.base + 32)
            store.base += 32

        adj_stack = ExitStack()
        dst_s = x_room[:, 0:TILES + QUAD]
        key_s = x_room[:, TILES + QUAD:2 * (TILES + QUAD)]
        with nc.Block() as block:
            @block.vector
            def _(dve):
                link = Chain(dve, vec)
                for t, value in ((lo_s, -1.0), (gidx_s, 0), (bucket_r, 0), (dst_s, -1.0), (key_s, -1.0)):
                    link(nc.vector.memset(t[:], value))
                link.close()

        def sorted_tables(half):
            tiles = slice(half * HT, (half + 1) * HT)
            with ExitStack() as t1:
                rec_s = sb("rec_s", [P, HT, 4], F32, t1)
                m1 = sb("m1", [P, HT], F32, t1)
                m2 = sb("m2", [P, HT], F32, t1)
                first_p = sb("first_p", [P, 2, BLOCKS], F32, t1)
                typ_t = sb("typ_t", [CH, NCH, P], BF16, t1)
                none_b = sb("none_b", [2 * GROUP, P], BF16, t1)
                out_deg = sb("out_deg", [LO, BLOCKS], F32, t1)
                most = sb("most", [LO, 1], F32, t1)
                extra = sb("extra", [1, 1], F32, t1)
                lohi = sb("lohi", [CH, 2, NCH], F32, t1)
                lohi_i = sb("lohi_i", [CH, 2, NCH], I32, t1)
                with nc.Block() as block:
                    @block.sync
                    def _(sp):
                        sp.dma_start(rec_s[:].rearrange("p t w -> p (t w)"),
                                     rec_d[half][0:SLOTS, :].rearrange("(p t) w -> p (t w)", p=P)).then_inc(load.sem, 16)
                        sp.wait_ge(load.sem, load.base + 16)
                        load.base += 16

                with nc.Block() as block:
                    @block.vector
                    def _(dve):
                        link = Chain(dve, vec)
                        v = nc.vector
                        link(v.memset(none_b[:], float(P - 1)))
                        link(v.tensor_copy(lo_s[:, tiles], rec_s[:, :, 0]))
                        link(v.tensor_copy(gidx_s[:, tiles], rec_s[:, :, 1]))
                        link(v.tensor_copy(bucket_r[:, GROUP + half * HT:GROUP + (half + 1) * HT], rec_s[0:1, :, 3]))
                        link(v.tensor_scalar(dst_s[:, tiles], rec_s[:, :, 1], float(-half * NODES), None, ALU.add))
                        link(v.tensor_scalar(m1[:], rec_s[:, :, 3], float(-half * BLOCKS), float(LO), ALU.add, ALU.mult))
                        link(v.tensor_tensor(key_s[:, tiles], m1[:], lo_s[:, tiles], ALU.add))
                        link(v.tensor_scalar(m1[:], lo_s[:, tiles], 0.0, None, ALU.is_lt))
                        link(v.scalar_tensor_tensor(m2[:], m1[:], -9999.0, dst_s[:, tiles], ALU.mult, ALU.add))
                        link(v.scalar_tensor_tensor(m1[:], m1[:], 9999.0, dst_s[:, tiles], ALU.mult, ALU.add))
                        link(v.tensor_reduce(out_deg[:], deg_half[:].rearrange("p (h b) -> p b h", h=2), AX.X, ALU.add))
                        link(v.tensor_reduce(most[:], out_deg[:], AX.X, ALU.max))
                        for h in range(2):
                            link(v.tensor_tensor(first_p[:, h, :], first_tile_f[:, h, :], ident[:, 0:BLOCKS], ALU.mult))
                        link(v.tensor_reduce(start_col[:], first_p[:], AX.X, ALU.add))
                        link.close()

                with nc.Block() as block:
                    @block.tensor
                    def _(pe):
                        nc.tensor.matmul(psum[0:1, 6 * BANK:6 * BANK + LO], most[:], ident[0:LO, 0:LO],
                                         start=True, stop=True).then_inc(pe_step.sem, 1)
                        for c in range(NCH):
                            if c > 1:
                                pe.wait_ge(vec.sem, vec.base + 3 * (c - 1))
                            for i, of in enumerate((rec_s[:, c * CH:(c + 1) * CH, 2], m1[:, c * CH:(c + 1) * CH],
                                                    m2[:, c * CH:(c + 1) * CH])):
                                nc.tensor.transpose(psum[0:CH, (3 * (c % 2) + i) * BANK:(3 * (c % 2) + i) * BANK + P], of,
                                                    ident).then_inc(pe_step.sem, 1)

                    @block.vector
                    def _(dve):
                        v = nc.vector
                        for c in range(NCH):
                            at = [psum[0:CH, (3 * (c % 2) + i) * BANK:(3 * (c % 2) + i) * BANK + P] for i in range(3)]
                            dve.wait_ge(pe_step.sem, pe_step.base + 3 * c + 4)
                            v.tensor_copy(typ_t[:, c, :], at[0]).then_inc(vec.sem, 1)
                            v.tensor_reduce(lohi[:, 0, c:c + 1], at[1], AX.X, ALU.min).then_inc(vec.sem, 1)
                            v.tensor_reduce(lohi[:, 1, c:c + 1], at[2], AX.X, ALU.max).then_inc(vec.sem, 1)
                        vec.base += 3 * NCH
                        dve.wait_ge(vec.sem, vec.base)
                        link = Chain(dve, vec)
                        link(v.tensor_reduce(extra[:], psum[0:1, 6 * BANK:6 * BANK + LO], AX.X, ALU.max))
                        link(v.tensor_scalar(extra[:], extra[:], 256.0, None, ALU.is_gt))
                        link(v.tensor_copy(extra_i[:], extra[:]))
                        link(v.tensor_scalar(lohi[:, 1, :], lohi[:, 1, :], 0.0, None, ALU.max))
                        link(v.tensor_tensor(lohi[:, 0, :], lohi[:, 0, :], lohi[:, 1, :], ALU.min))
                        link(v.tensor_copy(lohi_i[:], lohi[:]))
                        link(v.tensor_scalar(lohi_i[:], lohi_i[:], 9, None, ALU.arith_shift_right))
                        link(v.tensor_copy(lohi[:], lohi_i[:]))
                        link.close()

                    @block.sync
                    def _(sp):
                        sp.wait_ge(vec.sem, vec.base)
                        sp.dma_start(typ_d[half * HT:(half + 1) * HT, :].rearrange("(c t) p -> t c p", t=CH),
                                     typ_t[:]).then_inc(store.sem, 16)
                        sp.dma_start(typ_d[TILES:TILES + 2 * GROUP, :], none_b[:]).then_inc(store.sem, 16)
                        for i in range(2):
                            sp.dma_start(bank_d[i, half * HT:(half + 1) * HT].rearrange("(c t) -> t c", t=CH),
                                         lohi[:, i, :], allow_slow_non_contiguous=True).then_inc(store.sem, 16)
                        sp.wait_ge(store.sem, store.base + 64)
                        store.base += 64
                pe_step.base += 3 * NCH + 1

            with ExitStack() as t1:
                def row_of(name, dt=F32):
                    return sb(name, [1, ROW], dt, t1)
                quads = sb("quads", [1, ROW, 4], U16, t1)
                tiles_i = sb("tiles_i", [P, HT], I32, t1)
                starts = sb("starts", [P, HT], F32, t1)
                first, last, same, nth, nth_i, blocked, lead, q_first, q_end, t_a = (
                    row_of(n, I32 if n == "nth_i" else F32) for n in
                    ("first", "last", "same", "nth", "nth_i", "blocked", "lead", "q_first", "q_end", "t_a"))
                with nc.Block() as block:
                    @block.gpsimd
                    def _(pool):
                        nc.gpsimd.iota(tiles_i[:], pattern=[[1, HT]], base=0,
                                       channel_multiplier=0).then_inc(pool_step.sem, 1)

                    @block.sync
                    def _(sp):
                        sp.wait_ge(vec.sem, vec.base + 2)
                        for i, to in enumerate((first, last)):
                            sp.dma_start(to[:, 0:HT], bank_d[i:i + 1, half * HT:(half + 1) * HT]).then_inc(load.sem, 16)

                    @block.tensor
                    def _(pe):
                        pe.wait_ge(vec.sem, vec.base + 4)
                        nc.tensor.matmul(psum[0:1, 0:HT], ones_f[0:BLOCKS, 0:1], starts[0:BLOCKS, :],
                                         start=True, stop=True).then_inc(pe_step.sem, 1)

                    @block.vector
                    def _(dve):
                        link = Chain(dve, vec)
                        v = nc.vector
                        link(v.memset(first[:], 99.0))
                        link(v.memset(last[:], -99.0))
                        link(v.memset(same[:], 0.0))
                        dve.wait_ge(pool_step.sem, pool_step.base + 1)
                        link(v.tensor_scalar(starts[:], tiles_i[:], start_col[:, half:half + 1], None, ALU.is_equal))
                        dve.wait_ge(pe_step.sem, pe_step.base + 1)
                        link(v.tensor_scalar(same[:, 0:HT], psum[0:1, 0:HT], -1.0, 1.0, ALU.mult, ALU.add))
                        link(v.tensor_tensor_scan(nth[:], same[:], same[:], 0.0, ALU.mult, ALU.add))
                        link(v.tensor_copy(nth_i[:], nth[:]))
                        link(v.tensor_scalar(nth_i[:], nth_i[:], QUAD - 1, None, ALU.bitwise_and))
                        link(v.tensor_scalar(lead[:], nth_i[:], 0.0, None, ALU.is_equal))
                        link(v.memset(lead[:, HT:], 0.0))
                        dve.wait_ge(load.sem, load.base + 32)
                        link(v.tensor_copy(q_first[:], first[:]))
                        link(v.tensor_copy(q_end[:], last[:]))
                        for k in range(1, QUAD):
                            n = ROW - k
                            link(v.tensor_scalar(blocked[:, 0:n], nth[:, k:], float(k), 99.0, ALU.is_lt, ALU.mult))
                            link(v.tensor_tensor(t_a[:, 0:n], first[:, k:], blocked[:, 0:n], ALU.add))
                            link(v.tensor_tensor(q_first[:, 0:n], q_first[:, 0:n], t_a[:, 0:n], ALU.min))
                            link(v.tensor_tensor(t_a[:, 0:n], last[:, k:], blocked[:, 0:n], ALU.subtract))
                            link(v.tensor_tensor(q_end[:, 0:n], q_end[:, 0:n], t_a[:, 0:n], ALU.max))
                        link(v.tensor_scalar(q_first[:], q_first[:], float(BANKS - 1), None, ALU.min))
                        link(v.tensor_scalar(q_end[:], q_end[:], 0.0, 1.0, ALU.max, ALU.add))
                        link(v.tensor_copy(quads[:, :, 0], q_first[:]))
                        link(v.tensor_copy(quads[:, :, 1], q_end[:]))
                        link(v.tensor_tensor(t_a[:], q_end[:], q_first[:], ALU.subtract))
                        link(v.tensor_tensor(t_a[:], t_a[:], lead[:], ALU.mult))
                        link(v.tensor_tensor_scan(nth[:], t_a[:], t_a[:], 0.0, ALU.add, ALU.bypass))
                        link(v.tensor_tensor(nth[:], nth[:], t_a[:], ALU.subtract))
                        link(v.tensor_tensor(nth[:], nth[:], q_first[:], ALU.subtract))
                        link(v.tensor_scalar(quads[:, :, 2], nth[:], float(SHIFT), None, ALU.add))
                        link(v.tensor_tensor_scan(nth[:], lead[:], lead[:], 0.0, ALU.add, ALU.bypass))
                        link(v.tensor_tensor(quads[:, :, 3], nth[:], lead[:], ALU.subtract))
                        link.close()
                pool_step.base += 1
                load.base += 32
                pe_step.base += 1

                with nc.Block() as block:
                    @block.sync
                    def _(sp):
                        sp.dma_start(quads_d[half:half + 1, :], quads[:].rearrange("p t w -> p (t w)")).then_inc(store.sem, 16)
                        sp.wait_ge(store.sem, store.base + 16)
                store.base += 16

        def four(eng, regs, quads, t):
            eng.load(regs, quads[0:1, bass.ds(t, 1), :].rearrange("p a w -> p (a w)"))
            return [eng.snap(r, min_val=lo, max_val=hi) for r, lo, hi in
                    zip(regs, (0, 1, 0, 0), (BANKS - 1, BANKS, BANKS * TILES, TILES))]

        def tiles_of(eng, regs, half, b):
            eng.load(regs, first_tile_i[0:1, bass.ds(b + half * (BLOCKS + 1), 2)])
            return [eng.snap(r, min_val=0, max_val=HT) for r in regs]

        def first_tile(eng, half, b):
            return eng.value_load(first_tile_i[0:1, bass.ds(b + half * (BLOCKS + 1), 1)], min_val=0, max_val=HT)

        def count_half(half):
            with ExitStack() as t2:
                quads = sb("quads", [1, ROW, 4], U16, t2)
                oh_dst = sb("oh_dst", [P, VR * QUAD * BANK], BF16, t2)
                oh_src = sb("oh_src", [P, SR * QUAD, LO], BF16, t2)
                sq_src = sb("sq_src", [P, QUAD, LO], BF16, t2)
                src_made, src_used, src_squared, dst_made, dst_used, banks_free, kept = (
                    signal(f"{n}{half}") for n in ("src_made", "src_used", "src_squared", "dst_made", "dst_used",
                                                   "banks_free", "kept"))
                with nc.Block() as block:
                    @block.sync
                    def _(sp):
                        sp.dma_start(quads[:].rearrange("p t w -> p (t w)"), quads_d[half:half + 1, :]).then_inc(load.sem, 16)
                        sp.wait_ge(load.sem, load.base + 16)
                load.base += 16

                with nc.Block() as block:
                    @block.vector
                    def _(dve):
                        regs = [dve.alloc_register(f"four_v{half}_{i}") for i in range(4)]
                        ends = [dve.alloc_register(f"ends_v{half}_{i}") for i in range(2)]
                        with dve.Fori(0, BLOCKS) as b:
                            with dve.Fori(*tiles_of(dve, ends, half, b), QUAD) as t:
                                first_bank, end_bank, visits, _ = four(dve, regs, quads, t)
                                with dve.Fori(first_bank, end_bank) as bank:
                                    v = dve.snap(visits + bank, min_val=0, max_val=BANKS * TILES)
                                    dve.wait_ge(dst_used.sem, v + 1)
                                    for k in range(QUAD):
                                        ins = nc.vector.tensor_scalar(
                                            oh_dst[:, bass.ds((v % VR) * (QUAD * BANK) + k * BANK, BANK)],
                                            iota16[:, bass.ds(bank * BANK, BANK)], dst_s[:, bass.ds(t + (half * HT + k), 1)],
                                            None, ALU.is_equal)
                                    ins.then_inc(dst_made.sem, 1)

                    @block.tensor
                    def _(pe):
                        regs = [pe.alloc_register(f"four_p{half}_{i}") for i in range(4)]
                        pe.sem_inc(dst_made.sem, SHIFT)
                        pe.sem_inc(src_used.sem, SR)
                        pe.sem_inc(dst_used.sem, SHIFT + VR)
                        ends = [pe.alloc_register(f"ends_p{half}_{i}") for i in range(2)]
                        with pe.Fori(0, BLOCKS) as b:
                            t0, t1_ = tiles_of(pe, ends, half, b)
                            for bank in range(BANKS):
                                w = min(BANK, NODES - bank * BANK)
                                pe.wait_ge(banks_free.sem, b * BANKS + bank + 1)
                                if half == 0 or w < BANK:
                                    nc.tensor.matmul(psum[0:LO, bank * BANK:(bank + 1) * BANK], zeros[:], zeros[:, 0:1].to_broadcast([P, BANK]),
                                                     start=True, stop=False, skip_group_check=True)
                                if half == 1:
                                    nc.tensor.matmul(psum[0:LO, bank * BANK:bank * BANK + w], ident_b[:],
                                                     adj_t[:, bass.ds(b * NODES + bank * BANK, w)],
                                                     start=(w == BANK), stop=False, skip_group_check=True)
                            with pe.Fori(t0, t1_, QUAD) as t:
                                first_bank, end_bank, visits, number = four(pe, regs, quads, t)
                                pe.wait_ge(src_made.sem, number + 2)
                                pe.sem_inc(passed.sem)
                                with pe.Fori(first_bank, end_bank) as bank:
                                    v = pe.snap(visits + bank, min_val=0, max_val=BANKS * TILES)
                                    pe.wait_ge(dst_made.sem, v + 1)
                                    for k in range(QUAD):
                                        mm = nc.tensor.matmul(
                                            psum[0:LO, bass.ds(bank * BANK, BANK)],
                                            oh_src[:, bass.ds((number % SR) * QUAD + k, 1), :].rearrange("p a l -> p (a l)"),
                                            oh_dst[:, bass.ds((v % VR) * (QUAD * BANK) + k * BANK, BANK)],
                                            start=False, stop=False, skip_group_check=True)
                                    mm.then_inc(dst_used.sem, 1)
                                nc.tensor.matmul(psum[0:LO, BANKS * BANK:BANKS * BANK + 1], zeros[:], zeros[:, 0:1],
                                                 start=True, stop=True).then_inc(src_used.sem, 1)

                    @block.scalar
                    def _(act):
                        act.sem_inc(banks_free.sem, BANKS)
                        act.sem_inc(kept.sem, 16)
                        act.sem_inc(src_made.sem)
                        regs = [[act.alloc_register(f"four_a{half}_{n}_{i}") for i in range(4)] for n in range(2)]
                        ends = [act.alloc_register(f"ends_a{half}_{i}") for i in range(2)]

                        def src_one_hots(t, b, number):
                            act.wait_ge(src_used.sem, number + 1)
                            act.wait_ge(src_made.sem, number + 1)
                            for k in range(QUAD):
                                sq = nc.scalar.activation(sq_src[:, k, :], iota16[:, bass.ds(b * LO, LO)], ACT.Square,
                                                          bias=key_s[:, bass.ds(t + (half * HT + k), 1)], scale=-1.0)
                            sq.then_inc(src_squared.sem, 1)
                            act.wait_ge(src_squared.sem, number + 1)
                            nc.scalar.activation(oh_src[:, bass.ds((number % SR) * QUAD, QUAD), :], sq_src[:], ACT.Relu,
                                                 bias=one_col, scale=-2.0).then_inc(src_made.sem, 1)

                        src_one_hots(0, 0, 0)
                        with act.Fori(0, BLOCKS) as b:
                            t0, t1_ = tiles_of(act, ends, half, b)
                            _, _, _, number0 = four(act, regs[0], quads, t0)
                            first_bank, _, visits, number1 = four(act, regs[1], quads, t1_)
                            with act.If(number0 + 1 < number1):
                                with act.Fori(number0 + 1, number1) as number:
                                    src_one_hots(nc.s_assert_within(t0 + (number - number0) * QUAD, min_val=0, max_val=HT), b, number)
                            act.sem_inc(passed.sem)
                            src_one_hots(t1_, b + 1, number1)
                            act.wait_ge(dst_used.sem, visits + first_bank + VR)
                            for bank in range(BANKS):
                                w = min(BANK, NODES - bank * BANK)
                                nc.scalar.copy(adj_t[:, bass.ds(b * NODES + bank * BANK, w)],
                                               psum[0:LO, bank * BANK:bank * BANK + w]).then_inc(banks_free.sem, 1)
                        act.wait_ge(banks_free.sem, BANKS * (BLOCKS + 1))

                    if half == 0:
                        @block.sync
                        def _(sp):
                            with sp.Fori(0, STEPS) as k:
                                for u in range(2):
                                    sp.wait_ge(st_sent[u].sem, k * (16 * SCATTER) + 16 * SCATTER * STEPS)
                                    sp.sem_inc(passed.sem)
                                    sp.dma_start(st_row[u][:], out_row_d[:, bass.ds(k * (2 * SCATTER) + u * SCATTER, SCATTER)]
                                                 ).then_inc(out_staged[u].sem, 16)
                                    sp.dma_start(st_rec[u][:].rearrange("p c w -> p (c w)"),
                                                 out_rec_d[:, bass.ds(k * (8 * SCATTER) + u * (4 * SCATTER), 4 * SCATTER)]
                                                 ).then_inc(out_staged[u].sem, 16)

                        @block.gpsimd
                        def _(pool):
                            with pool.Fori(0, STEPS) as k:
                                for u in range(2):
                                    pool.wait_ge(out_staged[u].sem, k * 32 + 32)
                                    pool.sem_inc(passed.sem)
                                    for c in range(SCATTER):
                                        nc.gpsimd.indirect_dma_start(
                                            rec_d[1], bass.IndirectOffsetOnAxis(ap=st_row[u][:, c:c + 1], axis=0),
                                            st_rec[u][:, c, :], None).then_inc(st_sent[u].sem, 16)
                            for u in range(2):
                                pool.wait_ge(st_sent[u].sem, 2 * 16 * SCATTER * STEPS)
                    else:
                        @block.sync
                        def _(sp):
                            with sp.Fori(0, BLOCKS) as b:
                                sp.wait_ge(banks_free.sem, b * BANKS + 2 * BANKS)
                                sp.dma_start(adj_d[:, bass.ds(b * NODES, NODES)],
                                             adj_t[:, bass.ds(b * NODES, NODES)]).then_inc(kept.sem, 16)
                            sp.wait_ge(kept.sem, 16 * BLOCKS + 16)

        def count_left():
            with ExitStack() as t2:
                oh_dst = sb("left_oh_dst", [P, BANKS * BANK], BF16, t2)
                oh_src = sb("left_oh_src", [P, LO], BF16, t2)
                left = sb("left", [LO, BANK], BF16, t2)
                made, used, free, kept = (signal(n) for n in ("left_oh_made", "left_oh_used", "left_free", "left_kept"))

                def if_wanted(eng, part):
                    with eng.If(eng.value_load(extra_i[0:1, 0:1], min_val=0, max_val=1) != 0):
                        part(eng)
                    eng.sem_inc(passed.sem)

                def over_tiles(eng, b, step):
                    for half in range(2):
                        others = first_tile(eng, 1, b) if half == 0 else first_tile(eng, 0, b + 1)
                        with eng.Fori(first_tile(eng, half, b), first_tile(eng, half, b + 1)) as t:
                            step(t + half * HT, t + others)

                def dve_part(dve):
                    dve.sem_inc(used.sem)
                    dve.sem_inc(kept.sem, 16)
                    dve.sem_inc(free.sem, BANKS)
                    with dve.Fori(0, BLOCKS) as b:
                        def one_hots(t, n):
                            dve.wait_ge(used.sem, n + 1)
                            dve.sem_inc(passed.sem)
                            nc.vector.tensor_scalar(oh_src[:], iota16[:, bass.ds(b * LO, LO)], key_s[:, bass.ds(t, 1)],
                                                    None, ALU.is_equal)
                            nc.vector.tensor_scalar(oh_dst[:], iota16[:], dst_s[:, bass.ds(t, 1)], None,
                                                    ALU.is_equal).then_inc(made.sem, 1)
                        over_tiles(dve, b, one_hots)
                        dve.wait_ge(used.sem, first_tile(dve, 0, b + 1) + first_tile(dve, 1, b + 1) + 1)
                        for bank in range(BANKS):
                            w = min(BANK, NODES - bank * BANK)
                            dve.wait_ge(kept.sem, b * (16 * BANKS) + 16 * (bank + 1))
                            dve.sem_inc(passed.sem)
                            nc.vector.tensor_tensor(left[:, 0:w], psum[0:LO, bank * BANK:bank * BANK + w],
                                                    adj_t[:, bass.ds(b * NODES + bank * BANK, w)],
                                                    ALU.subtract).then_inc(free.sem, 1)

                def pe_part(pe):
                    with pe.Fori(0, BLOCKS) as b:
                        for bank in range(BANKS):
                            pe.wait_ge(free.sem, b * BANKS + bank + 1)
                            nc.tensor.matmul(psum[0:LO, bank * BANK:(bank + 1) * BANK], zeros[:], zeros[:, 0:1].to_broadcast([P, BANK]),
                                             start=True, stop=False, skip_group_check=True)

                        def count(t, n):
                            pe.wait_ge(made.sem, n + 1)
                            pe.sem_inc(passed.sem)
                            for bank in range(BANKS):
                                mm = nc.tensor.matmul(psum[0:LO, bank * BANK:(bank + 1) * BANK], oh_src[:],
                                                      oh_dst[:, bank * BANK:(bank + 1) * BANK],
                                                      start=False, stop=False, skip_group_check=True)
                            mm.then_inc(used.sem, 1)
                        over_tiles(pe, b, count)

                def sp_part(sp):
                    with sp.Fori(0, BLOCKS) as b:
                        for bank in range(BANKS):
                            w = min(BANK, NODES - bank * BANK)
                            sp.wait_ge(free.sem, b * BANKS + (BANKS + 1 + bank))
                            sp.sem_inc(passed.sem)
                            sp.dma_start(left_d[:, bass.ds(b * NODES + bank * BANK, w)], left[:, 0:w]).then_inc(kept.sem, 16)
                            sp.wait_ge(kept.sem, b * (16 * BANKS) + 16 * (bank + 2))
                            sp.sem_inc(passed.sem)

                with nc.Block() as block:
                    @block.vector
                    def _(dve):
                        if_wanted(dve, dve_part)

                    @block.tensor
                    def _(pe):
                        if_wanted(pe, pe_part)

                    @block.sync
                    def _(sp):
                        if_wanted(sp, sp_part)

        sorted_tables(0)
        adj_t = sb("adj", [LO, BLOCKS * NODES], BF16, adj_stack)
        counting = ExitStack()
        iota16 = sb("iota16", [P, BANKS * BANK], I16, counting)
        zeros = sb("zeros", [P, LO], BF16, counting)
        ident_b = sb("ident_b", [LO, LO], BF16, counting)
        out_staged = [signal(f"out_staged{u}") for u in range(2)]
        with nc.Block() as block:
            @block.gpsimd
            def _(pool):
                nc.gpsimd.iota(iota16[:], pattern=[[1, BANKS * BANK]], base=0,
                               channel_multiplier=0).then_inc(pool_step.sem, 1)
                pool.wait_ge(pool_step.sem, pool_step.base + 1)

            @block.vector
            def _(dve):
                link = Chain(dve, vec)
                link(nc.vector.memset(zeros[:], 0.0))
                link(nc.vector.tensor_copy(ident_b[:], ident[0:LO, 0:LO]))
                link.close()
        pool_step.base += 1
        count_half(0)
        sorted_tables(1)
        count_half(1)
        count_left()
        counting.close()

        adj = adj_t[:].rearrange("p (s l h) -> p s h l", s=BLOCKS, h=BLOCKS)

        left_in, left_made, left_summed, left_added = (signal(n) for n in ("left_in", "left_made", "left_summed", "left_added"))
        agg_done, agg_out = signal("agg_done"), signal("agg_out")
        staged, turned, copied = signal("dense_staged"), signal("turned"), signal("copied")
        projected, evacuated = signal("projected"), signal("evacuated")
        with nc.Block() as block:
            @block.vector
            def _(dve):
                for s in (agg_out, turned, copied, projected, evacuated, left_added):
                    dve.sem_inc(s.sem)
                    s.base = 1

        def aggregate(c, h, res, room=None):
            parts = sb("agg_parts", [LO, BLOCKS, 3 * D], BF16, c)
            room = sb("agg_left", [LO, BLOCKS * D], F32, c)[:] if room is None else room
            left = room.bitcast(BF16)
            rem = room.rearrange("p (s f) -> p s f", s=BLOCKS)
            left_sum = sb("agg_left_sum", [LO, D], F32, c)
            with nc.Block() as block:
                @block.vector
                def _(dve):
                    link = Chain(dve, vec)
                    v = nc.vector
                    link(v.tensor_copy(parts[:, :, 0:D], h))
                    link(v.tensor_tensor(rem, h, parts[:, :, 0:D], ALU.subtract))
                    link(v.tensor_copy(parts[:, :, D:2 * D], rem))
                    link(v.tensor_tensor(parts[:, :, 2 * D:3 * D], rem, parts[:, :, D:2 * D], ALU.subtract))
                    link.close()

            with nc.Block() as block:
                @block.tensor
                def _(pe):
                    with pe.Fori(0, BLOCKS // BLOCKS5) as i:
                        pe.wait_ge(agg_out.sem, i * BLOCKS5 + agg_out.base)
                        for k in range(BLOCKS5):
                            for s in range(BLOCKS):
                                mm = nc.tensor.matmul(psum[0:LO, k * BANK:k * BANK + 3 * D],
                                                      adj[:, s, bass.ds(i * BLOCKS5 + k, 1), :].rearrange("p a l -> p (a l)"),
                                                      parts[:, s, :],
                                                      start=(s == 0), stop=(s == BLOCKS - 1))
                            mm.then_inc(agg_done.sem, 1)

                @block.vector
                def _(dve):
                    with dve.Fori(0, BLOCKS // BLOCKS5) as i:
                        for k in range(BLOCKS5):
                            dve.wait_ge(agg_done.sem, i * BLOCKS5 + k + 1 + agg_done.base)
                            nc.vector.tensor_reduce(
                                res[:, bass.ds(i * BLOCKS5 + k, 1), :].rearrange("p a f -> p (a f)"),
                                psum[0:LO, k * BANK:k * BANK + 3 * D].rearrange("p (c f) -> p f c", c=3),
                                AX.X, ALU.add).then_inc(agg_out.sem, 1)
                    dve.wait_ge(agg_out.sem, agg_out.base + BLOCKS)
            agg_done.base += BLOCKS
            agg_out.base += BLOCKS

            with nc.Block() as block:
                @block.sync
                def _(sp):
                    with sp.If(sp.value_load(extra_i[0:1, 0:1], min_val=0, max_val=1) != 0):
                        with sp.Fori(0, BLOCKS) as s:
                            sp.wait_ge(left_added.sem, s * BLOCKS + left_added.base)
                            sp.sem_inc(passed.sem)
                            sp.dma_start(left[:, 0:NODES], left_d[:, bass.ds(s * NODES, NODES)]).then_inc(left_in.sem, 16)
                    sp.sem_inc(passed.sem)


                @block.tensor
                def _(pe):
                    with pe.If(pe.value_load(extra_i[0:1, 0:1], min_val=0, max_val=1) != 0):
                        with pe.Fori(0, BLOCKS) as s:
                            pe.wait_ge(left_in.sem, s * 16 + 16 + left_in.base)
                            pe.sem_inc(passed.sem)
                            with pe.Fori(0, BLOCKS) as i:
                                pe.wait_ge(left_added.sem, s * BLOCKS + i + left_added.base)
                                nc.tensor.matmul(psum[0:LO, 0:3 * D],
                                                 left[:, 0:NODES].rearrange("p (l h) -> p h l", h=BLOCKS)[:, bass.ds(i, 1), :].rearrange("p a l -> p (a l)"),
                                                 parts[:, bass.ds(s, 1), :].rearrange("p a f -> p (a f)"),
                                                 start=True, stop=True).then_inc(left_made.sem, 1)
                    pe.sem_inc(passed.sem)


                @block.vector
                def _(dve):
                    with dve.If(dve.value_load(extra_i[0:1, 0:1], min_val=0, max_val=1) != 0):
                        with dve.Fori(0, BLOCKS) as s:
                            with dve.Fori(0, BLOCKS) as i:
                                dve.wait_ge(left_made.sem, s * BLOCKS + i + 1 + left_made.base)
                                nc.vector.tensor_reduce(left_sum[:], psum[0:LO, 0:3 * D].rearrange("p (c f) -> p f c", c=3),
                                                        AX.X, ALU.add).then_inc(left_summed.sem, 1)
                                dve.wait_ge(left_summed.sem, s * BLOCKS + i + 1 + left_summed.base)
                                at = res[:, bass.ds(i, 1), :].rearrange("p a f -> p (a f)")
                                nc.vector.tensor_tensor(at, at, left_sum[:], ALU.add).then_inc(left_added.sem, 1)
                                dve.wait_ge(left_added.sem, s * BLOCKS + i + 1 + left_added.base)
                    dve.sem_inc(passed.sem)
            left_in.base += 16 * BLOCKS
            for s in (left_added, left_made, left_summed):
                s.base += BLOCKS * BLOCKS

        def project(ins, K, ws, res, M):
            C = len(ins)
            with ExitStack() as c:
                stage = sb("stage", [LO, C, BLOCKS5, K], F32, c)
                turn = sb("turn", [K, BLOCKS5, C * LO], F32, c)
                with nc.Block() as block:
                    @block.scalar
                    def _(act):
                        with act.Fori(0, BLOCKS // BLOCKS5) as i:
                            for k in range(BLOCKS5):
                                act.wait_ge(turned.sem, i * BLOCKS5 + k + 1 + turned.base)
                                act.wait_ge(projected.sem, i * BLOCKS5 + projected.base)
                                nc.scalar.copy(turn[:, k, :], psum[0:K, k * BANK:k * BANK + C * LO]).then_inc(copied.sem, 1)

                    @block.tensor
                    def _(pe):
                        with pe.Fori(0, BLOCKS // BLOCKS5) as i:
                            pe.wait_ge(staged.sem, i * C + C + staged.base)
                            pe.wait_ge(copied.sem, i * BLOCKS5 + copied.base)
                            pe.sem_inc(passed.sem)
                            for k in range(BLOCKS5):
                                for n in range(C):
                                    mm = nc.tensor.transpose(psum[0:K, k * BANK + n * LO:k * BANK + (n + 1) * LO],
                                                             stage[:, n, k, :], ident[0:LO, 0:LO])
                                mm.then_inc(turned.sem, 1)
                            pe.wait_ge(evacuated.sem, i + evacuated.base)
                            for k in range(BLOCKS5):
                                pe.wait_ge(copied.sem, i * BLOCKS5 + k + 1 + copied.base)
                                for n in range(C):
                                    mm = nc.tensor.matmul(psum[0:LO, 5 * BANK + k * P:5 * BANK + k * P + M],
                                                          turn[:, k, n * LO:(n + 1) * LO], ws[n],
                                                          start=(n == 0), stop=(n == C - 1))
                                mm.then_inc(projected.sem, 1)

                    @block.vector
                    def _(dve):
                        def fill(i):
                            for n in range(C):
                                nc.vector.tensor_copy(stage[:, n, :, :], ins[n][:, bass.ds(i * BLOCKS5, BLOCKS5), :]
                                                      ).then_inc(staged.sem, 1)

                        def empty_out(i):
                            dve.wait_ge(projected.sem, i * BLOCKS5 + BLOCKS5 + projected.base)
                            nc.vector.tensor_copy(
                                res[:, bass.ds(i * BLOCKS5, BLOCKS5), :],
                                psum[0:LO, 5 * BANK:5 * BANK + BLOCKS5 * P].rearrange("p (k m) -> p k m", m=P)[:, :, 0:M],
                            ).then_inc(evacuated.sem, 1)
                        fill(0)
                        with dve.Fori(0, BLOCKS // BLOCKS5 - 1) as i:
                            dve.wait_ge(turned.sem, i * BLOCKS5 + BLOCKS5 + turned.base)
                            fill(i + 1)
                            empty_out(i)
                        empty_out(BLOCKS // BLOCKS5 - 1)
                        dve.wait_ge(evacuated.sem, evacuated.base + BLOCKS // BLOCKS5)
            turned.base += BLOCKS
            copied.base += BLOCKS
            projected.base += BLOCKS
            staged.base += C * (BLOCKS // BLOCKS5)
            evacuated.base += BLOCKS // BLOCKS5

        def over_nodes(v, m):
            return v.rearrange("p (a m) -> p a m", a=1).to_broadcast([LO, BLOCKS, m])

        def over_features(v, m):
            return v.rearrange("p (b a) -> p b a", a=1).to_broadcast([LO, BLOCKS, m])

        def vector_steps(steps):
            with nc.Block() as block:
                @block.vector
                def _(dve):
                    link = Chain(dve, vec)
                    steps(nc.vector, link)
                    link.close()

        def scalar_step(step):
            with nc.Block() as block:
                @block.scalar
                def _(act):
                    link = Chain(act, act_step)
                    link(step())
                    link.close()

        def load_all(pairs):
            with nc.Block() as block:
                @block.sync
                def _(sp):
                    for dst, src in pairs:
                        sp.dma_start(dst, src).then_inc(load.sem, 16)
                    sp.wait_ge(load.sem, load.base + 16 * len(pairs))
            load.base += 16 * len(pairs)

        def store_all(pairs):
            with nc.Block() as block:
                @block.sync
                def _(sp):
                    for dst, src in pairs:
                        sp.dma_start(dst, src).then_inc(store.sem, 16)
                    sp.wait_ge(store.sem, store.base + 16 * len(pairs))
            store.base += 16 * len(pairs)

        def row(name, n):
            return a[name].rearrange("(a n) -> a n", a=1).to_broadcast([LO, n])

        def inverse_roots(c, name, vectors):
            roots = [sb(name, list(v.shape), F32, c) for v in vectors]
            with nc.Block() as block:
                @block.scalar
                def _(act):
                    for v, root in zip(vectors, roots):
                        nc.scalar.activation(root[:], v, ACT.Sqrt).then_inc(act_step.sem, 1)

                @block.vector
                def _(dve):
                    link = Chain(dve, vec)
                    for n, (v, root) in enumerate(zip(vectors, roots)):
                        dve.wait_ge(act_step.sem, act_step.base + n + 1)
                        link(nc.vector.reciprocal(v, root[:]))
                    link.close()
            act_step.base += len(vectors)

        def inverse_root(c, name, v):
            inverse_roots(c, name, [v])

        def layer_norm(y):
            with ExitStack() as c:
                mean = sb("ln_mean", [LO, BLOCKS], F32, c)
                var = sb("ln_var", [LO, BLOCKS], F32, c)
                sq = sb("ln_sq", [LO, BLOCKS, D], F32, c)

                def center(v, link):
                    link(v.tensor_tensor(x[:], x[:], y, ALU.add))
                    link(v.tensor_reduce(mean[:], x[:], AX.X, ALU.add))
                    link(v.tensor_scalar(mean[:], mean[:], 1.0 / D, None, ALU.mult))
                    link(v.tensor_tensor(x[:], x[:], over_features(mean[:], D), ALU.subtract))
                    link(v.tensor_tensor(sq[:], x[:], x[:], ALU.mult))
                    link(v.tensor_reduce(var[:], sq[:], AX.X, ALU.add))
                    link(v.tensor_scalar(var[:], var[:], 1.0 / D, EPS, ALU.mult, ALU.add))
                vector_steps(center)
                inverse_root(c, "ln_root", var[:])
                vector_steps(lambda v, link: link(v.tensor_tensor(x[:], x[:], over_features(var[:], D), ALU.mult)))

        def batch_norm(y, m, gamma, beta):
            with ExitStack() as c:
                part_sum = sb("bn_part", [LO, m], F32, c)
                stat = sb("bn_stat", [LO, m], F32, c)
                sq = sb("bn_sq", [LO, BLOCKS, m], F32, c)

                def total(src, finish):
                    vector_steps(lambda v, link: link(v.tensor_reduce(part_sum[:], src.rearrange("p b m -> p m b"), AX.X, ALU.add)))
                    with nc.Block() as block:
                        @block.tensor
                        def _(pe):
                            nc.tensor.matmul(psum[0:LO, 0:m], ones_f[0:LO, 0:LO], part_sum[:],
                                             start=True, stop=True).then_inc(pe_step.sem, 1)

                        @block.vector
                        def _(dve):
                            dve.wait_ge(pe_step.sem, pe_step.base + 1)
                            link = Chain(dve, vec)
                            finish(nc.vector, link)
                            link.close()
                    pe_step.base += 1

                def center(v, link):
                    link(v.tensor_scalar(stat[:], psum[0:LO, 0:m], 1.0 / NODES, None, ALU.mult))
                    link(v.tensor_tensor(y, y, over_nodes(stat[:], m), ALU.subtract))
                    link(v.tensor_tensor(sq[:], y, y, ALU.mult))
                total(y, center)
                total(sq[:], lambda v, link: link(v.tensor_scalar(stat[:], psum[0:LO, 0:m], 1.0 / NODES, EPS, ALU.mult, ALU.add)))
                inverse_root(c, "bn_root", stat[:])

                def scale(v, link):
                    link(v.tensor_tensor(stat[:], stat[:], gamma, ALU.mult))
                    link(v.tensor_tensor(y, y, over_nodes(stat[:], m), ALU.mult))
                    link(v.tensor_tensor(y, y, over_nodes(beta, m), ALU.add))
                vector_steps(scale)

        with ExitStack() as c:
            vectors = ["b1", "g1", "be1", "rm1", "rv1", "b2", "g2", "be2", "rm2", "rv2"]
            vs = sb("l0_vectors", [LO, len(vectors), D], F32, c)
            w = sb("l0_w", [D, 2, D], F32, c)
            load_all([(x[:].rearrange("p b f -> p (b f)"), a["x"].rearrange("(p b) f -> p (b f)", b=BLOCKS))]
                     + [(vs[:, i, :], row(f"L0_gnn_{n}", D)) for i, n in enumerate(vectors)]
                     + [(w[:, i, :], a[f"L0_gnn_W{i + 1}"]) for i in range(2)])
            at = {n: vs[:, i, :] for i, n in enumerate(vectors)}
            vector_steps(lambda v, link: (link(v.tensor_scalar(dinv[:], deg_in[:], 1.0, None, ALU.add)),
                                          link(v.tensor_scalar(at["rv1"], at["rv1"], EPS, None, ALU.add)),
                                          link(v.tensor_scalar(at["rv2"], at["rv2"], EPS, None, ALU.add))))
            inverse_roots(c, "l0_root", [dinv[:], at["rv1"], at["rv2"]])
            h = sb("l0_h", [LO, BLOCKS, D], F32, c)
            y = sb("l0_y", [LO, BLOCKS, D], F32, c)
            vector_steps(lambda v, link: link(v.tensor_copy(h[:], x[:])))
            for i in (1, 2):
                with ExitStack() as c2:
                    vector_steps(lambda v, link: link(v.tensor_tensor(h[:], h[:], over_features(dinv[:], D), ALU.mult)))
                    aggregate(c2, h[:], y[:])
                    vector_steps(lambda v, link: (link(v.tensor_tensor(y[:], y[:], h[:], ALU.add)),
                                                  link(v.tensor_tensor(y[:], y[:], over_features(dinv[:], D), ALU.mult))))
                project([y[:]], D, [w[:, i - 1, :]], h[:], D)

                def norm(v, link, i=i):
                    link(v.tensor_tensor(at[f"g{i}"], at[f"g{i}"], at[f"rv{i}"], ALU.mult))
                    link(v.tensor_tensor(at[f"b{i}"], at[f"b{i}"], at[f"rm{i}"], ALU.subtract))
                    link(v.tensor_tensor(at[f"b{i}"], at[f"b{i}"], at[f"g{i}"], ALU.mult))
                    link(v.tensor_tensor(at[f"b{i}"], at[f"b{i}"], at[f"be{i}"], ALU.add))
                    link(v.tensor_tensor(h[:], h[:], over_nodes(at[f"g{i}"], D), ALU.mult))
                    link(v.tensor_tensor(h[:], h[:], over_nodes(at[f"b{i}"], D), ALU.add))
                    if i == 1:
                        link(v.tensor_scalar(h[:], h[:], 0.0, None, ALU.max))
                vector_steps(norm)
            top = sb("l0_top", [LO, BLOCKS], F32, c)
            total = sb("l0_total", [LO, BLOCKS], F32, c)
            vector_steps(lambda v, link: (link(v.tensor_reduce(top[:], h[:], AX.X, ALU.max)),
                                          link(v.tensor_tensor(h[:], h[:], over_features(top[:], D), ALU.subtract))))
            scalar_step(lambda: nc.scalar.activation(y[:], h[:], ACT.Exp))
            vector_steps(lambda v, link: link(v.tensor_reduce(total[:], y[:], AX.X, ALU.add)))
            scalar_step(lambda: nc.scalar.activation(top[:], total[:], ACT.Ln))
            vector_steps(lambda v, link: link(v.tensor_tensor(h[:], h[:], over_features(top[:], D), ALU.subtract)))
            layer_norm(h[:])

        with ExitStack() as c:
            w1 = sb("l1_w1", [D, 2, 2 * D], F32, c)
            w2 = sb("l1_w2", [2 * D, D], F32, c)
            b1 = sb("l1_b1", [LO, 2 * D], F32, c)
            b2 = sb("l1_b2", [LO, D], F32, c)
            load_all([(w1[:], a["L1_gnn_W1"].rearrange("(c k) m -> k c m", c=2)), (w2[:], a["L1_gnn_W2"]),
                      (b1[:], row("L1_gnn_b1", 2 * D)), (b2[:], row("L1_gnn_b2", D))])
            y = sb("l1_y", [LO, BLOCKS, D], F32, c)
            with ExitStack() as c2:
                aggregate(c2, x[:], y[:])
            hid = sb("l1_hid", [LO, BLOCKS, 2 * D], F32, c)
            project([x[:], y[:]], D, [w1[:, 0, :], w1[:, 1, :]], hid[:], 2 * D)
            vector_steps(lambda v, link: (link(v.tensor_tensor(hid[:], hid[:], over_nodes(b1[:], 2 * D), ALU.add)),
                                          link(v.tensor_scalar(hid[:], hid[:], 0.0, None, ALU.max))))
            project([hid[:]], 2 * D, [w2[:]], y[:], D)
            vector_steps(lambda v, link: link(v.tensor_tensor(y[:], y[:], over_nodes(b2[:], D), ALU.add)))
            layer_norm(y[:])
        adj_stack.close()

        with ExitStack() as c:
            some = sb("some", [LO, BLOCKS, 2], F32, c)
            deg3 = deg_half[:].rearrange("p (h b) -> p b h", h=2)
            vector_steps(lambda v, link: (link(v.tensor_scalar(some[:], deg3, 0.0, None, ALU.is_gt)),
                                          link(v.tensor_scalar(dinv_half[:], deg3, 1.0, None, ALU.max))))
            inverse_root(c, "half_root", dinv_half[:])
            vector_steps(lambda v, link: link(v.tensor_tensor(dinv_half[:], dinv_half[:], some[:], ALU.mult)))

        RING = 4
        gathered = [signal(f"gathered{u}") for u in range(RING)]
        typed = [signal(f"typed{u}") for u in range(RING)]
        idx_ready, oh_t_made, oh_s_made = signal("idx_ready"), signal("oh_t_made"), signal("oh_s_made")
        rel_done, mult_done, prod_done = signal("rel_done"), signal("mult_done"), signal("prod_done")
        scat_done, squared, zeroed = signal("scat_done"), signal("squared"), signal("zeroed")
        TURNS = GROUPS // RING

        def edge_pass(d, acc, rel_parts):
            W = 3 * d // 2
            RS = 2 * d
            RB = GROUP * RS
            with ExitStack() as c:
                gi = [sb(f"gi{u}", [P, GROUP], I32, c) for u in range(RING)]
                gx = [sb(f"gx{u}", [P, GROUP, d], F32, c) for u in range(RING)]
                tb = [sb(f"tb{u}", [P, GROUP * P], BF16, c) for u in range(RING)]
                oh_t = [sb(f"oh_t{u}", [P, GROUP * P], BF16, c) for u in range(2)]
                oh_s = [sb(f"oh_s{u}", [P, GROUP, LO], F32, c) for u in range(2)]
                part_prod = sb("part_prod", [P, GROUP, 2, d], F32, c)
                zero_f = sb("zero_f", [P, LO], F32, c)
                sq_s = sb("sq_s", [P, GROUP, LO], F32, c)
                prod = [sb(f"prod{u}", [P, GROUP, d], F32, c) for u in range(2)]
                ps_rel = [psum[:, u * RB:(u + 1) * RB] for u in range(2)]
                ps_out = [psum[0:LO, 2 * RB + u * BANK:2 * RB + u * BANK + GROUP * d] for u in range(2)]
                types = typ_d.rearrange("(a t) p -> a (t p)", a=1)
                acc2 = acc.rearrange("p k f -> p (k f)")
                with nc.Block() as block:
                    @block.gpsimd
                    def _(pool):
                        with pool.Fori(0, TURNS) as i:
                            for u in range(RING):
                                g1 = i * RING + (u + 1)
                                pool.wait_ge(mult_done.sem, g1 + mult_done.base)
                                pool.wait_ge(idx_ready.sem, g1 + idx_ready.base)
                                pool.sem_inc(passed.sem)
                                for k in range(GROUP):
                                    nc.gpsimd.indirect_dma_start(
                                        gx[u][:, k, :], None, table_d[d],
                                        bass.IndirectOffsetOnAxis(ap=gi[u][:, k:k + 1], axis=0),
                                    ).then_inc(gathered[u].sem, 16)

                    @block.scalar
                    def _(act):
                        def indices(u, at):
                            nc.scalar.copy(gi[u][:], gidx_s[:, bass.ds(at, GROUP)]).then_inc(idx_ready.sem, 1)

                        def src_one_hot(at, u, n):
                            for k in range(GROUP):
                                if k == 0:
                                    act.wait_ge(scat_done.sem, n + scat_done.base)
                                    act.wait_ge(oh_s_made.sem, n + oh_s_made.base)
                                sq = nc.scalar.activation(sq_s[:, k, :], iota[:, 0:LO], ACT.Square,
                                                          bias=lo_s[:, bass.ds(at + k, 1)], scale=-1.0)
                            sq.then_inc(squared.sem, 1)
                            act.wait_ge(squared.sem, n + squared.base)
                            nc.scalar.activation(oh_s[u % 2][:], sq_s[:], ACT.Relu, bias=one_col,
                                                 scale=-2.0).then_inc(oh_s_made.sem, 1)
                        act.sem_inc(oh_s_made.sem)
                        act.sem_inc(scat_done.sem)
                        for u in range(RING):
                            indices(u, u * GROUP)

                        def ahead(u, turn):
                            w = (u + 2) % RING
                            act.wait_ge(gathered[w].sem, (turn + u // 2) * (16 * GROUP) + gathered[w].base)
                            indices(w, turn * (RING * GROUP) + (u + 2) * GROUP)

                        for u in range(RING):
                            if u >= 2:
                                ahead(u, 0)
                            src_one_hot(u * GROUP, u, u + 1)
                        with act.Fori(1, TURNS) as i:
                            for u in range(RING):
                                ahead(u, i)
                                src_one_hot(i * (RING * GROUP) + u * GROUP, u, i * RING + (u + 1))

                    @block.sync
                    def _(sp):
                        def types_of(at, u, n):
                            sp.wait_ge(oh_t_made.sem, n)
                            sp.dma_start(tb[u][:], types[:, bass.ds(at, GROUP * P)].to_broadcast([P, GROUP * P])).then_inc(typed[u].sem, 16)
                        with sp.Fori(0, TURNS) as i:
                            for u in range(RING):
                                types_of(i * (RING * GROUP * P) + u * GROUP * P, u, i * RING + (u + 1) + oh_t_made.base)
                        for u in range(2):
                            types_of((GROUPS + u) * GROUP * P, u, GROUPS + u + 1 + oh_t_made.base)

                    @block.vector
                    def _(dve):
                        link = Chain(dve, vec)
                        v = nc.vector
                        dve.sem_inc(mult_done.sem, RING)
                        dve.sem_inc(prod_done.sem)
                        dve.sem_inc(oh_t_made.sem, RING)

                        def type_one_hot(u, n):
                            dve.wait_ge(typed[u].sem, n * 16 + 16 + typed[u].base)
                            v.tensor_scalar(oh_t[u % 2][:], tb[u][:], part, None, ALU.is_equal).then_inc(oh_t_made.sem, 1)

                        def add(bucket, u, k):
                            to = acc2[:, bass.ds(bucket * d, d)]
                            link(v.tensor_tensor(to, to, ps_out[u % 2][:, k * d:(k + 1) * d], ALU.add))

                        link(v.memset(acc, 0.0))
                        v.memset(zero_f[:], 0.0).then_inc(zeroed.sem, 1)
                        type_one_hot(0, 0)
                        type_one_hot(1, 0)
                        regs = [[dve.alloc_register(f"bucket{d}_{u}_{k}") for k in range(GROUP)] for u in range(RING)]

                        def load_buckets(u, first):
                            dve.load(regs[u], bucket_r[0:1, bass.ds(first, GROUP)])
                            return [dve.snap(r, min_val=0, max_val=BUCKETS - 1) for r in regs[u]]

                        with dve.Fori(0, TURNS) as i:
                            link.turn = i * (RING * GROUP)
                            for u in range(RING):
                                g1 = i * RING + (u + 1)
                                dve.wait_ge(rel_done.sem, g1 + rel_done.base)

                                type_one_hot((u + 2) % RING, i + (u + 2) // RING)
                                dve.wait_ge(gathered[u].sem, i * (16 * GROUP) + 16 * GROUP + gathered[u].base)
                                dve.wait_ge(prod_done.sem, g1 + prod_done.base)
                                rel = ps_rel[u % 2].rearrange("p (g w) -> p g w", w=RS)
                                for s in range(2):
                                    mul = v.tensor_tensor(
                                        part_prod[:, :, s, :].rearrange("p g (a f) -> p g a f", a=2),
                                        gx[u][:, :, s * d // 2:(s + 1) * d // 2].rearrange("p g (a f) -> p g a f", a=1).to_broadcast([P, GROUP, 2, d // 2]),
                                        rel[:, :, s * d // 2:s * d // 2 + d].rearrange("p g (a f) -> p g a f", a=2),
                                        ALU.mult)
                                mul.then_inc(mult_done.sem, 1)
                                buckets = load_buckets(u, i * (RING * GROUP) + u * GROUP)

                                def add_last(k):
                                    add(buckets[k], u + 1, k)

                                dve.wait_ge(scat_done.sem, g1 + 1 + scat_done.base)
                                add_last(0)
                                dve.wait_ge(mult_done.sem, g1 + RING + mult_done.base)
                                v.tensor_tensor(prod[u % 2][:], part_prod[:, :, 0, :], part_prod[:, :, 1, :],
                                                ALU.add).then_inc(prod_done.sem, 1)
                                add_last(1)
                                add_last(2)
                                add_last(3)
                        link.turn = 0
                        link.n += (TURNS - 1) * RING * GROUP
                        buckets = load_buckets(0, TURNS * RING * GROUP)
                        dve.wait_ge(scat_done.sem, GROUPS + 2 + scat_done.base)
                        for k in range(GROUP):
                            add(buckets[k], RING - 1, k)
                        link.close()

                    @block.tensor
                    def _(pe):
                        def relations(u, n, free):
                            pe.wait_ge(oh_t_made.sem, n + RING + oh_t_made.base)
                            pe.wait_ge(mult_done.sem, free)
                            for k in range(GROUP):
                                for s in range(3):
                                    mm = nc.tensor.matmul(ps_rel[u % 2][:, k * RS:k * RS + W], oh_t[u % 2][:, k * P:(k + 1) * P],
                                                          rel_parts[:, s, :], start=(s == 0), stop=(s == 2))
                            mm.then_inc(rel_done.sem, 1)

                        for u in range(2):
                            relations(u, u + 1, RING + mult_done.base)
                        pe.wait_ge(zeroed.sem, 1 + zeroed.base)
                        for k in range(GROUP):
                            mm = nc.tensor.matmul(ps_out[1][:, k * d:(k + 1) * d], zero_f[:], zero_f[:, 0:1].to_broadcast([P, d]),
                                                  start=True, stop=True)
                        mm.then_inc(scat_done.sem, 1)
                        with pe.Fori(0, TURNS) as i:
                            for u in range(RING):
                                g1 = i * RING + (u + 1)
                                pe.wait_ge(oh_s_made.sem, g1 + 1 + oh_s_made.base)
                                pe.wait_ge(prod_done.sem, g1 + 1 + prod_done.base)
                                for k in range(GROUP):
                                    mm = nc.tensor.matmul(ps_out[u % 2][:, k * d:(k + 1) * d], oh_s[u % 2][:, k, :],
                                                          prod[u % 2][:, k, :], start=True, stop=True)
                                mm.then_inc(scat_done.sem, 1)
                                relations(u % 2, g1 + 2, g1 + RING + mult_done.base)
            for s, n in ((mult_done, GROUPS + RING), (oh_t_made, GROUPS + 2 + RING), (oh_s_made, GROUPS + 1), (squared, GROUPS), (zeroed, 1),
                         (idx_ready, GROUPS + 2), (rel_done, GROUPS + 2), (prod_done, GROUPS + 1), (scat_done, GROUPS + 2),
                         (typed[0], 16), (typed[1], 16)):
                s.base += n
            for u in range(RING):
                gathered[u].base += 16 * GROUP * TURNS
                typed[u].base += 16 * TURNS

        def small_products(jobs):
            with nc.Block() as block:
                @block.tensor
                def _(pe):
                    for j, (to, lhs, rhs, turned_) in enumerate(jobs):
                        k, m = to.shape
                        where = psum[0:k, j * BANK:j * BANK + m]
                        mm = nc.tensor.transpose(where, lhs, rhs) if turned_ else \
                            nc.tensor.matmul(where, lhs, rhs, start=True, stop=True)
                        mm.then_inc(pe_step.sem, 1)

                @block.vector
                def _(dve):
                    link = Chain(dve, vec)
                    for j, (to, *_) in enumerate(jobs):
                        k, m = to.shape
                        dve.wait_ge(pe_step.sem, pe_step.base + j + 1)
                        link(nc.vector.tensor_copy(to, psum[0:k, j * BANK:j * BANK + m]))
                    link.close()
            pe_step.base += len(jobs)

        load_all([(rel[:], a["L2_gnn_init_rel"])])

        def comp_layer(c, n, d, m, feats, rel_in, res, rel_next):
            W = 3 * d // 2
            pre = f"L2_gnn_c{n}_"
            wp = sb(f"wp{n}", [d, 3, m], F32, c)
            rel_parts = sb(f"rel_parts{n}", [P, 3, W], BF16, c)
            with ExitStack() as c2:
                dftc = sb(f"dft{n}", [d, 2 * d + W], F32, c2)
                win = sb(f"w{n}", [d, 3, m], F32, c2)
                wrel = sb(f"wrel{n}", [d, m], F32, c2)
                loop_col = sb(f"loop_col{n}", [d, 1], F32, c2)
                rel_t = sb(f"rel_t{n}", [d, RELS], F32, c2)
                inv_t = sb(f"inv_t{n}", [d, d], F32, c2)
                rel_f = sb(f"rel_f{n}", [P, W], F32, c2)
                loop_f = sb(f"loop_f{n}", [LO, W], F32, c2)
                load_all([(dftc[:], a[f"const_dft{d}"]), (wrel[:], a[pre + "w_rel"]),
                          (loop_col[:], a[pre + "loop_rel"].rearrange("a (k b) -> (a k) b", b=1))]
                         + [(win[:, i, :], a[pre + w]) for i, w in enumerate(("w_in", "w_out", "w_loop"))])
                fwd, relm, inv = dftc[:, 0:d], dftc[:, d:d + W], dftc[:, d + W:2 * d + W]
                vector_steps(lambda v, link: (link(v.memset(rel_f[:], 0.0)), link(v.memset(rel_parts[:], 0.0))))
                small_products([(rel_t[:], rel_in, ident[0:RELS, 0:RELS], True),
                                (inv_t[:], inv, ident[0:d, 0:d], True),
                                (loop_f[:], loop_col[:].to_broadcast([d, LO]), relm, False)])
                jobs = [(rel_f[0:RELS, :], rel_t[:], relm, False)]
                jobs += [(wp[:, i, :], inv, win[:, i, :], False) for i in range(3)]
                if rel_next is not None:
                    jobs += [(rel_next, rel_t[:], wrel[:], False)]
                small_products(jobs)

                rem = sb(f"rel_rem{n}", [P, W], F32, c2)

                def split(v, link):
                    link(v.tensor_copy(rel_parts[:, 0, :], rel_f[:]))
                    link(v.tensor_tensor(rem[:], rel_f[:], rel_parts[:, 0, :], ALU.subtract))
                    link(v.tensor_copy(rel_parts[:, 1, :], rem[:]))
                    link(v.tensor_tensor(rel_parts[:, 2, :], rem[:], rel_parts[:, 1, :], ALU.subtract))
                vector_steps(split)
                xf = sb(f"xf{n}", [LO, BLOCKS, d], F32, c2)
                project([feats], d, [fwd], xf[:], d)
                with ExitStack() as c3:
                    sc = [sb(f"scaled{n}_{hf}", [LO, BLOCKS, d], F32, c3) for hf in range(2)]
                    with nc.Block() as block:
                        @block.vector
                        def _(dve):
                            for hf in range(2):
                                nc.vector.tensor_tensor(sc[hf][:], xf[:], over_features(dinv_half[:, :, hf], d),
                                                        ALU.mult).then_inc(vec.sem, 1)

                        @block.sync
                        def _(sp):
                            for hf in range(2):
                                sp.wait_ge(vec.sem, vec.base + hf + 1)
                                sp.dma_start(table_d[d][hf * NODES:(hf + 1) * NODES, :].rearrange("(p b) f -> p (b f)", b=BLOCKS),
                                             sc[hf][:].rearrange("p b f -> p (b f)")).then_inc(store.sem, 16)
                            sp.wait_ge(store.sem, store.base + 32)
                    vec.base += 2
                    store.base += 32
                    def loop_term(v, link):
                        half = d // 2
                        for o in range(2):
                            to = keep[:, :, o * half:(o + 1) * half]
                            for s, t in ((0, to), (1, tmp2[:])):
                                link(v.tensor_tensor(t, xf[:, :, s * half:(s + 1) * half],
                                                     over_nodes(loop_f[:, (s + o) * half:(s + o + 1) * half], half), ALU.mult))
                            link(v.tensor_tensor(to, to, tmp2[:], ALU.add))
                    tmp2 = sb(f"loop_tmp{n}", [LO, BLOCKS, d // 2], F32, c3)
                    keep = sb(f"loop_keep{n}", [LO, BLOCKS, d], F32, c3)
                    vector_steps(loop_term)
                    store_all([(loop_d[d], keep[:].rearrange("p b f -> p (b f)"))])
            acc = sb(f"acc{n}", [LO, BUCKETS, d], F32, c)
            edge_pass(d, acc[:], rel_parts)
            acc3 = acc[:].rearrange("p (h b) f -> p b h f", h=2)
            with ExitStack() as c2:
                lt = sb(f"lt{n}", [LO, BLOCKS, d], F32, c2)
                load_all([(lt[:].rearrange("p b f -> p (b f)"), loop_d[d])])
                vector_steps(lambda v, link: [link(v.tensor_tensor(acc3[:, :, hf, :], acc3[:, :, hf, :],
                                                                   over_features(dinv_half[:, :, hf], d), ALU.mult)) for hf in range(2)])
                project([acc3[:, :, 0, :], acc3[:, :, 1, :], lt[:]], d, [wp[:, i, :] for i in range(3)], res, m)

        def finish_comp(n, m, y, then_load=None):
            pre = f"L2_gnn_c{n}_"
            with ExitStack() as c:
                vb = sb(f"comp_v{n}", [LO, 3, m], F32, c)
                load_all([(vb[:, i, :], row(pre + w, m)) for i, w in enumerate(("bias", "gamma", "beta"))])
                if then_load is not None:
                    with nc.Block() as block:
                        block.sync(then_load)
                vector_steps(lambda v, link: link(v.scalar_tensor_tensor(y, y, 1.0 / 3.0, over_nodes(vb[:, 0, :], m),
                                                                         ALU.mult, ALU.add)))
                batch_norm(y, m, vb[:, 1, :], vb[:, 2, :])
                scalar_step(lambda: nc.scalar.activation(y, y, ACT.Tanh))

        with ExitStack() as c:
            y1 = sb("comp_y1", [LO, BLOCKS, 2 * D], F32, c)
            y2 = sb("comp_y2", [LO, BLOCKS, D], F32, c)
            with ExitStack() as c2:
                comp_layer(c2, 1, D, 2 * D, x[:], rel[:], y1[:], rel2[:])
            finish_comp(1, 2 * D, y1[:])
            with ExitStack() as c2:
                comp_layer(c2, 2, 2 * D, D, y1[:], rel2[:], y2[:], None)
            adj_t = sb("adj_again", [LO, BLOCKS * NODES], BF16, c)
            adj = adj_t[:].rearrange("p (s l h) -> p s h l", s=BLOCKS, h=BLOCKS)
            w = sb("l3_w", [D, D], F32, c)
            vb = sb("l3_v", [LO, 3, D], F32, c)
            again = signal("adj_again_in")

            def load_again(sp):
                sp.dma_start(adj_t[:], adj_d).then_inc(again.sem, 16)
                sp.dma_start(w[:], a["L3_gnn_W"]).then_inc(again.sem, 16)
                for i, n in enumerate(("b", "gamma", "beta")):
                    sp.dma_start(vb[:, i, :], row(f"L3_gnn_{n}", D)).then_inc(again.sem, 16)
            finish_comp(2, D, y2[:], load_again)
            layer_norm(y2[:])

            with nc.Block() as block:
                @block.sync
                def _(sp):
                    sp.wait_ge(again.sem, 16 * 5)
            sc_out = sb("l3_out", [LO, BLOCKS], F32, c)
            sc_in = sb("l3_in", [LO, BLOCKS], F32, c)
            deg3 = deg_half[:].rearrange("p (h b) -> p b h", h=2)
            vector_steps(lambda v, link: (link(v.tensor_reduce(sc_out[:], deg3, AX.X, ALU.add)),
                                          link(v.tensor_scalar(sc_out[:], sc_out[:], 1.0, None, ALU.max)),
                                          link(v.tensor_scalar(sc_in[:], deg_in[:], 1.0, None, ALU.max))))
            inverse_roots(c, "l3_root", [sc_out[:], sc_in[:]])
            rooms = y1[:].rearrange("p b f -> p (b f)")
            h, y = rooms[:, 0:BLOCKS * D].rearrange("p (b f) -> p b f", b=BLOCKS), y2
            vector_steps(lambda v, link: link(v.tensor_tensor(h[:], x[:], over_features(sc_out[:], D), ALU.mult)))
            with ExitStack() as c2:
                aggregate(c2, h[:], y[:], rooms[:, BLOCKS * D:])
            vector_steps(lambda v, link: link(v.tensor_tensor(y[:], y[:], over_features(sc_in[:], D), ALU.mult)))
            project([y[:]], D, [w[:]], h[:], D)
            vector_steps(lambda v, link: link(v.tensor_tensor(h[:], h[:], over_nodes(vb[:, 0, :], D), ALU.add)))
            batch_norm(h[:], D, vb[:, 1, :], vb[:, 2, :])
            vector_steps(lambda v, link: link(v.tensor_scalar(y[:], h[:], 0.0, None, ALU.min)))
            scalar_step(lambda: nc.scalar.activation(y[:], y[:], ACT.Exp))
            vector_steps(lambda v, link: (link(v.tensor_scalar(h[:], h[:], 0.0, -1.0, ALU.max, ALU.add)),
                                          link(v.tensor_tensor(h[:], h[:], y[:], ALU.add)),
                                          link(v.tensor_tensor(h[:], h[:], x[:], ALU.add))))
            layer_norm(h[:])
        store_all([(out.rearrange("(p b) f -> p (b f)", b=BLOCKS), x[:].rearrange("p b f -> p (b f)"))])


_OUTS = [((NODES, D), "float32")]


def kernel(**inputs):
    import concourse.bacc as _bacc
    from concourse.bass_utils import run_bass_kernel_spmd as _run

    nc = _bacc.Bacc("TRN2", target_bir_lowering=False, num_devices=1)
    arrays, aps = {}, {}
    for name, value in {**inputs, **constants()}.items():
        v = np.ascontiguousarray(value)
        arrays[f"in_{name}"] = v
        aps[name] = nc.dram_tensor(f"in_{name}", v.shape, mybir.dt.from_np(v.dtype), kind="ExternalInput").ap()
    out = nc.dram_tensor("out_0", (NODES, D), F32, kind="ExternalOutput").ap()
    gnn_stack(nc, aps, out)
    r = _run(nc, [arrays], core_ids=[0])
    return r.results[0]["out_0"]
```
